# Optimizing a Trainium2 kernel written in Bass

```python
import numpy as np
import jax
import jax.numpy as jnp

def _softmax(x, axis=-1):
    return jax.nn.softmax(x, axis=axis)

def _gelu(x):
    return jax.nn.gelu(x, approximate=True)

def _silu(x):
    return jax.nn.silu(x)

def _sigmoid(x):
    return jax.nn.sigmoid(x)

def _layernorm(x, axis=-1, eps=1e-05):
    m = jnp.mean(x, axis=axis, keepdims=True)
    v = jnp.var(x, axis=axis, keepdims=True)
    return (x - m) / jnp.sqrt(v + eps)

def _scatter_add(tgt, idx, src, axis=0):
    return tgt.at[idx].add(src)

def _segment_sum(src, seg, n):
    return jax.ops.segment_sum(src, seg, n)
kernel_name = 'mk_conv_attn_hybrid_d2_conv_nchw512_r2_15d6fb'

def setup_inputs(seed: int=0):
    np.random.seed(seed)
    _w = jnp.asarray

    def _rec_inputs():
        import jax
        import jax.numpy as jnp
        _gk = jax.random.key(seed)
        x = 7.22e-05 + 1 * jax.random.normal(jax.random.fold_in(_gk, 1), (4, 256, 32, 32), jnp.float32)
        return x
    x = _rec_inputs()

    def _L0_conv_setup():
        import jax, jax.numpy as jnp
        import numpy as np
        B, C, H, W = (4, 256, 32, 32)
        RED = 8
        MID = C // RED
        key = jax.random.key(seed)
        ks = jax.random.split(key, 7)
        s = 0.02
        return {'x': jax.random.normal(ks[0], (B, C, H, W), dtype=jnp.float32), 'Wq': jax.random.normal(ks[1], (MID, C), dtype=jnp.float32) * s, 'bq': jnp.zeros((MID,), dtype=jnp.float32), 'Wk': jax.random.normal(ks[2], (MID, C), dtype=jnp.float32) * s, 'bk': jnp.zeros((MID,), dtype=jnp.float32), 'Wv': jax.random.normal(ks[3], (C, C), dtype=jnp.float32) * s, 'bv': jnp.zeros((C,), dtype=jnp.float32), 'alpha': jnp.ones((1,), dtype=jnp.float32)}
    _L0_conv_all = _L0_conv_setup()
    _L0_conv_in = {k: v for k, v in _L0_conv_all.items() if k in ('Wq', 'bq', 'Wk', 'bk', 'Wv', 'bv', 'alpha')}
    del _L0_conv_all

    def _L1_attn_setup():
        import jax, jax.numpy as jnp
        import numpy as np
        key = jax.random.key(seed)
        k1, k2 = jax.random.split(key)
        x = jax.random.normal(k1, (4, 1024, 256), dtype=jnp.float32)
        proxy = jax.random.normal(k2, (16, 256), dtype=jnp.float32)
        return {'x': x, 'proxy': proxy}
    _L1_attn_all = _L1_attn_setup()
    _L1_attn_in = {k: v for k, v in _L1_attn_all.items() if k in ('proxy',)}
    del _L1_attn_all

    def _L1_ffn_setup():
        import jax, jax.numpy as jnp
        import numpy as np
        E = 8
        TOP_K = 2
        H = 256
        DFF = 1024
        B, S = (4, 1024)
        key = jax.random.key(seed)
        k0, k1, k2, k3 = jax.random.split(key, 4)
        return {'hidden_states': jax.random.normal(k0, (B, S, H), jnp.float32), 'gate_w': jax.random.normal(k1, (E, H), jnp.float32) * 0.01, 'w1': jax.random.normal(k2, (E, H, DFF), jnp.float32) * (1.0 / np.sqrt(H)), 'b1': jnp.zeros((E, DFF), jnp.float32), 'w2': jax.random.normal(k3, (E, DFF, H), jnp.float32) * (1.0 / np.sqrt(DFF)), 'b2': jnp.zeros((E, H), jnp.float32)}
    _L1_ffn_all = _L1_ffn_setup()
    _L1_ffn_in = {k: v for k, v in _L1_ffn_all.items() if k in ('gate_w', 'w1', 'b1', 'w2', 'b2')}
    del _L1_ffn_all
    return {'x': x, 'L0_conv_Wq': _L0_conv_in['Wq'], 'L0_conv_bq': _L0_conv_in['bq'], 'L0_conv_Wk': _L0_conv_in['Wk'], 'L0_conv_bk': _L0_conv_in['bk'], 'L0_conv_Wv': _L0_conv_in['Wv'], 'L0_conv_bv': _L0_conv_in['bv'], 'L0_conv_alpha': _L0_conv_in['alpha'], 'L1_attn_proxy': _L1_attn_in['proxy'], 'L1_ffn_gate_w': _L1_ffn_in['gate_w'], 'L1_ffn_w1': _L1_ffn_in['w1'], 'L1_ffn_b1': _L1_ffn_in['b1'], 'L1_ffn_w2': _L1_ffn_in['w2'], 'L1_ffn_b2': _L1_ffn_in['b2']}

def reference(x, L0_conv_Wq, L0_conv_bq, L0_conv_Wk, L0_conv_bk, L0_conv_Wv, L0_conv_bv, L0_conv_alpha, L1_attn_proxy, L1_ffn_gate_w, L1_ffn_w1, L1_ffn_b1, L1_ffn_w2, L1_ffn_b2):
    import jax
    import jax.numpy as jnp

    def _L0_conv_ref(x, Wq, bq, Wk, bk, Wv, bv, alpha):
        import jax, jax.numpy as jnp
        import numpy as np
        B, C, H, W = (4, 256, 32, 32)
        RED = 8
        MID = C // RED
        b, c, h, w = x.shape
        n = h * w
        xf = x.reshape(b, c, n)
        q = jnp.einsum('mc,bcn->bmn', Wq, xf) + bq[None, :, None]
        k = jnp.einsum('mc,bcn->bmn', Wk, xf) + bk[None, :, None]
        v = jnp.einsum('oc,bcn->bon', Wv, xf) + bv[None, :, None]
        energy = jnp.einsum('bmi,bmj->bij', q, k)
        wmat = jax.nn.softmax(energy, axis=-1)
        y = jnp.einsum('bcj,bij->bci', v, wmat)
        y = y.reshape(b, c, h, w)
        return alpha[0] * y + x

    def _L1_attn_ref(x, proxy):
        import jax, jax.numpy as jnp
        import numpy as np
        num_proxies = proxy.shape[0]
        prods = jnp.einsum('pd,bsd->bps', proxy, x)
        y = jnp.cumsum(prods[..., None] * x[:, None, :, :], axis=2)
        w = jax.nn.softmax(prods / jnp.sqrt(jnp.float32(num_proxies)), axis=1)
        out = jnp.einsum('bps,bpsd->bsd', w, y)
        return out

    def _L1_ffn_ref(hidden_states, gate_w, w1, b1, w2, b2):
        import jax, jax.numpy as jnp
        import numpy as np
        E = 8
        TOP_K = 2
        H = 256
        DFF = 1024
        B, S = (4, 1024)
        b, s, h = hidden_states.shape
        flat = hidden_states.reshape(-1, h)
        logits = flat @ gate_w.T
        top_vals, top_idx = jax.lax.top_k(logits, TOP_K)
        top_w = jax.nn.softmax(top_vals, axis=-1)
        combine = jnp.sum(jax.nn.one_hot(top_idx, E, dtype=flat.dtype) * top_w[..., None], axis=1)
        out = jnp.zeros_like(flat)
        for e in range(E):
            hdn = jax.nn.gelu(flat @ w1[e] + b1[e])
            out = out + combine[:, e:e + 1] * (hdn @ w2[e] + b2[e])
        return out.reshape(b, s, h)

    def _gn(v, G=32, eps=1e-05):
        B_, C_, H_, W_ = v.shape
        g = v.reshape(B_, G, C_ // G, H_, W_)
        m = jnp.mean(g, axis=(2, 3, 4), keepdims=True)
        s = jnp.var(g, axis=(2, 3, 4), keepdims=True)
        return ((g - m) / jnp.sqrt(s + eps)).reshape(v.shape)

    def _ln_c(v, eps=1e-06):
        m = jnp.mean(v, axis=1, keepdims=True)
        s = jnp.var(v, axis=1, keepdims=True)
        return (v - m) / jnp.sqrt(s + eps)

    def _ln_t(v, eps=1e-05):
        m = jnp.mean(v, axis=-1, keepdims=True)
        s = jnp.var(v, axis=-1, keepdims=True)
        return (v - m) / jnp.sqrt(s + eps)

    def _to_tokens(v):
        B_, C_, H_, W_ = v.shape
        return v.reshape(B_, C_, H_ * W_).transpose(0, 2, 1)

    def _from_tokens(t, like):
        B_, C_, H_, W_ = like.shape
        return t.transpose(0, 2, 1).reshape(B_, C_, H_, W_)
    x = _L0_conv_ref(x, L0_conv_Wq, L0_conv_bq, L0_conv_Wk, L0_conv_bk, L0_conv_Wv, L0_conv_bv, L0_conv_alpha)
    t = _to_tokens(x)
    t = t + _L1_attn_ref(_ln_t(t), L1_attn_proxy)
    t = t + _L1_ffn_ref(_ln_t(t), L1_ffn_gate_w, L1_ffn_w1, L1_ffn_b1, L1_ffn_w2, L1_ffn_b2)
    x = _from_tokens(t, x)
    return x

_drawn_inputs = setup_inputs


def setup_inputs(seed=0):
    import zlib

    import numpy as np

    out = dict(_drawn_inputs(seed))
    spreads = {'L0_conv_bq': (0.0, 0.8),
     'L0_conv_bk': (0.0, 0.8),
     'L0_conv_bv': (0.0, 0.1),
     'L1_ffn_b1': (0.0, 0.8),
     'L1_ffn_b2': (0.0, 0.8)}
    factors = {'L1_ffn_gate_w': 8.0, 'L1_ffn_w1': 8.0, 'L1_ffn_w2': 8.0}
    for name, (base, spread) in spreads.items():
        noise = np.random.default_rng([zlib.crc32(name.encode()), seed]).standard_normal(out[name].shape)
        drawn = base * np.exp(spread * noise) if base else spread * noise
        out[name] = jnp.asarray(drawn.astype(out[name].dtype))
    for name, factor in factors.items():
        out[name] = (out[name] * factor).astype(out[name].dtype)
    return out
```

```python
from contextlib import ExitStack

import concourse.bass as bass
from concourse import mybir
from concourse.alu_op_type import AluOpType as ALU

F32 = mybir.dt.float32
F32R = mybir.dt.float32r
BF16 = mybir.dt.bfloat16
I32 = mybir.dt.int32
U32 = mybir.dt.uint32
ACT = mybir.ActivationFunctionType
AX = mybir.AxisListType

P = 128
B, C, N = 4, 256, 1024
KT = C // P
IT = N // P
NT = B * IT
TOK = B * N
MID = 32
HALF = 512
NP = 16
E, F = 8, 1024
FT = F // P
CAP = TOK
TILES = 2 * TOK // P + E - 1
SLOTS = -(-(E * CAP + E * P) // (P * P)) * P * P
WROW = 2 * KT * F + 2 * FT * C
W2AT = 2 * KT * F
LN_EPS = 1e-5
CREDIT = 2


def done(i):
    return i + (CREDIT + 1)


def wait_apart(eng, sem, value):
    eng.wait_ge(sem, value)
    eng.nop(nofuse=True)


def mm3(eng, out, lhs, rhs, cols, first=True, last=True):
    (lh, ll), (rh, rl) = lhs, rhs
    eng.matmul(out, ll, rh, start=first, stop=False)
    eng.matmul(out, lh, rl, start=False, stop=False)
    return eng.matmul(out, lh, rh, start=False, stop=last)


def build(nc, x_ch, x_tok, wqk3, bqk3, wv_t, bv, alpha, proxy_t, gate_t, w1, b1_t, w2, b2, out):
    wsplit = nc.dram_tensor("wsplit", [E, P, WROW], F32, kind="Internal").ap()
    normed = nc.dram_tensor("normed", [TOK + P, C], F32, kind="Internal").ap()
    places = nc.dram_tensor("places", [SLOTS, 2], I32, kind="Internal").ap()
    with ExitStack() as outer:
        def sem(name):
            return outer.enter_context(nc.semaphore(name))

        def keep(name, shape, dt=F32):
            return outer.enter_context(nc.sbuf_tensor(name, shape, dt))

        tok = keep("tok", [P, NT, C])
        wbuf = keep("wbuf", [P, 2, WROW], F32R)
        ident = keep("ident", [P, P])
        stage_a(nc, sem, tok, wbuf, ident, wsplit, x_ch, x_tok, wqk3, bqk3, wv_t, bv, alpha, w1, w2)
        counts_m = keep("counts_m", [P, E], BF16)
        stage_b(nc, sem, tok, ident, counts_m, normed, places, proxy_t, gate_t, out)
        tabs = keep("tabs", [P, 5, TILES], I32)
        stage_c(nc, sem, counts_m, tabs)
        stage_d(nc, sem, wbuf, ident, tabs, wsplit, normed, places, b1_t, b2, out)


def stage_a(nc, sem, tok, wbuf, ident, wsplit, x_ch, x_tok, wqk3, bqk3, wv_t, bv, alpha, w1, w2):
    with ExitStack() as ctx:
        def sb(name, shape, dt=F32):
            return ctx.enter_context(nc.sbuf_tensor(name, shape, dt))

        xraw = sb("xraw", [P, KT, N])
        xh, xl = sb("xh", [P, KT, N], F32R), sb("xl", [P, KT, N], F32R)
        wq_raw = sb("wq_raw", [P, 2, KT, 3 * MID])
        wqh, wql = sb("wqh", [P, 2, KT, 3 * MID], F32R), sb("wql", [P, 2, KT, 3 * MID], F32R)
        bqk = sb("bqk", [3 * MID, 2])
        wv_raw = sb("wv_raw", [P, KT, C])
        wvh, wvl = sb("wvh", [P, KT, C], F32R), sb("wvl", [P, KT, C], F32R)
        bvb = sb("bvb", [P, 1, C])
        alb = sb("alb", [P, 1])
        qk3 = sb("qk3", [3 * MID, 2, N], F32R)
        vf = sb("vf", [P, 2, HALF])
        vh, vl = sb("vh", [P, IT, C], F32R), sb("vl", [P, IT, C], F32R)
        prob = sb("prob", [P, 2, N])
        qkf = prob[0:3 * MID]
        pth, ptl = sb("pth", [P, 2, IT, P], F32R), sb("ptl", [P, 2, IT, P], F32R)
        negmax, rowsum, scale = sb("negmax", [P, 4]), sb("rowsum", [P, 4]), sb("scale", [P, 4])
        wraw = sb("wraw", [P, 2, WROW // 4])

        ps_sc = ctx.enter_context(nc.psum_tensor("ps_sc", [P, N], F32))
        ps_pt = [ctx.enter_context(nc.psum_tensor(f"ps_pt{i}", [P, N], F32)) for i in range(2)]
        ps_o = [ctx.enter_context(nc.psum_tensor(f"ps_o{i}", [P, HALF], F32)) for i in range(2)]

        consts, x_in, tok_in = sem("a_consts"), sem("a_x_in"), sem("a_tok_in")
        ident0, ident_ok, wsm_hi, wsm_ok = sem("a_ident0"), sem("a_ident"), sem("a_wsm_hi"), sem("a_wsm")
        x_hi, x_split = sem("a_x_hi"), sem("a_x_split")
        qk_mm, qk_full, qk_hi, qk_ok = sem("a_qk_mm"), sem("a_qk_full"), sem("a_qk_hi"), sem("a_qk_ok")
        v_mm, v_full, v_hi, v_ok = sem("a_v_mm"), sem("a_v_full"), sem("a_v_hi"), sem("a_v_ok")
        scored, maxed, exped = sem("a_scored"), sem("a_maxed"), sem("a_exped")
        turned, pt_hi, pt_ok = sem("a_turned"), sem("a_pt_hi"), sem("a_pt_ok")
        recip, scaled = sem("a_recip"), sem("a_scaled")
        summed, added = sem("a_summed"), sem("a_added")
        w_in, w_hi, w_lo = [sem("a_w1_in"), sem("a_w2_in")], sem("a_w_hi"), sem("a_w_lo")
        w_out = [[sem(f"a_w{part + 1}_out{par}") for part in range(2)] for par in range(2)]
        block = ctx.enter_context(nc.Block())

        @block.sync
        def _(sp):
            for kind in range(2):
                sp.dma_start(wq_raw[:, kind], wqk3[kind].rearrange("(k p) m -> p k m", p=P)).then_inc(consts, 16)
            sp.dma_start(bqk[:, :], bqk3).then_inc(consts, 16)
            sp.dma_start(wv_raw[:, :, :], wv_t.rearrange("(k p) m -> p k m", p=P)).then_inc(consts, 16)
            sp.dma_start(bvb[:, 0, :], bv.partition_broadcast(P)).then_inc(consts, 16)
            sp.dma_start(alb[:, :], alpha.partition_broadcast(P)).then_inc(consts, 16)
            sp.dma_start(tok[:, :, :], x_tok.rearrange("(g p) c -> p g c", p=P)).then_inc(tok_in, 16)

            def load(e, part):
                src = (w1, w2)[part][bass.ds(e, 1)].rearrange("a (k p) f -> p (a k) f", p=P)
                dst = wraw[:, part].rearrange("p (k f) -> p k f", k=(KT, FT)[part])
                sp.dma_start(dst, src).then_inc(w_in[part], 16)

            def store(e, par, part):
                sp.wait_ge(w_lo, done(e * 2 + part))
                at = slice(part * W2AT, (part + 1) * W2AT)
                sp.dma_start(wsplit[bass.ds(e, 1)].rearrange("a p w -> (a p) w")[:, at],
                             wbuf[:, par, at].bitcast(F32)).then_inc(w_out[par][part], 16)

            load(0, 0)
            load(0, 1)
            with sp.Fori(0, E // 2 - 1) as h:
                for par in range(2):
                    for part in range(2):
                        store(h * 2 + par, par, part)
                        load(h * 2 + (par + 1), part)
            for par in range(2):
                for part in range(2):
                    store(E - 2 + par, par, part)
                    if par == 0:
                        load(E - 1, part)
            for s in w_out[0] + w_out[1]:
                sp.wait_ge(s, 16 * (E // 2 + 1))

        @block.gpsimd
        def _(pool):
            pool.sem_inc(w_lo, CREDIT)
            for s in w_out[0] + w_out[1]:
                pool.sem_inc(s, 16)
            pool.memset(ident[:, :], 0.0).then_inc(ident0, 1)
            pool.wait_ge(ident0, 1)
            pool.affine_select(out=ident[:, :], in_=ident[:, :], compare_op=ALU.not_equal, fill=1.0,
                               base=0, pattern=[[-1, P]], channel_multiplier=1).then_inc(ident_ok, 1)

            with pool.Fori(0, E // 2) as h:
                for par in range(2):
                    for part in range(2):
                        pool.wait_ge(w_hi, (h * 4 + (par * 2 + part + 1)) * 2)
                        at, n = part * W2AT, W2AT // 2
                        pool.tensor_tensor(wbuf[:, par, at + n:at + 2 * n], wraw[:, part],
                                           wbuf[:, par, at:at + n].bitcast(F32), ALU.subtract).then_inc(w_lo, 1)

        @block.scalar
        def _(act):
            for s in (exped, pt_hi, qk_full, v_hi):
                act.sem_inc(s, CREDIT)
            act.dma_start(xraw[:, :, :], x_ch[0].rearrange("(k p) n -> p k n", p=P)).then_inc(x_in, 16)
            with act.Fori(0, B) as b:
                act.wait_ge(x_in, (b + 1) * 16)
                act.wait_ge(v_mm, done(b * 4 - 1))
                act.activation(xh[:, :, :], xraw[:, :, :], ACT.Copy).then_inc(x_hi, 1)
                act.wait_ge(x_split, b + 1)
                nxt = (b + 1) % B
                act.dma_start(xraw[:, :, :], x_ch[bass.ds(nxt, 1)].rearrange("a (k p) n -> p (a k) n", p=P)).then_inc(x_in, 16)
                for kind, src in enumerate((ps_sc, ps_pt[0])):
                    act.wait_ge(qk_mm, done(b * 2 + kind))
                    if kind == 0:
                        act.wait_ge(consts, 96)
                        act.wait_ge(turned, done(b * IT - 1))
                    act.activation(qkf[:, kind], src[0:3 * MID, :], ACT.Identity,
                                   bias=bqk[:, kind:kind + 1]).then_inc(qk_full, 1)
                for ch in range(4):
                    act.wait_ge(v_full, done(b * 4 + ch))
                    if ch == 0:
                        act.wait_ge(summed, done(b * IT - 1))
                    act.activation(vh[:, 2 * ch:2 * ch + 2, :], vf[:, ch % 2], ACT.Copy).then_inc(v_hi, 1)

                def exp_tile(it):
                    act.wait_ge(maxed, done(b * IT + it))
                    act.wait_ge(turned, done(b * IT + it - 2))
                    col = slice(it % 4, it % 4 + 1)
                    act.activation(prob[:, it % 2], ps_sc[:, :], ACT.Exp, bias=negmax[:, col],
                                   accum_out=rowsum[:, col]).then_inc(exped, 1)

                def hi_tile(it):
                    act.wait_ge(turned, done(b * IT + it))
                    act.wait_ge(summed, done(b * IT + it - 2))
                    act.activation(pth[:, it % 2], ps_pt[it % 2].rearrange("p (j i) -> p j i", j=IT),
                                   ACT.Copy).then_inc(pt_hi, 1)

                def weights_high(it):
                    par, part, half = it // 4, it // 2 % 2, it % 2
                    if half == 0:
                        act.wait_ge(w_in[part], (b * 2 + (par + 1)) * 16)
                        act.wait_ge(w_out[par][part], (b + 1) * 16)
                    at, n = part * W2AT, W2AT // 4
                    act.activation(wbuf[:, par, at + half * n:at + (half + 1) * n], wraw[:, part, half * n:(half + 1) * n],
                                   ACT.Copy).then_inc(w_hi, 1)

                exp_tile(0)
                exp_tile(1)
                hi_tile(0)
                for it in range(IT):
                    weights_high(it)
                    if it + 1 < IT:
                        hi_tile(it + 1)
                    if it + 2 < IT:
                        exp_tile(it + 2)
            act.wait_ge(x_in, 16 * (B + 1))

        @block.vector
        def _(dve):
            for s in (qk_ok, v_full, v_ok, maxed, pt_ok, scaled, recip, added, qk_hi):
                dve.sem_inc(s, CREDIT)
            dve.wait_ge(consts, 96)
            dve.tensor_copy(wqh[:, :, :, :], wq_raw[:, :, :, :]).then_inc(wsm_hi, 1)
            dve.tensor_copy(wvh[:, :, :], wv_raw[:, :, :]).then_inc(wsm_hi, 1)
            dve.wait_ge(wsm_hi, 2)
            dve.tensor_tensor(wql[:, :, :, :], wq_raw[:, :, :, :], wqh[:, :, :, :].bitcast(F32), ALU.subtract).then_inc(wsm_ok, 1)
            dve.tensor_tensor(wvl[:, :, :], wv_raw[:, :, :], wvh[:, :, :].bitcast(F32), ALU.subtract).then_inc(wsm_ok, 1)
            with dve.Fori(0, B) as b:
                dve.wait_ge(x_hi, b + 1)
                dve.tensor_tensor(xl[:, :, :], xraw[:, :, :], xh[:, :, :].bitcast(F32), ALU.subtract).then_inc(x_split, 1)
                for kind in range(2):
                    dve.wait_ge(qk_full, done(b * 2 + kind))
                    if kind == 0:
                        dve.wait_ge(scored, done(b * IT - 1))
                    dve.tensor_copy(qk3[:, kind], qkf[:, kind]).then_inc(qk_hi, 1)
                    dve.wait_ge(qk_hi, done(b * 2 + kind))
                    at = slice(MID, 2 * MID) if kind == 0 else slice(2 * MID, 3 * MID)
                    dve.tensor_tensor(qk3[at, kind], qkf[at, kind], qk3[at, kind].bitcast(F32), ALU.subtract).then_inc(qk_ok, 1)

                def v_low(ch):
                    dve.wait_ge(v_hi, done(b * 4 + ch))
                    dve.tensor_tensor(vl[:, 2 * ch:2 * ch + 2, :], vf[:, ch % 2].rearrange("p (j c) -> p j c", j=2),
                                      vh[:, 2 * ch:2 * ch + 2, :].bitcast(F32), ALU.subtract).then_inc(v_ok, 1)

                for ch in range(4):
                    dve.wait_ge(v_mm, done(b * 4 + ch))
                    if ch >= 2:
                        dve.wait_ge(v_ok, done(b * 4 + ch - 2))
                    src = ps_pt[1][:, ch * HALF:(ch + 1) * HALF] if ch < 2 else ps_o[ch - 2][:, :]
                    dve.tensor_tensor(vf[:, ch % 2].rearrange("p (j c) -> p j c", j=2), src.rearrange("p (j c) -> p j c", j=2),
                                      bvb[:, :, :].to_broadcast([P, 2, C]), ALU.add).then_inc(v_full, 1)
                    if ch >= 1:
                        v_low(ch - 1)
                v_low(3)

                def max_tile(it):
                    dve.wait_ge(scored, done(b * IT + it))
                    dve.tensor_reduce(negmax[:, it % 4:it % 4 + 1], ps_sc[:, :], AX.X, ALU.max, negate=True).then_inc(maxed, 1)

                def low_tile(it):
                    h = it % 2
                    dve.wait_ge(pt_hi, done(b * IT + it))
                    dve.tensor_tensor(ptl[:, h], ps_pt[h].rearrange("p (j i) -> p j i", j=IT), pth[:, h].bitcast(F32),
                                      ALU.subtract).then_inc(pt_ok, 1)

                max_tile(0)
                max_tile(1)
                low_tile(0)
                for it in range(IT):
                    g, h = b * IT + it, it % 2
                    col = slice(it % 4, it % 4 + 1)
                    if it + 2 < IT:
                        max_tile(it + 2)
                    dve.wait_ge(exped, done(g))
                    dve.reciprocal(scale[:, col], rowsum[:, col]).then_inc(recip, 1)
                    if it + 1 < IT:
                        low_tile(it + 1)
                    dve.wait_ge(recip, done(g))
                    dve.tensor_tensor(scale[:, col], scale[:, col], alb[:, :], ALU.mult).then_inc(scaled, 1)
                    dve.wait_ge(scaled, done(g))
                    if it == 0:
                        dve.wait_ge(tok_in, 16)
                    dve.wait_ge(summed, done(g))
                    mine = tok[:, bass.ds(g, 1), :].rearrange("p a c -> p (a c)")
                    dve.scalar_tensor_tensor(out=mine, in0=ps_o[h][:, 0:C], scalar=scale[:, col], in1=mine,
                                             op0=ALU.mult, op1=ALU.add).then_inc(added, 1)

        @block.tensor
        def _(pe):
            for s in (qk_mm, v_mm, scored, turned, summed):
                pe.sem_inc(s, CREDIT)
            pe.wait_ge(wsm_ok, 2)
            pe.wait_ge(ident_ok, 1)
            with pe.Fori(0, B) as b:
                pe.wait_ge(x_split, b + 1)
                pe.wait_ge(exped, done(b * IT - 1))
                pe.wait_ge(pt_ok, done(b * IT - 1))
                for kind, dst in enumerate((ps_sc, ps_pt[0])):
                    for n in range(N // HALF):
                        cols = slice(n * HALF, (n + 1) * HALF)
                        for k in range(KT):
                            last = mm3(pe, dst[0:3 * MID, cols], (wqh[:, kind, k], wql[:, kind, k]),
                                       (xh[:, k, cols], xl[:, k, cols]), HALF, k == 0, k == KT - 1)
                    last.then_inc(qk_mm, 1)
                pe.wait_ge(added, done(b * IT - 1))
                for ch in range(4):
                    dst = ps_pt[1][:, ch * HALF:(ch + 1) * HALF] if ch < 2 else ps_o[ch - 2][:, :]
                    for j in range(2):
                        rows = slice((2 * ch + j) * P, (2 * ch + j + 1) * P)
                        for k in range(KT):
                            last = mm3(pe, dst[:, j * C:(j + 1) * C], (xh[:, k, rows], xl[:, k, rows]),
                                       (wvh[:, k], wvl[:, k]), C, k == 0, k == KT - 1)
                    last.then_inc(v_mm, 1)

                def score(it):
                    if it == 0:
                        pe.wait_ge(qk_full, done(b * 2))
                        pe.wait_ge(qk_ok, done(b * 2 + 1))
                    pe.wait_ge(exped, done(b * IT + it - 1))
                    for n in range(N // HALF):
                        cols = slice(n * HALF, (n + 1) * HALF)
                        last = pe.matmul(ps_sc[:, cols], qk3[:, 0, it * P:(it + 1) * P], qk3[:, 1, cols],
                                         start=True, stop=True)
                    last.then_inc(scored, 1)

                def turn(it):
                    pe.wait_ge(exped, done(b * IT + it))
                    pe.wait_ge(pt_ok, done(b * IT + it - 2))
                    if it == 1:
                        pe.wait_ge(v_full, done(b * 4 + 1))
                    for j in range(IT):
                        last = pe.transpose(ps_pt[it % 2][:, j * P:(j + 1) * P], prob[:, it % 2, j * P:(j + 1) * P], ident[:, :])
                    last.then_inc(turned, 1)

                def weigh(it):
                    pe.wait_ge(pt_ok, done(b * IT + it))
                    pe.wait_ge(added, done(b * IT + it - 2))
                    if it == 0:
                        pe.wait_ge(v_ok, done(b * 4 + 3))
                    for j in range(IT):
                        last = mm3(pe, ps_o[it % 2][:, 0:C], (pth[:, it % 2, j], ptl[:, it % 2, j]),
                                   (vh[:, j], vl[:, j]), C, j == 0, j == IT - 1)
                    last.then_inc(summed, 1)

                score(0)
                score(1)
                turn(0)
                for it in range(IT):
                    if it + 2 < IT:
                        score(it + 2)
                    if it + 1 < IT:
                        turn(it + 1)
                    weigh(it)


def stage_b(nc, sem, tok, ident, counts_m, normed, places, proxy_t, gate_t, out):
    with ExitStack() as ctx:
        def sb(name, shape, dt=F32):
            return ctx.enter_context(nc.sbuf_tensor(name, shape, dt))

        def ps(name, shape):
            return ctx.enter_context(nc.psum_tensor(name, shape, F32))

        proxy, gate = sb("proxy", [P, KT, NP]), sb("gate", [P, KT, E])
        causal = sb("causal", [P, P])
        before = sb("before", [P, P], BF16)
        ones = sb("ones", [P, P], BF16)
        minus_half, eps = sb("minus_half", [P, B]), sb("eps", [P, B])
        expert_id = sb("expert_id", [P, E])
        place0 = sb("place0", [P, E])
        token_id = sb("token_id", [P, B])
        no_token = sb("no_token", [P, SLOTS // P, 2], I32)
        xn = sb("xn", [P, 2, B, C])
        xt1 = sb("xt1", [P, B, KT, P])
        prod = sb("prod", [P, 2, B, NP])
        prod_rel, prod_w = sb("prod_rel", [P, B, NP]), sb("prod_w", [P, B, NP])
        prod_max, prod_sum = sb("prod_max", [P, B]), sb("prod_sum", [P, B])
        turned_pw = sb("turned_pw", [NP, 2, 2 * B, P])
        attn = sb("attn", [P, B, P])
        state = sb("state", [NP, B, C])
        stat1, mv1, rs1 = sb("stat1", [P, B, 6]), sb("mv1", [P, B, 2]), sb("rs1", [P, B])
        stat2, mv2, rs2 = sb("stat2", [P, B, 6]), sb("mv2", [P, B, 2]), sb("rs2", [P, B])
        x2 = sb("x2", [P, B, C])
        xt2 = sb("xt2", [P, B, KT, P])
        logit = sb("logit", [P, B, E])
        top, top_id = sb("top", [P, B, 8]), sb("top_id", [P, B, 8], U32)
        top_f = sb("top_f", [P, B, 2])
        hot = sb("hot", [P, 2, B, E])
        chose = sb("chose", [P, B, E], BF16)
        earlier = sb("earlier", [P, B, E], BF16)
        rank = sb("rank", [P, B, E])
        hot_rank = sb("hot_rank", [P, 2, B, E])
        place_f = sb("place_f", [P, 2, B])
        place = sb("place", [P, 2, B], I32)
        gap, gap_exp, gap_den = sb("gap", [P, B]), sb("gap_exp", [P, B]), sb("gap_den", [P, B])
        record = sb("record", [P, 2, B, 2], I32)

        ps_xt = ps("ps_xt", [P, B * KT * P])
        ps_small = ps("ps_small", [P, HALF])
        ps_pw = ps("ps_pw", [P, 2 * B * P])
        ps_a = ps("ps_a", [P, B * P])
        ps_out = ps("ps_out", [P, B * C])
        ps_prod = ps_small[:, 0:B * NP].rearrange("p (b n) -> p b n", b=B)
        ps_logit = ps_small[:, 64:64 + B * E].rearrange("p (b n) -> p b n", b=B)
        ps_rank = ps_small[:, 128:128 + B * E]

        def sems(names):
            return [sem("b_" + n) for n in names.split()]

        consts, set0, setup, vset = sems("consts set0 setup vset")
        stat1_d, mv1_d, xn_d, prod_d, pmax_d, prel_d, psum_d, prec_d, pw_d = sems(
            "stat1 mv1 xn prod prod_max prod_rel prod_sum prod_recip prod_w")
        attn_d, tok_d, state_d, stat2_d, mv2_d, x2_d, logit_d, top_d, topid_d = sems(
            "attn tok state stat2 mv2 x2 logit top top_id")
        topf_d, hot_d, chose_d, early_d, rank_d, hotrank_d, placef_d, place_d = sems(
            "top_f hot chose earlier rank hot_rank place_f place")
        gap_d, den_d, share_d, record_d, tokid_d = sems("gap gap_den share record token_id")
        xt1_d, pexp_d, pw_turned_d, xt2_d, gexp_d = sems("xt1 prod_exp turned_pw xt2 gap_exp")
        var1_d, rs1_d, var2_d, rs2_d = sems("var1 rs1 var2 rs2")
        t1_mm, prod_mm, pw_mm, a_mm, state_mm, out_mm, t2_mm, logit_mm, rank_mm = sems(
            "t1_mm prod_mm pw_mm a_mm state_mm out_mm t2_mm logit_mm rank_mm")
        tok_out, x2_out, record_out = sems("tok_out x2_out record_out")
        CH = IT

        def chunks(eng, body):
            with eng.Fori(0, CH // 2 - 1) as k:
                for par in range(2):
                    body(k * 2 + par, par, True)
            body(CH - 2, 0, True)
            body(CH - 1, 1, False)

        def tiles(c):
            return tok[:, :, :].rearrange("p (b c) d -> p b c d", b=B)[:, :, bass.ds(c, 1), :].rearrange("p b a d -> p b (a d)")

        block = ctx.enter_context(nc.Block())
        out_v = out[0:TOK, :].rearrange("(b c p) d -> c p b d", b=B, p=P)
        normed_v = normed[0:TOK, :].rearrange("(b c p) d -> c p b d", b=B, p=P)

        @block.sync
        def _(sp):
            sp.dma_start(proxy[:, :, :], proxy_t.rearrange("(k p) n -> p k n", p=P)).then_inc(consts, 16)
            sp.dma_start(gate[:, :, :], gate_t.rearrange("(k p) n -> p k n", p=P)).then_inc(consts, 16)
            sp.wait_ge(vset, 3)
            sp.dma_start(normed[TOK:TOK + P, :], x2[:, 0, :]).then_inc(x2_out, 16)

            def body(c, par, more):
                sp.wait_ge(tok_d, done(c))
                sp.dma_start(out_v[bass.ds(c, 1)].rearrange("a p b d -> p (a b) d"),
                             tiles(c)).then_inc(tok_out, 16)
                sp.wait_ge(x2_d, done(c))
                sp.dma_start(normed_v[bass.ds(c, 1)].rearrange("a p b d -> p (a b) d"), x2[:, :, :]).then_inc(x2_out, 16)

            chunks(sp, body)
            sp.wait_ge(tok_out, 16 * CH)
            sp.wait_ge(x2_out, 16 * (CH + 1))

        @block.gpsimd
        def _(pool):
            for s in (var1_d, rs1_d, var2_d, rs2_d):
                pool.sem_inc(s, CREDIT)
            pool.memset(causal[:, :], 1.0).then_inc(set0, 1)
            pool.memset(before[:, :], 1.0).then_inc(set0, 1)
            pool.memset(ones[:, :], 1.0).then_inc(setup, 1)
            pool.memset(minus_half[:, :], -0.5).then_inc(setup, 1)
            pool.memset(eps[:, :], LN_EPS).then_inc(setup, 1)
            pool.iota(expert_id[:, :], pattern=[[1, E]], base=0, channel_multiplier=0,
                      allow_small_or_imprecise_dtypes=True).then_inc(setup, 1)
            pool.iota(place0[:, :], pattern=[[CAP, E]], base=0, channel_multiplier=0,
                      allow_small_or_imprecise_dtypes=True).then_inc(setup, 1)
            pool.iota(token_id[:, :], pattern=[[N, B]], base=0, channel_multiplier=1,
                      allow_small_or_imprecise_dtypes=True).then_inc(setup, 1)
            pool.iota(no_token[:, :, 0], pattern=[[0, SLOTS // P // P], [1, P]], base=TOK,
                      channel_multiplier=0).then_inc(setup, 1)
            pool.memset(no_token[:, :, 1], 0).then_inc(setup, 1)
            pool.wait_ge(set0, 2)
            pool.affine_select(out=causal[:, :], in_=causal[:, :], compare_op=ALU.is_ge, fill=0.0, base=0,
                               pattern=[[1, P]], channel_multiplier=-1).then_inc(setup, 1)
            pool.affine_select(out=before[:, :], in_=before[:, :], compare_op=ALU.is_gt, fill=0.0, base=0,
                               pattern=[[1, P]], channel_multiplier=-1).then_inc(setup, 1)

            def inv_std(mv_d, mv, var_d, rs_d, rs, c):
                pool.wait_ge(mv_d, done(c))
                pool.tensor_tensor(rs[:, :], mv[:, :, 1], eps[:, :], ALU.add).then_inc(var_d, 1)
                pool.wait_ge(var_d, done(c))
                pool.tensor_tensor(rs[:, :], rs[:, :], minus_half[:, :], ALU.pow).then_inc(rs_d, 1)

            def body(c, par, more):
                if more:
                    inv_std(mv1_d, mv1, var1_d, rs1_d, rs1, c + 1)
                inv_std(mv2_d, mv2, var2_d, rs2_d, rs2, c)
                wait_apart(pool, record_d, done(c))
                for b in range(B):
                    for k in range(2):
                        pool.indirect_dma_start(
                            out=places, out_offset=bass.IndirectOffsetOnAxis(ap=place[:, k, b:b + 1], axis=0),
                            in_=record[:, k, b, :], in_offset=None).then_inc(record_out, 16)

            pool.wait_ge(setup, 10)
            inv_std(mv1_d, mv1, var1_d, rs1_d, rs1, 0)
            pool.dma_start(places.rearrange("(p g) r -> p (g r)", p=P),
                           no_token[:, :, :].rearrange("p g r -> p (g r)")).then_inc(record_out, 16)
            pool.wait_ge(record_out, 16)
            chunks(pool, body)
            pool.wait_ge(record_out, 16 * (2 * B * CH + 1))

        @block.scalar
        def _(act):
            for s in (xt1_d, pexp_d, pw_turned_d, xt2_d, gexp_d):
                act.sem_inc(s, CREDIT)

            def first(c, par):
                act.wait_ge(t1_mm, done(c))
                act.wait_ge(prod_mm, done(c - 1))
                act.activation(xt1[:, :, :, :], ps_xt[:, :].rearrange("p (b k t) -> p b k t", b=B, k=KT),
                               ACT.Copy).then_inc(xt1_d, 1)
                act.wait_ge(prel_d, done(c))
                act.activation(prod_rel[:, :, :], prod_rel[:, :, :], ACT.Exp, scale=float(NP) ** -0.5).then_inc(pexp_d, 1)
                act.wait_ge(pw_mm, done(c))
                act.wait_ge(out_mm, done(c - 2))
                act.activation(turned_pw[:, par], ps_pw[0:NP, :].rearrange("p (b t) -> p b t", b=2 * B),
                               ACT.Copy).then_inc(pw_turned_d, 1)

            def body(c, par, more):
                if more:
                    first(c + 1, 1 - par)
                act.wait_ge(t2_mm, done(c))
                act.wait_ge(logit_mm, done(c - 1))
                act.activation(xt2[:, :, :, :], ps_xt[:, :].rearrange("p (b k t) -> p b k t", b=B, k=KT),
                               ACT.Copy).then_inc(xt2_d, 1)
                act.wait_ge(gap_d, done(c))
                act.activation(gap_exp[:, :], gap[:, :], ACT.Exp).then_inc(gexp_d, 1)

            first(0, 0)
            chunks(act, body)

        @block.vector
        def _(dve):
            for s in (stat1_d, mv1_d, xn_d, prod_d, pmax_d, prel_d, psum_d, prec_d, pw_d, attn_d, tok_d, state_d,
                      stat2_d, mv2_d, x2_d, logit_d, top_d, topid_d, topf_d, hot_d, chose_d, early_d, rank_d,
                      hotrank_d, placef_d, place_d, gap_d, den_d, share_d, record_d, tokid_d):
                dve.sem_inc(s, CREDIT)
            dve.memset(state[:, :, :], 0.0).then_inc(vset, 1)
            dve.memset(x2[:, 0, :], 0.0).then_inc(vset, 1)
            dve.memset(counts_m[:, :], 0.0).then_inc(vset, 1)
            dve.wait_ge(setup, 10)

            def tiles_of(c):
                return [tiles(c)[:, b, :] for b in range(B)]

            def stats(c, stat, stat_d, mv, mv_d, rs_d):
                wait_apart(dve, rs_d, done(c - 1))
                for b, t in enumerate(tiles_of(c)):
                    last = dve.bn_stats(stat[:, b, :], t)
                last.then_inc(stat_d, 1)
                wait_apart(dve, stat_d, done(c))
                for b in range(B):
                    last = dve.bn_aggr(mv[:, b, :], stat[:, b, :])
                last.then_inc(mv_d, 1)

            def normalise(c, dst, mv, rs, rs_d, ready):
                dve.wait_ge(rs_d, done(c))
                for b, t in enumerate(tiles_of(c)):
                    last = dve.tensor_scalar(dst[:, b, :], t, mv[:, b, 0:1], rs[:, b:b + 1], ALU.subtract, ALU.mult)
                last.then_inc(ready, 1)

            def first_norm(c, par):
                stats(c, stat1, stat1_d, mv1, mv1_d, rs1_d)
                dve.wait_ge(state_mm, done(c - 2))
                normalise(c, xn[:, par], mv1, rs1, rs1_d, xn_d)

            def wide(small):
                return small.unsqueeze(2).to_broadcast([P, B, NP])

            def proxy_softmax_in(c, par):
                dve.wait_ge(prod_mm, done(c))
                dve.wait_ge(state_mm, done(c - 2))
                dve.tensor_copy(prod[:, par], ps_prod).then_inc(prod_d, 1)
                dve.tensor_reduce(prod_max[:, :], ps_prod, AX.X, ALU.max).then_inc(pmax_d, 1)
                dve.wait_ge(prod_d, done(c))
                dve.wait_ge(pmax_d, done(c))
                dve.tensor_tensor(prod_rel[:, :, :], prod[:, par], wide(prod_max[:, :]), ALU.subtract).then_inc(prel_d, 1)

            def proxy_softmax_out(c):
                dve.wait_ge(pexp_d, done(c))
                dve.tensor_reduce(prod_sum[:, :], prod_rel[:, :, :], AX.X, ALU.add).then_inc(psum_d, 1)
                dve.wait_ge(psum_d, done(c))
                dve.reciprocal(prod_sum[:, :], prod_sum[:, :]).then_inc(prec_d, 1)
                dve.wait_ge(prec_d, done(c))
                dve.wait_ge(pw_mm, done(c - 1))
                dve.tensor_tensor(prod_w[:, :, :], prod_rel[:, :, :], wide(prod_sum[:, :]), ALU.mult).then_inc(pw_d, 1)

            def mask(c):
                dve.wait_ge(a_mm, done(c))
                dve.tensor_tensor(attn[:, :, :], ps_a[:, :].rearrange("p (b t) -> p b t", b=B),
                                  causal[:, :].unsqueeze(1).to_broadcast([P, B, P]), ALU.mult).then_inc(attn_d, 1)

            def add_out(c):
                dve.wait_ge(out_mm, done(c))
                dve.tensor_tensor(tiles(c), ps_out[:, :].rearrange("p (b d) -> p b d", b=B), tiles(c),
                                  ALU.add).then_inc(tok_d, 1)
                dve.wait_ge(state_mm, done(c))
                dve.tensor_tensor(state[:, :, :], ps_pw[0:NP, :].rearrange("p (b d) -> p b d", b=B), state[:, :, :],
                                  ALU.add).then_inc(state_d, 1)

            def choose(c):
                dve.wait_ge(logit_mm, done(c))
                dve.tensor_copy(logit[:, :, :], ps_logit).then_inc(logit_d, 1)
                wait_apart(dve, logit_d, done(c))
                for b in range(B):
                    last = dve.max(top[:, b, :], logit[:, b, :])
                last.then_inc(top_d, 1)
                dve.wait_ge(top_d, done(c))
                dve.tensor_tensor(gap[:, :], top[:, :, 1], top[:, :, 0], ALU.subtract).then_inc(gap_d, 1)
                for b in range(B):
                    last = dve.max_index(top_id[:, b, :], top[:, b, :], logit[:, b, :])
                last.then_inc(topid_d, 1)
                dve.wait_ge(topid_d, done(c))
                dve.tensor_copy(top_f[:, :, :], top_id[:, :, 0:2]).then_inc(topf_d, 1)
                dve.wait_ge(topf_d, done(c))
                for k in range(2):
                    last = dve.tensor_tensor(hot[:, k], expert_id[:, :].unsqueeze(1).to_broadcast([P, B, E]),
                                             top_f[:, :, k:k + 1].to_broadcast([P, B, E]), ALU.is_equal)
                last.then_inc(hot_d, 1)
                dve.wait_ge(hot_d, done(c))
                dve.wait_ge(rank_mm, done(c - 1))
                dve.tensor_tensor(chose[:, :, :], hot[:, 0], hot[:, 1], ALU.add).then_inc(chose_d, 1)
                dve.wait_ge(chose_d, done(c))
                for b in range(B + 1):
                    dst = earlier[:, b, :] if b < B else counts_m[:, :]
                    if b == 0:
                        dve.tensor_copy(dst, counts_m[:, :]).then_inc(early_d, 1)
                    else:
                        dve.tensor_tensor(dst, earlier[:, b - 1, :], chose[:, b - 1, :], ALU.add).then_inc(early_d, 1)
                    dve.wait_ge(early_d, c * (B + 1) + (CREDIT + b + 1))

            def find_places(c):
                dve.wait_ge(rank_mm, done(c))
                dve.tensor_tensor(rank[:, :, :], ps_rank.rearrange("p (b e) -> p b e", b=B),
                                  place0[:, :].unsqueeze(1).to_broadcast([P, B, E]), ALU.add).then_inc(rank_d, 1)
                dve.wait_ge(rank_d, done(c))
                for k in range(2):
                    last = dve.tensor_tensor(hot_rank[:, k], hot[:, k], rank[:, :, :], ALU.mult)
                last.then_inc(hotrank_d, 1)
                dve.wait_ge(gexp_d, done(c))
                dve.tensor_scalar(gap_den[:, :], gap_exp[:, :], 1.0, None, ALU.add).then_inc(den_d, 1)
                dve.wait_ge(hotrank_d, done(c))
                dve.tensor_reduce(place_f[:, :, :], hot_rank[:, :, :, :], AX.X, ALU.add).then_inc(placef_d, 1)
                dve.wait_ge(record_out, c * (2 * B * 16) + 16)
                dve.wait_ge(den_d, done(c))
                dve.reciprocal(record[:, 0, :, 1].bitcast(F32), gap_den[:, :]).then_inc(share_d, 1)
                dve.wait_ge(placef_d, done(c))
                dve.tensor_copy(place[:, :, :], place_f[:, :, :]).then_inc(place_d, 1)
                for k in range(2):
                    last = dve.tensor_copy(record[:, k, :, 0], token_id[:, :])
                last.then_inc(place_d, 1)
                dve.wait_ge(share_d, done(c))
                dve.wait_ge(place_d, c * 2 + (CREDIT + 2))
                dve.tensor_scalar(token_id[:, :], token_id[:, :], float(P), None, ALU.add).then_inc(tokid_d, 1)
                dve.tensor_tensor(record[:, 1, :, 1].bitcast(F32), gap_exp[:, :], record[:, 0, :, 1].bitcast(F32),
                                  ALU.mult).then_inc(record_d, 1)
                dve.wait_ge(tokid_d, done(c))

            def body(c, par, more):
                mask(c)
                if more:
                    first_norm(c + 1, 1 - par)
                add_out(c)
                dve.wait_ge(tok_d, done(c))
                stats(c, stat2, stat2_d, mv2, mv2_d, rs2_d)
                if more:
                    proxy_softmax_in(c + 1, 1 - par)
                dve.wait_ge(x2_out, (c + 1) * 16)
                dve.wait_ge(t2_mm, done(c - 1))
                normalise(c, x2, mv2, rs2, rs2_d, x2_d)
                if more:
                    proxy_softmax_out(c + 1)
                choose(c)
                find_places(c)

            first_norm(0, 0)
            proxy_softmax_in(0, 0)
            proxy_softmax_out(0)
            dve.wait_ge(vset, 3)
            chunks(dve, body)

        @block.tensor
        def _(pe):
            for s in (t1_mm, prod_mm, pw_mm, a_mm, state_mm, out_mm, t2_mm, logit_mm, rank_mm):
                pe.sem_inc(s, CREDIT)
            pe.wait_ge(consts, 32)
            pe.wait_ge(setup, 10)

            def turn(src, ready):
                for b in range(B):
                    for k in range(KT):
                        last = pe.transpose(ps_xt[:, (b * KT + k) * P:(b * KT + k + 1) * P], src[:, b, k * P:(k + 1) * P],
                                            ident[:, :])
                last.then_inc(ready, 1)

            def project(dst, x, w, n, ready):
                for b in range(B):
                    for k in range(KT):
                        last = pe.matmul(dst[:, b, :], x[:, b, k, :], w[:, k, :], start=k == 0, stop=k == KT - 1)
                last.then_inc(ready, 1)

            def first(c, par):
                pe.wait_ge(xn_d, done(c))
                pe.wait_ge(xt2_d, done(c - 2))
                turn(xn[:, par], t1_mm)
                pe.wait_ge(xt1_d, done(c))
                pe.wait_ge(rank_d, done(c - 2))
                project(ps_prod, xt1, proxy, NP, prod_mm)

            def first_turn(c, par):
                pe.wait_ge(pw_d, done(c))
                pe.wait_ge(state_d, done(c - 1))
                for i, src in enumerate((prod[:, par], prod_w)):
                    for b in range(B):
                        at = (i * B + b) * P
                        last = pe.transpose(ps_pw[0:NP, at:at + P], src[:, b, :], ident[:, :])
                last.then_inc(pw_mm, 1)

            def body(c, par, more):
                pe.wait_ge(pw_turned_d, done(c))
                pe.wait_ge(attn_d, done(c - 1))
                for b in range(B):
                    last = pe.matmul(ps_a[:, b * P:(b + 1) * P], turned_pw[:, par, b, :], turned_pw[:, par, B + b, :],
                                     start=True, stop=True)
                last.then_inc(a_mm, 1)
                for b in range(B):
                    last = pe.matmul(ps_pw[0:NP, b * C:(b + 1) * C], prod[:, par, b, :], xn[:, par, b, :],
                                     start=True, stop=True)
                last.then_inc(state_mm, 1)
                pe.wait_ge(attn_d, done(c))
                pe.wait_ge(tok_d, done(c - 1))
                pe.wait_ge(state_d, done(c - 1))
                for b in range(B):
                    dst = ps_out[:, b * C:(b + 1) * C]
                    pe.matmul(dst, attn[:, b, :], xn[:, par, b, :], start=True, stop=False)
                    last = pe.matmul(dst, turned_pw[:, par, B + b, :], state[:, b, :], start=False, stop=True)
                last.then_inc(out_mm, 1)
                if more:
                    first(c + 1, 1 - par)
                pe.wait_ge(x2_d, done(c))
                if more:
                    pe.wait_ge(xt1_d, done(c + 1))
                turn(x2, t2_mm)
                if more:
                    first_turn(c + 1, 1 - par)
                    pe.wait_ge(prel_d, done(c + 1))
                pe.wait_ge(xt2_d, done(c))
                project(ps_logit, xt2, gate, E, logit_mm)
                pe.wait_ge(early_d, c * (B + 1) + (CREDIT + B + 1))
                flat = [t[:, :, :].rearrange("p b e -> p (b e)") for t in (chose, earlier)]
                pe.matmul(ps_rank, before[:, :], flat[0], start=True, stop=False)
                pe.matmul(ps_rank, ones[:, :], flat[1], start=False, stop=True).then_inc(rank_mm, 1)

            first(0, 0)
            first_turn(0, 0)
            chunks(pe, body)


T_EXPERT, T_PLACE, T_FIRST, T_NEXT, T_BUFFER = range(5)


def stage_c(nc, sem, counts_m, tabs):
    with ExitStack() as ctx:
        def sb(name, shape, dt=F32):
            return ctx.enter_context(nc.sbuf_tensor(name, shape, dt))

        ones = sb("c_ones", [P, P], BF16)
        ones_f = sb("ones_f", [P, E])
        tile_id = sb("tile_id", [P, TILES])
        count_i, tiles_i = sb("count_i", [P, E], I32), sb("tiles_i", [P, E], I32)
        tiles, ends, used = sb("tiles", [P, E]), sb("ends", [P, E]), sb("used", [P, E])
        past, picked = sb("past", [P, TILES, E]), sb("picked", [P, TILES, E])
        expert, starts, run, end, nxt = (sb(n, [P, TILES]) for n in ("expert", "starts", "run", "end", "nxt"))
        runs = sb("runs", [P, 1])
        run_i = sb("run_i", [P, TILES], I32)
        ps_count = ctx.enter_context(nc.psum_tensor("ps_count", [P, E], F32))
        ready, counted, step = sem("c_ready"), sem("c_counted"), sem("c_step")
        block = ctx.enter_context(nc.Block())

        @block.gpsimd
        def _(pool):
            pool.memset(ones[:, :], 1.0).then_inc(ready, 1)
            pool.memset(ones_f[:, :], 1.0).then_inc(ready, 1)
            pool.iota(tile_id[:, :], pattern=[[1, TILES]], base=0, channel_multiplier=0,
                      allow_small_or_imprecise_dtypes=True).then_inc(ready, 1)

        @block.tensor
        def _(pe):
            pe.wait_ge(ready, 3)
            pe.matmul(ps_count[:, :], ones[:, :], counts_m[:, :], start=True, stop=True).then_inc(counted, 1)

        @block.vector
        def _(dve):
            n = 0

            def then(instruction):
                nonlocal n
                n += 1
                instruction.then_inc(step, 1)
                dve.wait_ge(step, n)

            def per_tile(x):
                return x.unsqueeze(1).to_broadcast([P, TILES, E])

            def per_expert(x):
                return x.unsqueeze(2).to_broadcast([P, TILES, E])

            dve.wait_ge(counted, 1)
            then(dve.tensor_scalar(count_i[:, :], ps_count[:, :], float(P - 1), None, ALU.add))
            then(dve.tensor_scalar(tiles_i[:, :], count_i[:, :], 7, None, ALU.arith_shift_right))
            then(dve.tensor_copy(tiles[:, :], tiles_i[:, :]))
            then(dve.tensor_tensor_scan(ends[:, :], ones_f[:, :], tiles[:, :], 0.0, ALU.mult, ALU.add))
            then(dve.tensor_tensor(past[:, :, :], per_expert(tile_id[:, :]), per_tile(ends[:, :]), ALU.is_ge))
            then(dve.tensor_reduce(expert[:, :], past[:, :, :], AX.X, ALU.add))
            then(dve.tensor_tensor(picked[:, :, :], past[:, :, :], per_tile(tiles[:, :]), ALU.mult))
            then(dve.tensor_reduce(starts[:, :], picked[:, :, :], AX.X, ALU.add))
            then(dve.tensor_scalar(used[:, :], tiles[:, :], 0.0, None, ALU.is_gt))
            then(dve.tensor_tensor(picked[:, :, :], past[:, :, :], per_tile(used[:, :]), ALU.mult))
            then(dve.tensor_reduce(run[:, :], picked[:, :, :], AX.X, ALU.add))
            then(dve.tensor_reduce(runs[:, :], used[:, :], AX.X, ALU.add))
            then(dve.tensor_scalar(runs[:, :], runs[:, :], 1.0, None, ALU.subtract))
            then(dve.tensor_scalar(run[:, :], run[:, :], runs[:, :], None, ALU.min))
            then(dve.scalar_tensor_tensor(out=picked[:, :, :], in0=past[:, :, :], scalar=float(2 * TILES),
                                          in1=per_tile(ends[:, :]), op0=ALU.mult, op1=ALU.add))
            then(dve.tensor_reduce(end[:, :], picked[:, :, :], AX.X, ALU.min))
            then(dve.tensor_tensor(picked[:, :, :], per_expert(end[:, :]), per_tile(ends[:, :]), ALU.is_ge))
            then(dve.tensor_reduce(nxt[:, :], picked[:, :, :], AX.X, ALU.add))
            then(dve.tensor_scalar(tabs[:, T_NEXT, :], nxt[:, :], float(E - 1), None, ALU.min))
            then(dve.tensor_copy(run_i[:, :], run[:, :]))
            then(dve.tensor_scalar(tabs[:, T_BUFFER, :], run_i[:, :], 1, None, ALU.bitwise_and))
            then(dve.memset(tabs[:, T_FIRST, 0:1], 1))
            then(dve.tensor_tensor(tabs[:, T_FIRST, 1:TILES], run[:, 1:TILES], run[:, 0:TILES - 1], ALU.is_gt))
            then(dve.tensor_tensor(starts[:, :], tile_id[:, :], starts[:, :], ALU.subtract))
            then(dve.tensor_scalar(nxt[:, :], expert[:, :], float(CAP // P), None, ALU.mult))
            then(dve.tensor_tensor(starts[:, :], nxt[:, :], starts[:, :], ALU.add))
            then(dve.tensor_copy(tabs[:, T_PLACE, :], starts[:, :]))
            then(dve.tensor_scalar(tabs[:, T_EXPERT, :], expert[:, :], float(E - 1), None, ALU.min))


def stage_d(nc, sem, wbuf, ident, tabs, wsplit, normed, places, b1_t, b2, out):
    with ExitStack() as ctx:
        def sb(name, shape, dt=F32):
            return ctx.enter_context(nc.sbuf_tensor(name, shape, dt))

        def ps(name, shape):
            return ctx.enter_context(nc.psum_tensor(name, shape, F32))

        bias1, bias2 = sb("bias1", [P, E, FT]), sb("bias2", [P, E, C])
        records = sb("records", [P, TILES, 2], I32)
        from_row, to_row = sb("from_row", [P, 2], I32), sb("to_row", [P, 2], I32)
        x = sb("x_rows", [P, 2, C])
        xth, xtl = sb("xth", [P, 2, KT, P], F32R), sb("xtl", [P, 2, KT, P], F32R)
        h = sb("h", [P, F])
        hb = sb("hb", [P, FT, P])
        g = sb("g", [P, FT, P])
        gh, gl = sb("gh", [P, 2, FT, P], F32R), sb("gl", [P, 2, FT, P], F32R)
        yb, y = sb("yb", [P, C]), sb("y", [P, 2, C])
        ps_x = ps("ps_x", [P, KT * P])
        ps_h = ps("ps_h", [P, F])
        ps_ht = ps("ps_ht", [P, F])
        ps_y = [ps(f"ps_y{i}", [P, HALF]) for i in range(2)]

        consts, record_in = sem("d_consts"), sem("d_record_in")
        w_in = [sem("d_w1_in"), sem("d_w2_in")]
        x_in = [sem("d_x_in0"), sem("d_x_in1")]
        y_out, from_d, to_d = sem("d_y_out"), sem("d_from_row"), sem("d_to_row")
        xt_mm, h_mm, ht_mm, y_mm = sem("d_xt_mm"), sem("d_h_mm"), sem("d_ht_mm"), sem("d_y_mm")
        xh_d, h_d, g_d = sem("d_x_high"), sem("d_h"), sem("d_g")
        xl_d, hb_d, gh_d, gl_d, yb_d, y_d = (sem("d_" + n) for n in ("x_low", "hb", "g_high", "g_low", "yb", "y"))
        AHEAD = 4

        def steps(eng, body, first, last):
            lo, hi = max(first, 4), TILES - 1 - AHEAD
            hi -= (hi - lo) % 2
            for u in range(first, lo):
                body(u, u % 2)
            with eng.Fori(0, (hi - lo) // 2) as k:
                for i in range(2):
                    body(k * 2 + (lo + i), (lo + i) % 2)
            for u in range(hi, last + 1):
                body(u, u % 2)

        def exists(u):
            return not isinstance(u, int) or 0 <= u < TILES

        def entry(eng, row, u, top):
            return eng.value_load(tabs[0:1, row, bass.ds(u, 1)], min_val=0, max_val=top)

        def half(u, par):
            return u // 2 if isinstance(u, int) else (u - par) // 2

        block = ctx.enter_context(nc.Block())

        @block.sync
        def _(sp):
            def load_record(u):
                if u is not None:
                    at = entry(sp, T_PLACE, u, SLOTS // P - 1)
                    sp.dma_start(records[:, bass.ds(u, 1), :].rearrange("p a r -> p (a r)"),
                                 places.rearrange("(t p) r -> t p r", p=P)[bass.ds(at, 1)].rearrange("a p r -> (a p) r")
                                 ).then_inc(record_in, 16)

            def load_weights(part, expert, buffer, cond=None):
                at = slice(part * W2AT, (part + 1) * W2AT)
                sp.dma_start(wbuf[:, bass.ds(buffer, 1), at].rearrange("p a w -> p (a w)").bitcast(F32),
                             wsplit[bass.ds(expert, 1)].rearrange("a p w -> (a p) w")[:, at],
                             **({} if cond is None else {"cond": cond})).then_inc(w_in[part], 16)

            e0 = entry(sp, T_EXPERT, 0, E - 1)
            for part in range(2):
                load_weights(part, e0, 0)
            load_record(0)
            for u in range(1, AHEAD):
                sp.wait_ge(record_in, 16 * u)
                load_record(u)
            sp.dma_start(bias1[:, :, :], b1_t).then_inc(consts, 16)
            sp.dma_start(bias2[:, :, :].rearrange("p e c -> p (e c)"),
                         b2.rearrange("e c -> (e c)").partition_broadcast(P)).then_inc(consts, 16)

            def body(u, par):
                if exists(u + AHEAD):
                    wait_apart(sp, record_in, (u + AHEAD) * 16)
                    load_record(u + AHEAD)
                first = entry(sp, T_FIRST, u, 1)
                nxt = entry(sp, T_NEXT, u, E - 1)
                buffer = entry(sp, T_BUFFER, u, 1)
                for part, used in enumerate((h_mm, y_mm)):
                    wait_apart(sp, used, done(u - 1))
                    wait_apart(sp, w_in[part], (u + 1) * 16)
                    load_weights(part, nxt, 1 - buffer, cond=first)

            steps(sp, body, 0, TILES - 2)
            for part in range(2):
                sp.wait_ge(w_in[part], TILES * 16)

        @block.gpsimd
        def _(pool):
            for s in (from_d, to_d):
                pool.sem_inc(s, CREDIT)

            def later(u, step):
                return not isinstance(u, int) or u >= step

            def gather(u, par):
                if later(u, 2):
                    wait_apart(pool, x_in[par], half(u, par) * 16)
                wait_apart(pool, record_in, (u + 1) * 16)
                pool.tensor_copy(from_row[:, par:par + 1], records[:, bass.ds(u, 1), 0]).then_inc(from_d, 1)
                wait_apart(pool, xt_mm, done(u - 2))
                wait_apart(pool, from_d, done(u))
                pool.indirect_dma_start(out=x[:, par, :], out_offset=None, in_=normed,
                                        in_offset=bass.IndirectOffsetOnAxis(ap=from_row[:, par:par + 1], axis=0)
                                        ).then_inc(x_in[par], 16)

            def scatter(u, par):
                if later(u, 1):
                    wait_apart(pool, y_out, u * 16)
                pool.tensor_copy(to_row[:, par:par + 1], records[:, bass.ds(u, 1), 0]).then_inc(to_d, 1)
                wait_apart(pool, y_d, done(u))
                wait_apart(pool, to_d, done(u))
                pool.indirect_dma_start(out=out, out_offset=bass.IndirectOffsetOnAxis(ap=to_row[:, par:par + 1], axis=0),
                                        in_=y[:, par, :], in_offset=None, compute_op=ALU.add).then_inc(y_out, 16)

            def body(u, par):
                if exists(u + 3):
                    gather(u + 3, 1 - par)
                if exists(u - 2):
                    scatter(u - 2, par)

            for u in range(3):
                gather(u, u % 2)
            steps(pool, body, 0, TILES + 1)
            pool.wait_ge(y_out, TILES * 16)

        @block.scalar
        def _(act):
            for s in (xh_d, h_d, g_d):
                act.sem_inc(s, CREDIT)

            def x_high(u, par):
                act.wait_ge(xt_mm, done(u))
                act.wait_ge(h_mm, done(u - 2))
                act.activation(xth[:, par], ps_x[:, :].rearrange("p (k t) -> p k t", k=KT), ACT.Copy).then_inc(xh_d, 1)

            def body(u, par):
                if exists(u):
                    act.wait_ge(h_mm, done(u))
                    act.wait_ge(ht_mm, done(u - 1))
                    act.activation(h[:, :], ps_h[:, :], ACT.Copy).then_inc(h_d, 1)
                if exists(u + 2):
                    x_high(u + 2, par)
                if exists(u):
                    act.wait_ge(hb_d, done(u))
                    act.wait_ge(gl_d, done(u - 1))
                    act.activation(g[:, :, :], hb[:, :, :], ACT.Gelu_apprx_tanh).then_inc(g_d, 1)

            x_high(0, 0)
            x_high(1, 1)
            steps(act, body, 0, TILES - 1)

        @block.vector
        def _(dve):
            for s in (xl_d, hb_d, gh_d, gl_d, yb_d, y_d):
                dve.sem_inc(s, CREDIT)
            dve.wait_ge(consts, 32)

            def x_low(u, par):
                dve.wait_ge(xh_d, done(u))
                dve.tensor_tensor(xtl[:, par], ps_x[:, :].rearrange("p (k t) -> p k t", k=KT), xth[:, par].bitcast(F32),
                                  ALU.subtract).then_inc(xl_d, 1)

            def result(u, par):
                e = entry(dve, T_EXPERT, u, E - 1)
                dve.wait_ge(y_mm, done(u))
                dve.wait_ge(y_d, done(u - 1))
                dve.tensor_tensor(yb[:, :], ps_y[par][:, 0:C], bias2[:, bass.ds(e, 1), :].rearrange("p a c -> p (a c)"),
                                  ALU.add).then_inc(yb_d, 1)
                if exists(u - 2):
                    dve.wait_ge(y_out, (u - 1) * 16)
                dve.wait_ge(yb_d, done(u))
                share = records[:, bass.ds(u, 1), 1].bitcast(F32)
                dve.tensor_scalar(y[:, par, :], yb[:, :], share, None, ALU.mult).then_inc(y_d, 1)

            def body(u, par):
                if exists(u - 2):
                    result(u - 2, par)
                if exists(u):
                    e = entry(dve, T_EXPERT, u, E - 1)
                    dve.wait_ge(ht_mm, done(u))
                    dve.wait_ge(g_d, done(u - 1))
                    bias = bias1[:, bass.ds(e, 1), :].rearrange("p a f -> p (a f)").unsqueeze(2).to_broadcast([P, FT, P])
                    dve.tensor_tensor(hb[:, :, :], ps_ht[:, :].rearrange("p (f t) -> p f t", f=FT), bias,
                                      ALU.add).then_inc(hb_d, 1)
                if exists(u + 2):
                    x_low(u + 2, par)
                if exists(u):
                    dve.wait_ge(g_d, done(u))
                    dve.wait_ge(y_mm, done(u - 2))
                    dve.tensor_copy(gh[:, par], g[:, :, :]).then_inc(gh_d, 1)
                    dve.wait_ge(gh_d, done(u))
                    dve.tensor_tensor(gl[:, par], g[:, :, :], gh[:, par].bitcast(F32), ALU.subtract).then_inc(gl_d, 1)

            dve.wait_ge(record_in, AHEAD * 16)
            x_low(0, 0)
            x_low(1, 1)
            steps(dve, body, 0, TILES + 1)

        @block.tensor
        def _(pe):
            for s in (xt_mm, h_mm, ht_mm, y_mm):
                pe.sem_inc(s, CREDIT)

            def turn_x(u, par):
                pe.wait_ge(x_in[par], (half(u, par) + 1) * 16)
                pe.wait_ge(xl_d, done(u - 1))
                for k in range(KT):
                    last = pe.transpose(ps_x[:, k * P:(k + 1) * P], x[:, par, k * P:(k + 1) * P], ident[:, :])
                last.then_inc(xt_mm, 1)

            def weights(u, part):
                buffer = entry(pe, T_BUFFER, u, 1)
                both = wbuf[:, bass.ds(buffer, 1), part * W2AT:(part + 1) * W2AT].rearrange("p a w -> p (a w)")
                rows = (KT, FT)[part]
                return [both[:, i * W2AT // 2:(i + 1) * W2AT // 2].rearrange("p (k n) -> p k n", k=rows) for i in range(2)]

            def layer1(u, par):
                wh, wl = weights(u, 0)
                pe.wait_ge(w_in[0], (u + 1) * 16)
                pe.wait_ge(xl_d, done(u))
                pe.wait_ge(h_d, done(u - 1))
                for n in range(F // HALF):
                    cols = slice(n * HALF, (n + 1) * HALF)
                    for k in range(KT):
                        last = mm3(pe, ps_h[:, cols], (xth[:, par, k], xtl[:, par, k]), (wh[:, k, cols], wl[:, k, cols]),
                                   HALF, k == 0, k == KT - 1)
                last.then_inc(h_mm, 1)

            def turn_h(u):
                pe.wait_ge(h_d, done(u))
                pe.wait_ge(hb_d, done(u - 1))
                for f in range(FT):
                    last = pe.transpose(ps_ht[:, f * P:(f + 1) * P], h[:, f * P:(f + 1) * P], ident[:, :])
                last.then_inc(ht_mm, 1)

            def layer2(u, par):
                wh, wl = weights(u, 1)
                pe.wait_ge(w_in[1], (u + 1) * 16)
                pe.wait_ge(gl_d, done(u))
                pe.wait_ge(yb_d, done(u - 2))
                for f in range(FT):
                    last = mm3(pe, ps_y[par][:, 0:C], (gh[:, par, f], gl[:, par, f]), (wh[:, f], wl[:, f]), C,
                               f == 0, f == FT - 1)
                last.then_inc(y_mm, 1)

            def body(u, par):
                if exists(u):
                    layer1(u, par)
                if exists(u - 2):
                    layer2(u - 2, par)
                if exists(u):
                    turn_h(u)
                if exists(u + 2):
                    turn_x(u + 2, par)

            turn_x(0, 0)
            turn_x(1, 1)
            steps(pe, body, 0, TILES + 1)


INPUTS = ["x_ch", "x_tok", "wqk3", "bqk3", "wv_t", "bv", "alpha", "proxy_t", "gate_t", "w1", "b1_t", "w2", "b2"]


def kernel(x, L0_conv_Wq, L0_conv_bq, L0_conv_Wk, L0_conv_bk, L0_conv_Wv, L0_conv_bv, L0_conv_alpha,
           L1_attn_proxy, L1_ffn_gate_w, L1_ffn_w1, L1_ffn_b1, L1_ffn_w2, L1_ffn_b2):
    import numpy as np
    import concourse.bacc as bacc
    from concourse.bass_utils import run_bass_kernel_spmd

    flat = np.asarray(x).reshape(B, C, N)
    wq, wk, wv = (np.asarray(w) for w in (L0_conv_Wq, L0_conv_Wk, L0_conv_Wv))
    laid = {
        "x_ch": flat,
        "x_tok": flat.transpose(0, 2, 1).reshape(TOK, C),
        "wqk3": np.stack([np.tile(wq.T, (1, 3)), np.tile(wk.T, (1, 3))]),
        "bqk3": np.stack([np.tile(np.asarray(L0_conv_bq), 3), np.tile(np.asarray(L0_conv_bk), 3)], axis=1),
        "wv_t": wv.T,
        "bv": L0_conv_bv,
        "alpha": L0_conv_alpha,
        "proxy_t": np.asarray(L1_attn_proxy).T,
        "gate_t": np.asarray(L1_ffn_gate_w).T,
        "w1": L1_ffn_w1,
        "b1_t": np.asarray(L1_ffn_b1).reshape(E, FT, P).transpose(2, 0, 1),
        "w2": L1_ffn_w2,
        "b2": L1_ffn_b2,
    }
    nc = bacc.Bacc("TRN2", target_bir_lowering=False, num_devices=1)
    arrays, args = {}, []
    for name in INPUTS:
        a = np.ascontiguousarray(laid[name])
        arrays[f"in_{name}"] = a
        args.append(nc.dram_tensor(f"in_{name}", a.shape, mybir.dt.from_np(a.dtype), kind="ExternalInput").ap())
    out = nc.dram_tensor("out_tok", (TOK + P, C), F32, kind="ExternalOutput").ap()
    build(nc, *args, out)
    got = run_bass_kernel_spmd(nc, [arrays], core_ids=[0]).results[0]["out_tok"]
    return np.ascontiguousarray(np.asarray(got)[:TOK].reshape(B, N, C).transpose(0, 2, 1)).reshape(x.shape)
```

```python
from contextlib import ExitStack

import concourse.bass as bass
from concourse import mybir
from concourse.alu_op_type import AluOpType as ALU

F32 = mybir.dt.float32
F32R = mybir.dt.float32r
BF16 = mybir.dt.bfloat16
I32 = mybir.dt.int32
U32 = mybir.dt.uint32
ACT = mybir.ActivationFunctionType
AX = mybir.AxisListType

P = 128
B, C, N = 4, 256, 1024
KT = C // P
IT = N // P
NT = B * IT
TOK = B * N
MID = 32
HALF = 512
NP = 16
E, F = 8, 1024
FT = F // P
CAP = TOK
TILES = 2 * TOK // P + E - 1
SLOTS = -(-(E * CAP + E * P) // (P * P)) * P * P
WROW = 2 * KT * F + 2 * FT * C
W2AT = 2 * KT * F
LN_EPS = 1e-5
CREDIT = 2


def done(i):
    return i + (CREDIT + 1)


def wait_apart(eng, sem, value):
    eng.wait_ge(sem, value)
    eng.nop(nofuse=True)


def mm3(eng, out, lhs, rhs, cols, first=True, last=True):
    (lh, ll), (rh, rl) = lhs, rhs
    eng.matmul(out, ll, rh, start=first, stop=False)
    eng.matmul(out, lh, rl, start=False, stop=False)
    return eng.matmul(out, lh, rh, start=False, stop=last)


def build(nc, x_ch, x_tok, wqk3, bqk3, wv_t, bv, alpha, proxy_t, gate_t, w1, b1_t, w2, b2, out):
    wsplit = nc.dram_tensor("wsplit", [E, P, WROW], F32, kind="Internal").ap()
    normed = nc.dram_tensor("normed", [TOK + P, C], F32, kind="Internal").ap()
    places = nc.dram_tensor("places", [SLOTS, 2], I32, kind="Internal").ap()
    with ExitStack() as outer:
        def sem(name):
            return outer.enter_context(nc.semaphore(name))

        def keep(name, shape, dt=F32):
            return outer.enter_context(nc.sbuf_tensor(name, shape, dt))

        tok = keep("tok", [P, NT, C])
        wbuf = keep("wbuf", [P, 2, WROW], F32R)
        ident = keep("ident", [P, P])
        stage_a(nc, sem, tok, wbuf, ident, wsplit, x_ch, x_tok, wqk3, bqk3, wv_t, bv, alpha, w1, w2)
        tabs = keep("tabs", [P, 5, TILES], I32)
        bias1, bias2 = keep("bias1", [P, E, FT]), keep("bias2", [P, E, C])
        stage_b(nc, sem, tok, ident, tabs, bias1, bias2, normed, places, proxy_t, gate_t, b1_t, b2, out)
        stage_d(nc, sem, wbuf, ident, tabs, bias1, bias2, wsplit, normed, places, out)


def stage_a(nc, sem, tok, wbuf, ident, wsplit, x_ch, x_tok, wqk3, bqk3, wv_t, bv, alpha, w1, w2):
    with ExitStack() as ctx:
        def sb(name, shape, dt=F32):
            return ctx.enter_context(nc.sbuf_tensor(name, shape, dt))

        xraw = sb("xraw", [P, KT, N])
        xh, xl = sb("xh", [P, KT, N], F32R), sb("xl", [P, KT, N], F32R)
        wq_raw = sb("wq_raw", [P, 2, KT, 3 * MID])
        wqh, wql = sb("wqh", [P, 2, KT, 3 * MID], F32R), sb("wql", [P, 2, KT, 3 * MID], F32R)
        bqk = sb("bqk", [3 * MID, 2])
        wv_raw = sb("wv_raw", [P, KT, C])
        wvh, wvl = sb("wvh", [P, KT, C], F32R), sb("wvl", [P, KT, C], F32R)
        bvb = sb("bvb", [P, 1, C])
        alb = sb("alb", [P, 1])
        qk3 = sb("qk3", [3 * MID, 2, N], F32R)
        vf = sb("vf", [P, 2, HALF])
        vh, vl = sb("vh", [P, IT, C], F32R), sb("vl", [P, IT, C], F32R)
        prob = sb("prob", [P, 2, N])
        qkf = prob[0:3 * MID]
        pth, ptl = sb("pth", [P, 2, IT, P], F32R), sb("ptl", [P, 2, IT, P], F32R)
        negmax, rowsum, scale = sb("negmax", [P, 4]), sb("rowsum", [P, 4]), sb("scale", [P, 4])
        wraw = sb("wraw", [P, 2, WROW // 4])

        ps_sc = ctx.enter_context(nc.psum_tensor("ps_sc", [P, N], F32))
        ps_pt = [ctx.enter_context(nc.psum_tensor(f"ps_pt{i}", [P, N], F32)) for i in range(2)]
        ps_o = [ctx.enter_context(nc.psum_tensor(f"ps_o{i}", [P, HALF], F32)) for i in range(2)]

        wqk_in, consts, x_in, tok_in = sem("a_wqk_in"), sem("a_consts"), sem("a_x_in"), sem("a_tok_in")
        ident0, ident_ok, wsm_hi, wsm_ok = sem("a_ident0"), sem("a_ident"), sem("a_wsm_hi"), sem("a_wsm")
        x_hi, x_split = sem("a_x_hi"), sem("a_x_split")
        qk_mm, qk_full, qk_hi, qk_ok = sem("a_qk_mm"), sem("a_qk_full"), sem("a_qk_hi"), sem("a_qk_ok")
        v_mm, v_full, v_hi, v_ok = sem("a_v_mm"), sem("a_v_full"), sem("a_v_hi"), sem("a_v_ok")
        scored, maxed, exped = sem("a_scored"), sem("a_maxed"), sem("a_exped")
        turned, pt_hi, pt_ok = sem("a_turned"), sem("a_pt_hi"), sem("a_pt_ok")
        recip, scaled = sem("a_recip"), sem("a_scaled")
        summed, added = sem("a_summed"), sem("a_added")
        w_in, w_hi, w_lo = [sem("a_w1_in"), sem("a_w2_in")], sem("a_w_hi"), sem("a_w_lo")
        w_out = [[sem(f"a_w{part + 1}_out{par}") for part in range(2)] for par in range(2)]

        def images(eng, image):
            with eng.Fori(0, B - 1) as b:
                image(b, True)
            image(B - 1, False)

        block = ctx.enter_context(nc.Block())

        @block.sync
        def _(sp):
            for kind in range(2):
                sp.dma_start(wq_raw[:, kind], wqk3[kind].rearrange("(k p) m -> p k m", p=P)).then_inc(wqk_in, 16)
            sp.dma_start(bqk[:, :], bqk3).then_inc(consts, 16)
            sp.dma_start(wv_raw[:, :, :], wv_t.rearrange("(k p) m -> p k m", p=P)).then_inc(consts, 16)
            sp.dma_start(bvb[:, 0, :], bv.partition_broadcast(P)).then_inc(consts, 16)
            sp.dma_start(alb[:, :], alpha.partition_broadcast(P)).then_inc(consts, 16)
            sp.wait_ge(x_in, 16)
            sp.wait_ge(consts, 64)
            sp.dma_start(tok[:, :, :], x_tok.rearrange("(g p) c -> p g c", p=P)).then_inc(tok_in, 16)

            def load(e, part):
                src = (w1, w2)[part][bass.ds(e, 1)].rearrange("a (k p) f -> p (a k) f", p=P)
                dst = wraw[:, part].rearrange("p (k f) -> p k f", k=(KT, FT)[part])
                sp.dma_start(dst, src).then_inc(w_in[part], 16)

            def store(i, par, part):
                wait_apart(sp, w_lo, done(i * 2 + part))
                at = slice(part * W2AT, (part + 1) * W2AT)
                sp.dma_start(wsplit[bass.ds(i + 2, 1)].rearrange("a p w -> (a p) w")[:, at],
                             wbuf[:, par, at].bitcast(F32)).then_inc(w_out[par][part], 16)

            load(2, 0)
            load(2, 1)
            with sp.Fori(0, E // 2 - 1) as h:
                for par in range(2):
                    for part in range(2):
                        store(h * 2 + par, par, part)
                        load((h * 2 + (par + 3)) % E, part)
            for part in range(2):
                wait_apart(sp, w_lo, done((E - 2) * 2 + part))
                load(1, part)
            for s in w_out[0] + w_out[1]:
                sp.wait_ge(s, 16 * (E // 2))

        @block.gpsimd
        def _(pool):
            pool.sem_inc(w_lo, CREDIT)
            pool.sem_inc(v_ok, CREDIT)
            for s in w_out[0] + w_out[1]:
                pool.sem_inc(s, 16)
            pool.memset(ident[:, :], 0.0).then_inc(ident0, 1)
            pool.wait_ge(ident0, 1)
            pool.affine_select(out=ident[:, :], in_=ident[:, :], compare_op=ALU.not_equal, fill=1.0,
                               base=0, pattern=[[-1, P]], channel_multiplier=1).then_inc(ident_ok, 1)

            def image(b, more):
                for ch in range(4):
                    pool.wait_ge(v_hi, done(b * 4 + ch))
                    pool.tensor_tensor(vl[:, 2 * ch:2 * ch + 2, :], vf[:, ch % 2].rearrange("p (j c) -> p j c", j=2),
                                       vh[:, 2 * ch:2 * ch + 2, :].bitcast(F32), ALU.subtract).then_inc(v_ok, 1)
                for par in range(2):
                    for part in range(2):
                        pool.wait_ge(w_hi, (b * 4 + (par * 2 + part + 1)) * 2)
                        at, n = part * W2AT, W2AT // 2
                        pool.tensor_tensor(wbuf[:, par, at + n:at + 2 * n], wraw[:, part],
                                           wbuf[:, par, at:at + n].bitcast(F32), ALU.subtract).then_inc(w_lo, 1)
                        if more and (par, part) == (0, 1):
                            pool.wait_ge(x_hi, b + 3)
                            pool.tensor_tensor(xl[:, :, :], xraw[:, :, :], xh[:, :, :].bitcast(F32),
                                               ALU.subtract).then_inc(x_split, 1)

            images(pool, image)

        @block.scalar
        def _(act):
            for s in (exped, pt_hi, qk_full, v_hi):
                act.sem_inc(s, CREDIT)
            def load_x(b):
                act.dma_start(xraw[:, :, :], x_ch[bass.ds(b, 1)].rearrange("a (k p) n -> p (a k) n", p=P)).then_inc(x_in, 16)

            def whole_qk(b, kind):
                act.wait_ge(qk_mm, done(b * 2 + kind))
                act.wait_ge(turned, done(b * IT - 2 + kind))
                act.activation(qkf[:, kind], (ps_sc, ps_pt[0])[kind][0:3 * MID, :], ACT.Identity,
                               bias=bqk[:, kind:kind + 1]).then_inc(qk_full, 1)

            def image(b, more):
                def high_v(ch):
                    act.wait_ge(v_full, done(b * 4 + ch))
                    if ch == 0:
                        act.wait_ge(summed, done(b * IT - 1))
                    act.activation(vh[:, 2 * ch:2 * ch + 2, :], vf[:, ch % 2], ACT.Copy).then_inc(v_hi, 1)

                def exp_tile(it):
                    act.wait_ge(maxed, done(b * IT + it))
                    act.wait_ge(turned, done(b * IT + it - 2))
                    col = slice(it % 4, it % 4 + 1)
                    act.activation(prob[:, it % 2], ps_sc[:, :], ACT.Exp, bias=negmax[:, col],
                                   accum_out=rowsum[:, col]).then_inc(exped, 1)

                def hi_tile(it):
                    act.wait_ge(turned, done(b * IT + it))
                    act.wait_ge(summed, done(b * IT + it - 2))
                    act.activation(pth[:, it % 2], ps_pt[it % 2].rearrange("p (j i) -> p j i", j=IT),
                                   ACT.Copy).then_inc(pt_hi, 1)

                def weights_high(it):
                    par, part, half = it // 4, it // 2 % 2, it % 2
                    if half == 0:
                        act.wait_ge(w_in[part], (b * 2 + (par + 1)) * 16)
                        act.wait_ge(w_out[par][part], (b + 1) * 16)
                    at, n = part * W2AT, W2AT // 4
                    act.activation(wbuf[:, par, at + half * n:at + (half + 1) * n], wraw[:, part, half * n:(half + 1) * n],
                                   ACT.Copy).then_inc(w_hi, 1)

                high_v(0)
                high_v(1)
                exp_tile(0)
                high_v(2)
                high_v(3)
                exp_tile(1)
                hi_tile(0)
                for it in range(IT):
                    if it == 7 and more:
                        whole_qk(b + 1, 0)
                    weights_high(it)
                    if it + 1 < IT:
                        hi_tile(it + 1)
                    if it + 2 < IT:
                        exp_tile(it + 2)
                    if it == 2 and more:
                        act.wait_ge(x_in, (b + 2) * 16)
                        act.wait_ge(v_mm, done(b * 4 + 3))
                        act.activation(xh[:, :, :], xraw[:, :, :], ACT.Copy).then_inc(x_hi, 1)
                    if it == 6 and more:
                        wait_apart(act, x_split, b + 3)
                        load_x((b + 2) % B)
                if more:
                    whole_qk(b + 1, 1)

            load_x(0)
            act.wait_ge(x_in, 16)
            for k in range(KT):
                act.activation(xh[:, k], xraw[:, k], ACT.Copy).then_inc(x_hi, 1)
            act.wait_ge(x_split, 2)
            load_x(1)
            act.wait_ge(consts, 64)
            whole_qk(0, 0)
            whole_qk(0, 1)
            images(act, image)
            act.wait_ge(x_in, 16 * (B + 1))

        @block.vector
        def _(dve):
            for s in (qk_ok, v_full, maxed, pt_ok, scaled, recip, added, qk_hi):
                dve.sem_inc(s, CREDIT)
            dve.wait_ge(wqk_in, 32)
            dve.tensor_copy(wqh[:, :, :, :], wq_raw[:, :, :, :]).then_inc(wsm_hi, 1)
            dve.wait_ge(wsm_hi, 1)
            dve.tensor_tensor(wql[:, :, :, :], wq_raw[:, :, :, :], wqh[:, :, :, :].bitcast(F32), ALU.subtract).then_inc(wsm_ok, 1)
            for k in range(KT):
                dve.wait_ge(x_hi, k + 1)
                dve.tensor_tensor(xl[:, k], xraw[:, k], xh[:, k].bitcast(F32), ALU.subtract).then_inc(x_split, 1)
            dve.wait_ge(consts, 64)
            dve.tensor_copy(wvh[:, :, :], wv_raw[:, :, :]).then_inc(wsm_hi, 1)
            dve.wait_ge(wsm_hi, 2)
            dve.tensor_tensor(wvl[:, :, :], wv_raw[:, :, :], wvh[:, :, :].bitcast(F32), ALU.subtract).then_inc(wsm_ok, 1)

            def stack(b, kind):
                dve.wait_ge(qk_full, done(b * 2 + kind))
                dve.wait_ge(scored, done(b * IT - 1))
                dve.tensor_copy(qk3[:, kind], qkf[:, kind]).then_inc(qk_hi, 1)
                dve.wait_ge(qk_hi, done(b * 2 + kind))
                at = slice(MID, 2 * MID) if kind == 0 else slice(2 * MID, 3 * MID)
                dve.tensor_tensor(qk3[at, kind], qkf[at, kind], qk3[at, kind].bitcast(F32), ALU.subtract).then_inc(qk_ok, 1)

            def image(b, more):
                def full_v(ch):
                    dve.wait_ge(v_mm, done(b * 4 + ch))
                    dve.wait_ge(v_ok, done(b * 4 + ch - 2))
                    src = ps_pt[1][:, ch * HALF:(ch + 1) * HALF] if ch < 2 else ps_o[ch - 2][:, :]
                    dve.tensor_tensor(vf[:, ch % 2].rearrange("p (j c) -> p j c", j=2), src.rearrange("p (j c) -> p j c", j=2),
                                      bvb[:, :, :].to_broadcast([P, 2, C]), ALU.add).then_inc(v_full, 1)

                def max_tile(it):
                    dve.wait_ge(scored, done(b * IT + it))
                    dve.tensor_reduce(negmax[:, it % 4:it % 4 + 1], ps_sc[:, :], AX.X, ALU.max, negate=True).then_inc(maxed, 1)

                def low_tile(it):
                    h = it % 2
                    dve.wait_ge(pt_hi, done(b * IT + it))
                    dve.tensor_tensor(ptl[:, h], ps_pt[h].rearrange("p (j i) -> p j i", j=IT), pth[:, h].bitcast(F32),
                                      ALU.subtract).then_inc(pt_ok, 1)

                full_v(0)
                full_v(1)
                max_tile(0)
                full_v(2)
                full_v(3)
                max_tile(1)
                low_tile(0)
                for it in range(IT):
                    g, h = b * IT + it, it % 2
                    col = slice(it % 4, it % 4 + 1)
                    if it + 2 < IT:
                        max_tile(it + 2)
                    dve.wait_ge(exped, done(g))
                    dve.reciprocal(scale[:, col], rowsum[:, col]).then_inc(recip, 1)
                    if it + 1 < IT:
                        low_tile(it + 1)
                    dve.wait_ge(recip, done(g))
                    dve.tensor_tensor(scale[:, col], scale[:, col], alb[:, :], ALU.mult).then_inc(scaled, 1)
                    dve.wait_ge(scaled, done(g))
                    if it == 0:
                        wait_apart(dve, tok_in, 16)
                    dve.wait_ge(summed, done(g))
                    mine = tok[:, bass.ds(g, 1), :].rearrange("p a c -> p (a c)")
                    dve.scalar_tensor_tensor(out=mine, in0=ps_o[h][:, 0:C], scalar=scale[:, col], in1=mine,
                                             op0=ALU.mult, op1=ALU.add).then_inc(added, 1)
                    if more and it >= IT - 2:
                        stack(b + 1, it - (IT - 2))

            stack(0, 0)
            stack(0, 1)
            images(dve, image)

        @block.tensor
        def _(pe):
            for s in (qk_mm, v_mm, scored, turned, summed):
                pe.sem_inc(s, CREDIT)
            pe.wait_ge(wsm_ok, 1)
            pe.wait_ge(ident_ok, 1)

            def project_qk(b, kind):
                if kind == 0:
                    pe.wait_ge(x_split, b + 2)
                    pe.wait_ge(exped, done(b * IT - 1))
                else:
                    pe.wait_ge(pt_ok, done(b * IT - 2))
                dst = (ps_sc, ps_pt[0])[kind]
                for n in range(N // HALF):
                    cols = slice(n * HALF, (n + 1) * HALF)
                    for k in range(KT):
                        last = mm3(pe, dst[0:3 * MID, cols], (wqh[:, kind, k], wql[:, kind, k]),
                                   (xh[:, k, cols], xl[:, k, cols]), HALF, k == 0, k == KT - 1)
                last.then_inc(qk_mm, 1)

            def image(b, more):
                pe.wait_ge(pt_ok, done(b * IT - 1))

                def project_v(ch):
                    if ch == 2:
                        pe.wait_ge(added, done(b * IT - 1))
                    dst = ps_pt[1][:, ch * HALF:(ch + 1) * HALF] if ch < 2 else ps_o[ch - 2][:, :]
                    for j in range(2):
                        rows = slice((2 * ch + j) * P, (2 * ch + j + 1) * P)
                        for k in range(KT):
                            last = mm3(pe, dst[:, j * C:(j + 1) * C], (xh[:, k, rows], xl[:, k, rows]),
                                       (wvh[:, k], wvl[:, k]), C, k == 0, k == KT - 1)
                    last.then_inc(v_mm, 1)

                def score(it):
                    if it == 0:
                        pe.wait_ge(qk_full, done(b * 2))
                        pe.wait_ge(qk_ok, done(b * 2 + 1))
                    pe.wait_ge(exped, done(b * IT + it - 1))
                    for n in range(N // HALF):
                        cols = slice(n * HALF, (n + 1) * HALF)
                        last = pe.matmul(ps_sc[:, cols], qk3[:, 0, it * P:(it + 1) * P], qk3[:, 1, cols],
                                         start=True, stop=True)
                    last.then_inc(scored, 1)

                def turn(it):
                    pe.wait_ge(exped, done(b * IT + it))
                    pe.wait_ge(pt_ok, done(b * IT + it - 2))
                    if it == 1:
                        pe.wait_ge(v_full, done(b * 4 + 1))
                    for j in range(IT):
                        last = pe.transpose(ps_pt[it % 2][:, j * P:(j + 1) * P], prob[:, it % 2, j * P:(j + 1) * P], ident[:, :])
                    last.then_inc(turned, 1)

                def weigh(it):
                    pe.wait_ge(pt_ok, done(b * IT + it))
                    pe.wait_ge(added, done(b * IT + it - 2))
                    if it == 0:
                        pe.wait_ge(v_ok, done(b * 4 + 3))
                    for j in range(IT):
                        last = mm3(pe, ps_o[it % 2][:, 0:C], (pth[:, it % 2, j], ptl[:, it % 2, j]),
                                   (vh[:, j], vl[:, j]), C, j == 0, j == IT - 1)
                    last.then_inc(summed, 1)

                project_v(0)
                project_v(1)
                score(0)
                project_v(2)
                project_v(3)
                score(1)
                turn(0)
                for it in range(IT):
                    if it + 2 < IT:
                        score(it + 2)
                    if it + 1 < IT:
                        turn(it + 1)
                    if more and it >= IT - 2:
                        project_qk(b + 1, it - (IT - 2))
                    weigh(it)

            project_qk(0, 0)
            project_qk(0, 1)
            pe.wait_ge(wsm_ok, 2)
            images(pe, image)


def stage_b(nc, sem, tok, ident, tabs, bias1, bias2, normed, places, proxy_t, gate_t, b1_t, b2, out):
    with ExitStack() as ctx:
        def sb(name, shape, dt=F32):
            return ctx.enter_context(nc.sbuf_tensor(name, shape, dt))

        def ps(name, shape):
            return ctx.enter_context(nc.psum_tensor(name, shape, F32))

        proxy, gate = sb("proxy", [P, KT, NP]), sb("gate", [P, KT, E])
        causal = sb("causal", [P, P])
        before = sb("before", [P, P], BF16)
        ones = sb("ones", [P, P], BF16)
        minus_half, minus_one, eps = sb("minus_half", [P, B]), sb("minus_one", [P, B]), sb("eps", [P, B])
        expert_id = sb("expert_id", [P, E])
        place0 = sb("place0", [P, E])
        token_id = sb("token_id", [P, B])
        no_token = sb("no_token", [P, SLOTS // P, 2], I32)
        xn = sb("xn", [P, 2, B, C])
        xt1 = sb("xt1", [P, B, KT, P])
        prod = sb("prod", [P, 2, B, NP])
        prod_rel, prod_w = sb("prod_rel", [P, B, NP]), sb("prod_w", [P, B, NP])
        prod_max, prod_sum = sb("prod_max", [P, B]), sb("prod_sum", [P, B])
        turned_pw = sb("turned_pw", [NP, 2, 2 * B, P])
        attn = sb("attn", [P, B, P])
        state = sb("state", [NP, 2, B, C])
        stat1, mv1, rs1 = sb("stat1", [P, B, 6]), sb("mv1", [P, B, 2]), sb("rs1", [P, B])
        shift1, shift2 = sb("shift1", [P, B]), sb("shift2", [P, B])
        stat2, mv2, rs2 = sb("stat2", [P, B, 6]), sb("mv2", [P, B, 2]), sb("rs2", [P, B])
        x2 = sb("x2", [P, B, C])
        xt2 = sb("xt2", [P, B, KT, P])
        logit = sb("logit", [P, B, E])
        top, top_id = sb("top", [P, B, 8]), sb("top_id", [P, B, 8], U32)
        top_f = sb("top_f", [P, B, 2])
        hot = sb("hot", [P, 2, B, E])
        chose = sb("chose", [P, B, E], BF16)
        counts_m = sb("counts_m", [P, E], BF16)
        newly = sb("newly", [P, E])
        rank = sb("rank", [P, B, E])
        hot_rank = sb("hot_rank", [P, 2, B, E])
        place_f = sb("place_f", [P, 2, B])
        place = sb("place", [P, 2, 2, B], I32)
        gap, gap_exp, gap_den = sb("gap", [P, B]), sb("gap_exp", [P, B]), sb("gap_den", [P, B])
        record = sb("record", [P, 2, 2, B, 2], I32)

        tile_id = sb("tile_id", [P, TILES])
        count_i, tiles_i = sb("count_i", [P, E], I32), sb("tiles_i", [P, E], I32)
        n_tiles, ends = sb("n_tiles", [P, E]), sb("ends", [P, E])
        past, picked = sb("past", [P, TILES, E]), sb("picked", [P, TILES, E])
        passed, starts, first = sb("passed", [P, TILES]), sb("starts", [P, TILES]), sb("first", [P, TILES])
        expert, expert_i = sb("expert", [P, TILES]), sb("expert_i", [P, TILES], I32)

        ps_xt = ps("ps_xt", [P, B * KT * P])
        ps_small = ps("ps_small", [P, HALF])
        ps_pw = ps("ps_pw", [P, 2 * B * P])
        ps_a = ps("ps_a", [P, B * P])
        ps_out = ps("ps_out", [P, B * C])
        ps_prod = ps_small[:, 0:B * NP].rearrange("p (b n) -> p b n", b=B)
        ps_logit = ps_small[:, 64:64 + B * E].rearrange("p (b n) -> p b n", b=B)
        ps_rank = ps_a[:, 0:B * E]
        ps_count = ps_small[:, 0:E]

        def sems(names):
            return [sem("b_" + n) for n in names.split()]

        consts, set0, setup, vset = sems("consts set0 setup vset")
        biases_in, counted, table_step = sems("biases_in counted table_step")
        stat1_d, mv1_d, xn_d, prod_d, pmax_d, prel_d, psum_d, prec_d, pw_d = sems(
            "stat1 mv1 xn prod prod_max prod_rel prod_sum prod_recip prod_w")
        attn_d, tok_d, state_d, stat2_d, mv2_d, x2_d, logit_d, top_d, topid_d = sems(
            "attn tok state stat2 mv2 x2 logit top top_id")
        topf_d, hot_d, chose_d, newly_d, count_d, rank_d, hotrank_d, placef_d, place_d = sems(
            "top_f hot chose newly count rank hot_rank place_f place")
        gap_d, den_d, share_d, record_d, tokid_d = sems("gap gap_den share record token_id")
        xt1_d, pexp_d, pw_turned_d, xt2_d, gexp_d = sems("xt1 prod_exp turned_pw xt2 gap_exp")
        var1_d, rs1_d, shift1_d, var2_d, rs2_d, shift2_d = sems("var1 rs1 shift1 var2 rs2 shift2")
        t1_mm, prod_mm, pw_mm, a_mm, state_mm, out_mm, t2_mm, logit_mm, rank_mm = sems(
            "t1_mm prod_mm pw_mm a_mm state_mm out_mm t2_mm logit_mm rank_mm")
        tok_out, x2_out, cleared = sems("tok_out x2_out cleared")
        record_out = sems("record_out0 record_out1")
        CH = IT

        def exists(c):
            return not isinstance(c, int) or 0 <= c < CH

        def steps(eng, body):
            for i in range(-3, 1):
                body(i, i % 2)
            with eng.Fori(0, CH // 2 - 2) as k:
                for j in range(2):
                    body(k * 2 + (1 + j), 1 - j)
            for i in range(CH - 3, CH + 1):
                body(i, i % 2)

        def tiles(c):
            return tok[:, :, :].rearrange("p (b c) d -> p b c d", b=B)[:, :, bass.ds(c, 1), :].rearrange("p b a d -> p b (a d)")

        block = ctx.enter_context(nc.Block())
        out_v = out[0:TOK, :].rearrange("(b c p) d -> c p b d", b=B, p=P)
        normed_v = normed[0:TOK, :].rearrange("(b c p) d -> c p b d", b=B, p=P)

        @block.sync
        def _(sp):
            sp.dma_start(proxy[:, :, :], proxy_t.rearrange("(k p) n -> p k n", p=P)).then_inc(consts, 16)
            sp.dma_start(gate[:, :, :], gate_t.rearrange("(k p) n -> p k n", p=P)).then_inc(consts, 16)
            sp.dma_start(bias1[:, :, :], b1_t).then_inc(biases_in, 16)
            sp.dma_start(bias2[:, :, :].rearrange("p e c -> p (e c)"),
                         b2.rearrange("e c -> (e c)").partition_broadcast(P)).then_inc(biases_in, 16)
            sp.wait_ge(vset, 3)
            sp.dma_start(normed[TOK:TOK + P, :], x2[:, 0, :]).then_inc(x2_out, 16)

            def body(i, par):
                if exists(i):
                    wait_apart(sp, x2_d, done(i))
                    sp.dma_start(normed_v[bass.ds(i, 1)].rearrange("a p b d -> p (a b) d"), x2[:, :, :]).then_inc(x2_out, 16)
                near = i + 1
                if exists(near):
                    wait_apart(sp, tok_d, done(near))
                    sp.dma_start(out_v[bass.ds(near, 1)].rearrange("a p b d -> p (a b) d"),
                                 tiles(near)).then_inc(tok_out, 16)

            steps(sp, body)
            sp.wait_ge(tok_out, 16 * CH)
            sp.wait_ge(x2_out, 16 * (CH + 1))
            sp.wait_ge(biases_in, 32)

        @block.gpsimd
        def _(pool):
            for s in (var1_d, rs1_d, shift1_d, var2_d, rs2_d, shift2_d):
                pool.sem_inc(s, CREDIT)
            pool.memset(causal[:, :], 1.0).then_inc(set0, 1)
            pool.memset(before[:, :], 1.0).then_inc(set0, 1)
            pool.memset(ones[:, :], 1.0).then_inc(setup, 1)
            pool.memset(minus_half[:, :], -0.5).then_inc(setup, 1)
            pool.memset(minus_one[:, :], -1.0).then_inc(setup, 1)
            pool.memset(eps[:, :], LN_EPS).then_inc(setup, 1)
            pool.iota(expert_id[:, :], pattern=[[1, E]], base=0, channel_multiplier=0,
                      allow_small_or_imprecise_dtypes=True).then_inc(setup, 1)
            pool.iota(tile_id[:, :], pattern=[[1, TILES]], base=0, channel_multiplier=0,
                      allow_small_or_imprecise_dtypes=True).then_inc(setup, 1)
            pool.iota(place0[:, :], pattern=[[CAP, E]], base=0, channel_multiplier=0,
                      allow_small_or_imprecise_dtypes=True).then_inc(setup, 1)
            pool.iota(token_id[:, :], pattern=[[N, B]], base=0, channel_multiplier=1,
                      allow_small_or_imprecise_dtypes=True).then_inc(setup, 1)
            pool.iota(no_token[:, :, 0], pattern=[[0, SLOTS // P // P], [1, P]], base=TOK,
                      channel_multiplier=0).then_inc(setup, 1)
            pool.memset(no_token[:, :, 1], 0).then_inc(setup, 1)
            pool.wait_ge(set0, 2)
            pool.affine_select(out=causal[:, :], in_=causal[:, :], compare_op=ALU.is_ge, fill=0.0, base=0,
                               pattern=[[1, P]], channel_multiplier=-1).then_inc(setup, 1)
            pool.affine_select(out=before[:, :], in_=before[:, :], compare_op=ALU.is_gt, fill=0.0, base=0,
                               pattern=[[1, P]], channel_multiplier=-1).then_inc(setup, 1)

            def scale_and_shift(mv_d, mv, var_d, rs_d, rs, shift_d, shift, applied, c):
                pool.wait_ge(mv_d, done(c))
                pool.wait_ge(applied, done(c - 1))
                pool.tensor_tensor(shift[:, :], mv[:, :, 0], minus_one[:, :], ALU.mult)
                pool.tensor_tensor(rs[:, :], mv[:, :, 1], eps[:, :], ALU.add).then_inc(var_d, 1)
                pool.wait_ge(var_d, done(c))
                pool.tensor_tensor(rs[:, :], rs[:, :], minus_half[:, :], ALU.pow).then_inc(rs_d, 1)
                pool.wait_ge(rs_d, done(c))
                pool.tensor_tensor(shift[:, :], shift[:, :], rs[:, :], ALU.mult).then_inc(shift_d, 1)

            def scatter(c, par):
                wait_apart(pool, record_d, done(c))
                for k, b in [(k, b) for k in range(2) for b in range(B)]:
                    pool.indirect_dma_start(
                        out=places, out_offset=bass.IndirectOffsetOnAxis(ap=place[:, par, k, b:b + 1], axis=0),
                        in_=record[:, par, k, b, :], in_offset=None).then_inc(record_out[par], 16)

            def body(i, par):
                if exists(i):
                    scale_and_shift(mv2_d, mv2, var2_d, rs2_d, rs2, shift2_d, shift2, x2_d, i)
                if exists(i + 3):
                    scale_and_shift(mv1_d, mv1, var1_d, rs1_d, rs1, shift1_d, shift1, xn_d, i + 3)
                if exists(i - 1):
                    scatter(i - 1, 1 - par)

            pool.wait_ge(setup, 12)
            pool.dma_start(places.rearrange("(p g) r -> p (g r)", p=P),
                           no_token[:, :, :].rearrange("p g r -> p (g r)")).then_inc(cleared, 16)
            pool.wait_ge(cleared, 16)
            steps(pool, body)
            for par in range(2):
                pool.wait_ge(record_out[par], 16 * B * CH)

        @block.scalar
        def _(act):
            for s in (xn_d, x2_d, xt1_d, pexp_d, pw_turned_d, xt2_d, gexp_d):
                act.sem_inc(s, CREDIT)

            def evacuate_turned(c, dst, ready, turned, read):
                act.wait_ge(turned, done(c))
                act.wait_ge(read, done(c - 1))
                act.activation(dst[:, :, :, :], ps_xt[:, :].rearrange("p (b k t) -> p b k t", b=B, k=KT),
                               ACT.Copy).then_inc(ready, 1)

            def normalise(c, dst, rs, shift, shift_d, ready):
                act.wait_ge(shift_d, done(c))
                for b in range(B):
                    last = act.activation(dst[:, b, :], tiles(c)[:, b, :], ACT.Identity, bias=shift[:, b:b + 1],
                                          scale=rs[:, b:b + 1])
                last.then_inc(ready, 1)

            def body(i, par):
                far, new = i + 2, i + 3
                if exists(far):
                    evacuate_turned(far, xt1, xt1_d, t1_mm, prod_mm)
                if exists(i):
                    act.wait_ge(x2_out, (i + 1) * 16)
                    act.wait_ge(t2_mm, done(i - 1))
                    normalise(i, x2, rs2, shift2, shift2_d, x2_d)
                if exists(i - 1):
                    act.wait_ge(gap_d, done(i - 1))
                    act.activation(gap_exp[:, :], gap[:, :], ACT.Exp).then_inc(gexp_d, 1)
                if exists(far):
                    act.wait_ge(prel_d, done(far))
                    act.activation(prod_rel[:, :, :], prod_rel[:, :, :], ACT.Exp, scale=float(NP) ** -0.5).then_inc(pexp_d, 1)
                if exists(i):
                    evacuate_turned(i, xt2, xt2_d, t2_mm, logit_mm)
                if exists(new):
                    act.wait_ge(out_mm, done(new - 2))
                    normalise(new, xn[:, 1 - par], rs1, shift1, shift1_d, xn_d)
                if exists(far):
                    act.wait_ge(pw_mm, done(far))
                    act.wait_ge(out_mm, done(far - 2))
                    act.activation(turned_pw[:, par], ps_pw[0:NP, :].rearrange("p (b t) -> p b t", b=2 * B),
                                   ACT.Copy).then_inc(pw_turned_d, 1)

            steps(act, body)

        @block.vector
        def _(dve):
            for s in (stat1_d, mv1_d, prod_d, pmax_d, prel_d, psum_d, prec_d, pw_d, attn_d, tok_d, state_d,
                      stat2_d, mv2_d, logit_d, top_d, topid_d, topf_d, hot_d, chose_d, newly_d, count_d, rank_d,
                      hotrank_d, placef_d, place_d, gap_d, den_d, share_d, record_d, tokid_d):
                dve.sem_inc(s, CREDIT)
            dve.memset(state[:, 0], 0.0).then_inc(vset, 1)
            dve.memset(x2[:, 0, :], 0.0).then_inc(vset, 1)
            dve.memset(counts_m[:, :], 0.0).then_inc(vset, 1)
            dve.wait_ge(setup, 12)

            def tiles_of(c):
                return [tiles(c)[:, b, :] for b in range(B)]

            def stats(c, stat, stat_d, mv, mv_d, rs_d):
                wait_apart(dve, rs_d, done(c - 1))
                for b, t in enumerate(tiles_of(c)):
                    last = dve.bn_stats(stat[:, b, :], t)
                last.then_inc(stat_d, 1)
                wait_apart(dve, stat_d, done(c))
                for b in range(B):
                    last = dve.bn_aggr(mv[:, b, :], stat[:, b, :])
                last.then_inc(mv_d, 1)

            def wide(small):
                return small.unsqueeze(2).to_broadcast([P, B, NP])

            def proxy_softmax_in(c, par):
                dve.wait_ge(prod_mm, done(c))
                dve.wait_ge(state_mm, done(c - 2))
                dve.tensor_copy(prod[:, par], ps_prod).then_inc(prod_d, 1)
                dve.tensor_reduce(prod_max[:, :], ps_prod, AX.X, ALU.max).then_inc(pmax_d, 1)
                dve.wait_ge(prod_d, done(c))
                dve.wait_ge(pmax_d, done(c))
                dve.tensor_tensor(prod_rel[:, :, :], prod[:, par], wide(prod_max[:, :]), ALU.subtract).then_inc(prel_d, 1)

            def proxy_softmax_out(c):
                dve.wait_ge(pexp_d, done(c))
                dve.tensor_reduce(prod_sum[:, :], prod_rel[:, :, :], AX.X, ALU.add).then_inc(psum_d, 1)
                dve.wait_ge(psum_d, done(c))
                dve.reciprocal(prod_sum[:, :], prod_sum[:, :]).then_inc(prec_d, 1)
                dve.wait_ge(prec_d, done(c))
                dve.wait_ge(pw_mm, done(c - 1))
                dve.tensor_tensor(prod_w[:, :, :], prod_rel[:, :, :], wide(prod_sum[:, :]), ALU.mult).then_inc(pw_d, 1)

            def mask(c):
                dve.wait_ge(a_mm, done(c))
                dve.tensor_tensor(attn[:, :, :], ps_a[:, :].rearrange("p (b t) -> p b t", b=B),
                                  causal[:, :].unsqueeze(1).to_broadcast([P, B, P]), ALU.mult).then_inc(attn_d, 1)

            def grow_state(c, par):
                dve.wait_ge(state_mm, done(c))
                dve.wait_ge(out_mm, done(c - 1))
                dve.tensor_tensor(state[:, 1 - par], ps_pw[0:NP, :].rearrange("p (b d) -> p b d", b=B), state[:, par],
                                  ALU.add).then_inc(state_d, 1)

            def add_out(c):
                dve.wait_ge(out_mm, done(c))
                dve.tensor_tensor(tiles(c), ps_out[:, :].rearrange("p (b d) -> p b d", b=B), tiles(c),
                                  ALU.add).then_inc(tok_d, 1)

            def choose(c):
                dve.wait_ge(logit_mm, done(c))
                dve.tensor_copy(logit[:, :, :], ps_logit).then_inc(logit_d, 1)
                wait_apart(dve, logit_d, done(c))
                for b in range(B):
                    last = dve.max(top[:, b, :], logit[:, b, :])
                last.then_inc(top_d, 1)
                dve.wait_ge(top_d, done(c))
                dve.tensor_tensor(gap[:, :], top[:, :, 1], top[:, :, 0], ALU.subtract).then_inc(gap_d, 1)
                for b in range(B):
                    last = dve.max_index(top_id[:, b, :], top[:, b, :], logit[:, b, :])
                last.then_inc(topid_d, 1)

            def mark(c):
                dve.wait_ge(topid_d, done(c))
                dve.tensor_copy(top_f[:, :, :], top_id[:, :, 0:2]).then_inc(topf_d, 1)
                dve.wait_ge(topf_d, done(c))
                for k in range(2):
                    last = dve.tensor_tensor(hot[:, k], expert_id[:, :].unsqueeze(1).to_broadcast([P, B, E]),
                                             top_f[:, :, k:k + 1].to_broadcast([P, B, E]), ALU.is_equal)
                last.then_inc(hot_d, 1)
                dve.wait_ge(hot_d, done(c))
                dve.wait_ge(rank_mm, done(c - 1))
                dve.wait_ge(newly_d, done(c - 1))
                dve.tensor_tensor(chose[:, :, :], hot[:, 0], hot[:, 1], ALU.add).then_inc(chose_d, 1)

            def find_places(c, par):
                dve.wait_ge(rank_mm, done(c))
                dve.tensor_tensor(rank[:, :, :], ps_rank.rearrange("p (b e) -> p b e", b=B),
                                  place0[:, :].unsqueeze(1).to_broadcast([P, B, E]), ALU.add).then_inc(rank_d, 1)
                dve.wait_ge(rank_d, done(c))
                for k in range(2):
                    last = dve.tensor_tensor(hot_rank[:, k], hot[:, k], rank[:, :, :], ALU.mult)
                last.then_inc(hotrank_d, 1)
                dve.tensor_reduce(newly[:, :], chose[:, :, :].rearrange("p b e -> p e b"), AX.X, ALU.add).then_inc(newly_d, 1)
                dve.wait_ge(newly_d, done(c))
                dve.tensor_tensor(counts_m[:, :], counts_m[:, :], newly[:, :], ALU.add).then_inc(count_d, 1)
                dve.wait_ge(gexp_d, done(c))
                dve.tensor_scalar(gap_den[:, :], gap_exp[:, :], 1.0, None, ALU.add).then_inc(den_d, 1)
                dve.wait_ge(hotrank_d, done(c))
                dve.tensor_reduce(place_f[:, :, :], hot_rank[:, :, :, :], AX.X, ALU.add).then_inc(placef_d, 1)
                if exists(c - 2):
                    dve.wait_ge(record_out[par], (c - par) * (B * 16))
                dve.wait_ge(den_d, done(c))
                dve.reciprocal(record[:, par, 0, :, 1].bitcast(F32), gap_den[:, :]).then_inc(share_d, 1)
                dve.wait_ge(placef_d, done(c))
                dve.tensor_copy(place[:, par], place_f[:, :, :]).then_inc(place_d, 1)
                for k in range(2):
                    last = dve.tensor_copy(record[:, par, k, :, 0], token_id[:, :])
                last.then_inc(place_d, 1)
                dve.wait_ge(share_d, done(c))
                dve.wait_ge(place_d, c * 2 + (CREDIT + 2))
                dve.tensor_scalar(token_id[:, :], token_id[:, :], float(P), None, ALU.add).then_inc(tokid_d, 1)
                dve.tensor_tensor(record[:, par, 1, :, 1].bitcast(F32), gap_exp[:, :], record[:, par, 0, :, 1].bitcast(F32),
                                  ALU.mult).then_inc(record_d, 1)
                dve.wait_ge(tokid_d, done(c))

            def body(i, par):
                near, far, new = i + 1, i + 2, i + 3
                if exists(near):
                    mask(near)
                if exists(new):
                    stats(new, stat1, stat1_d, mv1, mv1_d, rs1_d)
                if exists(i - 1):
                    find_places(i - 1, 1 - par)
                if exists(near):
                    grow_state(near, 1 - par)
                if exists(far):
                    proxy_softmax_in(far, par)
                    proxy_softmax_out(far)
                if exists(near):
                    add_out(near)
                    dve.wait_ge(tok_d, done(near))
                    stats(near, stat2, stat2_d, mv2, mv2_d, rs2_d)
                if exists(i):
                    choose(i)
                    mark(i)

            def make_table():
                n = 0

                def then(instruction):
                    nonlocal n
                    n += 1
                    instruction.then_inc(table_step, 1)
                    dve.wait_ge(table_step, n)

                def per_tile(x):
                    return x.unsqueeze(1).to_broadcast([P, TILES, E])

                dve.wait_ge(counted, 1)
                then(dve.tensor_scalar(count_i[:, :], ps_count, float(P - 1), None, ALU.add))
                then(dve.tensor_scalar(tiles_i[:, :], count_i[:, :], P.bit_length() - 1, None, ALU.arith_shift_right))
                then(dve.tensor_scalar(n_tiles[:, :], tiles_i[:, :], 1.0, None, ALU.max))
                then(dve.tensor_tensor_scan(ends[:, :], ones[:, 0:E], n_tiles[:, :], 0.0, ALU.mult, ALU.add))
                then(dve.tensor_tensor(past[:, :, :], tile_id[:, :].unsqueeze(2).to_broadcast([P, TILES, E]),
                                       per_tile(ends[:, :]), ALU.is_ge))
                then(dve.tensor_reduce(passed[:, :], past[:, :, :], AX.X, ALU.add))
                then(dve.tensor_tensor(picked[:, :, :], past[:, :, :], per_tile(n_tiles[:, :]), ALU.mult))
                then(dve.tensor_reduce(starts[:, :], picked[:, :, :], AX.X, ALU.add))
                then(dve.tensor_tensor(starts[:, :], tile_id[:, :], starts[:, :], ALU.subtract))
                then(dve.scalar_tensor_tensor(out=tabs[:, T_PLACE, :], in0=passed[:, :], scalar=float(CAP // P),
                                              in1=starts[:, :], op0=ALU.mult, op1=ALU.add))
                then(dve.tensor_scalar(expert[:, :], passed[:, :], float(E - 1), None, ALU.min))
                dve.tensor_copy(tabs[:, T_EXPERT, :], expert[:, :])
                dve.tensor_scalar(tabs[:, T_NEXT, :], expert[:, :], 1.0, float(E - 1), ALU.add, ALU.min)
                dve.memset(tabs[:, T_FIRST, 0:1], 0)
                dve.tensor_tensor(first[:, 1:TILES], expert[:, 1:TILES], expert[:, 0:TILES - 1], ALU.is_gt)
                then(dve.tensor_copy(expert_i[:, :], expert[:, :]))
                dve.tensor_scalar(tabs[:, T_BUFFER, :], expert_i[:, :], 1, None, ALU.bitwise_and)
                then(dve.scalar_tensor_tensor(out=tabs[:, T_FIRST, 1:TILES], in0=expert[:, 1:TILES], scalar=float(E - 1),
                                              in1=first[:, 1:TILES], op0=ALU.is_lt, op1=ALU.mult))

            dve.wait_ge(vset, 3)
            steps(dve, body)
            make_table()

        @block.tensor
        def _(pe):
            for s in (t1_mm, prod_mm, pw_mm, a_mm, state_mm, out_mm, t2_mm, logit_mm, rank_mm):
                pe.sem_inc(s, CREDIT)
            pe.wait_ge(consts, 32)
            pe.wait_ge(setup, 12)

            def turn(src, ready):
                for b in range(B):
                    for k in range(KT):
                        last = pe.transpose(ps_xt[:, (b * KT + k) * P:(b * KT + k + 1) * P], src[:, b, k * P:(k + 1) * P],
                                            ident[:, :])
                last.then_inc(ready, 1)

            def project(dst, x, w, n, ready):
                for b in range(B):
                    for k in range(KT):
                        last = pe.matmul(dst[:, b, :], x[:, b, k, :], w[:, k, :], start=k == 0, stop=k == KT - 1)
                last.then_inc(ready, 1)

            def attend(c, par):
                pe.wait_ge(pw_turned_d, done(c))
                pe.wait_ge(rank_d, done(c - 3))
                for b in range(B):
                    last = pe.matmul(ps_a[:, b * P:(b + 1) * P], turned_pw[:, par, b, :], turned_pw[:, par, B + b, :],
                                     start=True, stop=True)
                last.then_inc(a_mm, 1)
                for b in range(B):
                    last = pe.matmul(ps_pw[0:NP, b * C:(b + 1) * C], prod[:, par, b, :], xn[:, par, b, :],
                                     start=True, stop=True)
                last.then_inc(state_mm, 1)

            def output(c, par):
                pe.wait_ge(attn_d, done(c))
                pe.wait_ge(tok_d, done(c - 1))
                pe.wait_ge(state_d, done(c - 1))
                for b in range(B):
                    dst = ps_out[:, b * C:(b + 1) * C]
                    pe.matmul(dst, attn[:, b, :], xn[:, par, b, :], start=True, stop=False)
                    last = pe.matmul(dst, turned_pw[:, par, B + b, :], state[:, par, b, :], start=False, stop=True)
                last.then_inc(out_mm, 1)

            def turn_products(c, par):
                pe.wait_ge(pw_d, done(c))
                pe.wait_ge(state_d, done(c - 1))
                for j, src in enumerate((prod[:, par], prod_w)):
                    for b in range(B):
                        at = (j * B + b) * P
                        last = pe.transpose(ps_pw[0:NP, at:at + P], src[:, b, :], ident[:, :])
                last.then_inc(pw_mm, 1)

            def rank_choices(c):
                pe.wait_ge(chose_d, done(c))
                pe.wait_ge(count_d, done(c - 1))
                if exists(c + 2):
                    pe.wait_ge(attn_d, done(c + 2))
                pe.matmul(ps_rank, before[:, :], chose[:, :, :].rearrange("p b e -> p (b e)"), start=True, stop=False)
                for d in range(1, B):
                    pe.matmul(ps_rank[:, d * E:B * E], ones[:, :], chose[:, 0:B - d, :].rearrange("p b e -> p (b e)"),
                              start=False, stop=False)
                for b in range(B):
                    last = pe.matmul(ps_rank[:, b * E:(b + 1) * E], ones[:, :], counts_m[:, :], start=False, stop=b == B - 1)
                last.then_inc(rank_mm, 1)

            def body(i, par):
                near, far = i + 1, i + 2
                if exists(far):
                    pe.wait_ge(xn_d, done(far))
                    pe.wait_ge(xt2_d, done(i - 1))
                    turn(xn[:, par], t1_mm)
                if exists(near):
                    attend(near, 1 - par)
                if exists(i - 1):
                    rank_choices(i - 1)
                if exists(far):
                    pe.wait_ge(xt1_d, done(far))
                    pe.wait_ge(logit_d, done(i - 1))
                    project(ps_prod, xt1, proxy, NP, prod_mm)
                if exists(i):
                    pe.wait_ge(x2_d, done(i))
                    if exists(far):
                        pe.wait_ge(xt1_d, done(far))
                    turn(x2, t2_mm)
                if exists(near):
                    output(near, 1 - par)
                if exists(i):
                    pe.wait_ge(xt2_d, done(i))
                    if exists(far):
                        pe.wait_ge(prel_d, done(far))
                    project(ps_logit, xt2, gate, E, logit_mm)
                if exists(far):
                    turn_products(far, par)

            steps(pe, body)
            pe.wait_ge(count_d, done(CH - 1))
            pe.wait_ge(logit_d, done(CH - 1))
            pe.matmul(ps_count, ones[:, :], counts_m[:, :], start=True, stop=True).then_inc(counted, 1)


T_EXPERT, T_PLACE, T_FIRST, T_NEXT, T_BUFFER = range(5)


def stage_d(nc, sem, wbuf, ident, tabs, bias1, bias2, wsplit, normed, places, out):
    with ExitStack() as ctx:
        def sb(name, shape, dt=F32):
            return ctx.enter_context(nc.sbuf_tensor(name, shape, dt))

        def ps(name, shape):
            return ctx.enter_context(nc.psum_tensor(name, shape, F32))

        records = sb("records", [P, TILES, 2], I32)
        from_row, to_row = sb("from_row", [P, 2], I32), sb("to_row", [P, 2], I32)
        x = sb("x_rows", [P, 2, C])
        xth, xtl = sb("xth", [P, 2, KT, P], F32R), sb("xtl", [P, 2, KT, P], F32R)
        h = sb("h", [P, F])
        hb = sb("hb", [P, FT, P])
        g = sb("g", [P, FT, P])
        gh, gl = sb("gh", [P, 2, FT, P], F32R), sb("gl", [P, 2, FT, P], F32R)
        yb, y = sb("yb", [P, C]), sb("y", [P, 2, C])
        ps_x = ps("ps_x", [P, KT * P])
        ps_h = ps("ps_h", [P, F])
        ps_ht = ps("ps_ht", [P, F])
        ps_y = [ps(f"ps_y{i}", [P, HALF]) for i in range(2)]

        record_in = sem("d_record_in")
        w_in = [sem("d_w1_in"), sem("d_w2_in")]
        x_in = [sem("d_x_in0"), sem("d_x_in1")]
        y_out, from_d, to_d = sem("d_y_out"), sem("d_from_row"), sem("d_to_row")
        xt_mm, h_mm, ht_mm, y_mm = sem("d_xt_mm"), sem("d_h_mm"), sem("d_ht_mm"), sem("d_y_mm")
        xh_d, h_d, g_d = sem("d_x_high"), sem("d_h"), sem("d_g")
        xl_d, hb_d, gh_d, gl_d, yb_d, y_d = (sem("d_" + n) for n in ("x_low", "hb", "g_high", "g_low", "yb", "y"))
        AHEAD = 4

        def steps(eng, body, first, last):
            lo, hi = max(first, 4), TILES - 1 - AHEAD
            hi -= (hi - lo) % 2
            for u in range(first, lo):
                body(u, u % 2)
            with eng.Fori(0, (hi - lo) // 2) as k:
                for i in range(2):
                    body(k * 2 + (lo + i), (lo + i) % 2)
            for u in range(hi, last + 1):
                body(u, u % 2)

        def exists(u):
            return not isinstance(u, int) or 0 <= u < TILES

        def later(u, step):
            return not isinstance(u, int) or u >= step

        def entry(eng, row, u, top):
            return eng.value_load(tabs[0:1, row, bass.ds(u, 1)], min_val=0, max_val=top)

        def half(u, par):
            return u // 2 if isinstance(u, int) else (u - par) // 2

        block = ctx.enter_context(nc.Block())

        @block.sync
        def _(sp):
            def load_record(u):
                if u is not None:
                    at = entry(sp, T_PLACE, u, SLOTS // P - 1)
                    sp.dma_start(records[:, bass.ds(u, 1), :].rearrange("p a r -> p (a r)"),
                                 places.rearrange("(t p) r -> t p r", p=P)[bass.ds(at, 1)].rearrange("a p r -> (a p) r")
                                 ).then_inc(record_in, 16)

            def load_weights(part, expert, buffer, cond=None):
                at = slice(part * W2AT, (part + 1) * W2AT)
                sp.dma_start(wbuf[:, bass.ds(buffer, 1), at].rearrange("p a w -> p (a w)").bitcast(F32),
                             wsplit[bass.ds(expert, 1)].rearrange("a p w -> (a p) w")[:, at],
                             **({} if cond is None else {"cond": cond})).then_inc(w_in[part], 16)

            load_record(0)
            for u in range(1, AHEAD):
                sp.wait_ge(record_in, 16 * u)
                load_record(u)
            def body(u, par):
                if exists(u + AHEAD):
                    wait_apart(sp, record_in, (u + AHEAD) * 16)
                    load_record(u + AHEAD)
                for part, used in enumerate((h_mm, y_mm)):
                    t = u - 2 * part
                    if not exists(t) or (isinstance(t, int) and t > TILES - 2):
                        continue
                    first = entry(sp, T_FIRST, t, 1)
                    nxt = entry(sp, T_NEXT, t, E - 1)
                    buffer = entry(sp, T_BUFFER, t, 1)
                    wait_apart(sp, used, done(t - 1))
                    if later(t, 1):
                        wait_apart(sp, w_in[part], t * 16)
                    load_weights(part, nxt, 1 - buffer, cond=first)

            steps(sp, body, 0, TILES)
            for part in range(2):
                sp.wait_ge(w_in[part], (TILES - 1) * 16)

        @block.gpsimd
        def _(pool):
            for s in (from_d, to_d):
                pool.sem_inc(s, CREDIT)

            def gather(u, par):
                if later(u, 2):
                    wait_apart(pool, x_in[par], half(u, par) * 16)
                wait_apart(pool, record_in, (u + 1) * 16)
                pool.tensor_copy(from_row[:, par:par + 1], records[:, bass.ds(u, 1), 0]).then_inc(from_d, 1)
                wait_apart(pool, xt_mm, done(u - 2))
                wait_apart(pool, from_d, done(u))
                pool.indirect_dma_start(out=x[:, par, :], out_offset=None, in_=normed,
                                        in_offset=bass.IndirectOffsetOnAxis(ap=from_row[:, par:par + 1], axis=0)
                                        ).then_inc(x_in[par], 16)

            def scatter(u, par):
                if later(u, 1):
                    wait_apart(pool, y_out, u * 16)
                pool.tensor_copy(to_row[:, par:par + 1], records[:, bass.ds(u, 1), 0]).then_inc(to_d, 1)
                wait_apart(pool, y_d, done(u))
                wait_apart(pool, to_d, done(u))
                pool.indirect_dma_start(out=out, out_offset=bass.IndirectOffsetOnAxis(ap=to_row[:, par:par + 1], axis=0),
                                        in_=y[:, par, :], in_offset=None, compute_op=ALU.add).then_inc(y_out, 16)

            def body(u, par):
                if exists(u + 3):
                    gather(u + 3, 1 - par)
                if exists(u - 2):
                    scatter(u - 2, par)

            for u in range(3):
                gather(u, u % 2)
            steps(pool, body, 0, TILES + 1)
            pool.wait_ge(y_out, TILES * 16)

        @block.scalar
        def _(act):
            for s in (xh_d, h_d, g_d):
                act.sem_inc(s, CREDIT)

            def x_high(u, par):
                act.wait_ge(xt_mm, done(u))
                act.wait_ge(h_mm, done(u - 2))
                act.activation(xth[:, par], ps_x[:, :].rearrange("p (k t) -> p k t", k=KT), ACT.Copy).then_inc(xh_d, 1)

            def body(u, par):
                if exists(u):
                    act.wait_ge(h_mm, done(u))
                    act.wait_ge(ht_mm, done(u - 1))
                    act.activation(h[:, :], ps_h[:, :], ACT.Copy).then_inc(h_d, 1)
                if exists(u + 2):
                    x_high(u + 2, par)
                if exists(u):
                    act.wait_ge(hb_d, done(u))
                    act.wait_ge(gl_d, done(u - 1))
                    act.activation(g[:, :, :], hb[:, :, :], ACT.Gelu_apprx_tanh).then_inc(g_d, 1)

            x_high(0, 0)
            x_high(1, 1)
            steps(act, body, 0, TILES - 1)

        @block.vector
        def _(dve):
            for s in (xl_d, hb_d, gh_d, gl_d, yb_d, y_d):
                dve.sem_inc(s, CREDIT)

            def x_low(u, par):
                dve.wait_ge(xh_d, done(u))
                dve.tensor_tensor(xtl[:, par], ps_x[:, :].rearrange("p (k t) -> p k t", k=KT), xth[:, par].bitcast(F32),
                                  ALU.subtract).then_inc(xl_d, 1)

            def result(u, par):
                e = entry(dve, T_EXPERT, u, E - 1)
                dve.wait_ge(y_mm, done(u))
                dve.wait_ge(y_d, done(u - 1))
                dve.tensor_tensor(yb[:, :], ps_y[par][:, 0:C], bias2[:, bass.ds(e, 1), :].rearrange("p a c -> p (a c)"),
                                  ALU.add).then_inc(yb_d, 1)
                if exists(u - 2):
                    dve.wait_ge(y_out, (u - 1) * 16)
                dve.wait_ge(yb_d, done(u))
                share = records[:, bass.ds(u, 1), 1].bitcast(F32)
                dve.tensor_scalar(y[:, par, :], yb[:, :], share, None, ALU.mult).then_inc(y_d, 1)

            def body(u, par):
                if exists(u - 2):
                    result(u - 2, par)
                if exists(u):
                    e = entry(dve, T_EXPERT, u, E - 1)
                    dve.wait_ge(ht_mm, done(u))
                    dve.wait_ge(g_d, done(u - 1))
                    bias = bias1[:, bass.ds(e, 1), :].rearrange("p a f -> p (a f)").unsqueeze(2).to_broadcast([P, FT, P])
                    dve.tensor_tensor(hb[:, :, :], ps_ht[:, :].rearrange("p (f t) -> p f t", f=FT), bias,
                                      ALU.add).then_inc(hb_d, 1)
                if exists(u + 2):
                    x_low(u + 2, par)
                if exists(u):
                    dve.wait_ge(g_d, done(u))
                    dve.wait_ge(y_mm, done(u - 2))
                    dve.tensor_copy(gh[:, par], g[:, :, :]).then_inc(gh_d, 1)
                    dve.wait_ge(gh_d, done(u))
                    dve.tensor_tensor(gl[:, par], g[:, :, :], gh[:, par].bitcast(F32), ALU.subtract).then_inc(gl_d, 1)

            dve.wait_ge(record_in, AHEAD * 16)
            x_low(0, 0)
            x_low(1, 1)
            steps(dve, body, 0, TILES + 1)

        @block.tensor
        def _(pe):
            for s in (xt_mm, h_mm, ht_mm, y_mm):
                pe.sem_inc(s, CREDIT)

            def turn_x(u, par):
                pe.wait_ge(x_in[par], (half(u, par) + 1) * 16)
                pe.wait_ge(xl_d, done(u - 1))
                for k in range(KT):
                    last = pe.transpose(ps_x[:, k * P:(k + 1) * P], x[:, par, k * P:(k + 1) * P], ident[:, :])
                last.then_inc(xt_mm, 1)

            def weights(u, part):
                buffer = entry(pe, T_BUFFER, u, 1)
                both = wbuf[:, bass.ds(buffer, 1), part * W2AT:(part + 1) * W2AT].rearrange("p a w -> p (a w)")
                rows = (KT, FT)[part]
                return [both[:, i * W2AT // 2:(i + 1) * W2AT // 2].rearrange("p (k n) -> p k n", k=rows) for i in range(2)]

            def layer1(u, par):
                wh, wl = weights(u, 0)
                if later(u, 1):
                    pe.wait_ge(w_in[0], u * 16)
                pe.wait_ge(xl_d, done(u))
                pe.wait_ge(h_d, done(u - 1))
                for n in range(F // HALF):
                    cols = slice(n * HALF, (n + 1) * HALF)
                    for k in range(KT):
                        last = mm3(pe, ps_h[:, cols], (xth[:, par, k], xtl[:, par, k]), (wh[:, k, cols], wl[:, k, cols]),
                                   HALF, k == 0, k == KT - 1)
                last.then_inc(h_mm, 1)

            def turn_h(u):
                pe.wait_ge(h_d, done(u))
                pe.wait_ge(hb_d, done(u - 1))
                for f in range(FT):
                    last = pe.transpose(ps_ht[:, f * P:(f + 1) * P], h[:, f * P:(f + 1) * P], ident[:, :])
                last.then_inc(ht_mm, 1)

            def layer2(u, par):
                wh, wl = weights(u, 1)
                if later(u, 1):
                    pe.wait_ge(w_in[1], u * 16)
                pe.wait_ge(gl_d, done(u))
                pe.wait_ge(yb_d, done(u - 2))
                for f in range(FT):
                    last = mm3(pe, ps_y[par][:, 0:C], (gh[:, par, f], gl[:, par, f]), (wh[:, f], wl[:, f]), C,
                               f == 0, f == FT - 1)
                last.then_inc(y_mm, 1)

            def body(u, par):
                if exists(u):
                    layer1(u, par)
                if exists(u - 2):
                    layer2(u - 2, par)
                if exists(u):
                    turn_h(u)
                if exists(u + 2):
                    turn_x(u + 2, par)

            turn_x(0, 0)
            turn_x(1, 1)
            steps(pe, body, 0, TILES + 1)


INPUTS = ["x_ch", "x_tok", "wqk3", "bqk3", "wv_t", "bv", "alpha", "proxy_t", "gate_t", "w1", "b1_t", "w2", "b2"]


def kernel(x, L0_conv_Wq, L0_conv_bq, L0_conv_Wk, L0_conv_bk, L0_conv_Wv, L0_conv_bv, L0_conv_alpha,
           L1_attn_proxy, L1_ffn_gate_w, L1_ffn_w1, L1_ffn_b1, L1_ffn_w2, L1_ffn_b2):
    import numpy as np
    import concourse.bacc as bacc
    from concourse.bass_utils import run_bass_kernel_spmd

    flat = np.asarray(x).reshape(B, C, N)
    wq, wk, wv = (np.asarray(w) for w in (L0_conv_Wq, L0_conv_Wk, L0_conv_Wv))
    laid = {
        "x_ch": flat,
        "x_tok": flat.transpose(0, 2, 1).reshape(TOK, C),
        "wqk3": np.stack([np.tile(wq.T, (1, 3)), np.tile(wk.T, (1, 3))]),
        "bqk3": np.stack([np.tile(np.asarray(L0_conv_bq), 3), np.tile(np.asarray(L0_conv_bk), 3)], axis=1),
        "wv_t": wv.T,
        "bv": L0_conv_bv,
        "alpha": L0_conv_alpha,
        "proxy_t": np.asarray(L1_attn_proxy).T,
        "gate_t": np.asarray(L1_ffn_gate_w).T,
        "w1": L1_ffn_w1,
        "b1_t": np.asarray(L1_ffn_b1).reshape(E, FT, P).transpose(2, 0, 1),
        "w2": L1_ffn_w2,
        "b2": L1_ffn_b2,
    }
    nc = bacc.Bacc("TRN2", target_bir_lowering=False, num_devices=1)
    arrays, args = {}, []
    for name in INPUTS:
        a = np.ascontiguousarray(laid[name])
        arrays[f"in_{name}"] = a
        args.append(nc.dram_tensor(f"in_{name}", a.shape, mybir.dt.from_np(a.dtype), kind="ExternalInput").ap())
    out = nc.dram_tensor("out_tok", (TOK + P, C), F32, kind="ExternalOutput").ap()
    build(nc, *args, out)
    got = run_bass_kernel_spmd(nc, [arrays], core_ids=[0]).results[0]["out_tok"]
    return np.ascontiguousarray(np.asarray(got)[:TOK].reshape(B, N, C).transpose(0, 2, 1)).reshape(x.shape)
```

```python
from contextlib import ExitStack

import concourse.bass as bass
from concourse import mybir
from concourse.alu_op_type import AluOpType as ALU

F32 = mybir.dt.float32
F32R = mybir.dt.float32r
BF16 = mybir.dt.bfloat16
I32 = mybir.dt.int32
U32 = mybir.dt.uint32
ACT = mybir.ActivationFunctionType
AX = mybir.AxisListType

P = 128
B, C, N = 4, 256, 1024
KT = C // P
IT = N // P
NT = B * IT
TOK = B * N
MID = 32
HALF = 512
NP = 16
E, F = 8, 1024
FT = F // P
CAP = TOK
TILES = 2 * TOK // P + E - 1
USUAL = 2 * TOK // P + E // 2
SLOTS = -(-(E * CAP + E * P) // (P * P)) * P * P
WROW = 2 * KT * F + 2 * FT * C
W2AT = 2 * KT * F
LN_EPS = 1e-5
CREDIT = 2


def done(i):
    return i + (CREDIT + 1)


def wait_apart(eng, sem, value):
    eng.wait_ge(sem, value)
    eng.nop(nofuse=True)


def mm3(eng, out, lhs, rhs, first, last):
    (lh, ll), (rh, rl) = lhs, rhs
    eng.matmul(out, ll, rh, start=first, stop=False)
    eng.matmul(out, lh, rl, start=False, stop=False)
    return eng.matmul(out, lh, rh, start=False, stop=last)


class Fixed:

    def __init__(self, keep):
        self.proxy, self.gate = keep("proxy", [P, KT, NP]), keep("gate", [P, KT, E])
        self.causal = keep("causal", [P, P])
        self.before = keep("before", [P, P], BF16)
        self.ones = keep("ones", [P, P], BF16)
        self.minus_half, self.minus_one = keep("minus_half", [P, B]), keep("minus_one", [P, B])
        self.eps = keep("eps", [P, B])
        self.expert_id = keep("expert_id", [P, E])
        self.place0 = keep("place0", [P, E])
        self.token_id = keep("token_id", [P, B])
        self.tile_id = keep("tile_id", [P, TILES])


class Norm:

    def __init__(self, keep, sem, name, fixed):
        self.fixed = fixed
        self.stat, self.mv = keep(name + "_stat", [P, B, 6]), keep(name + "_mv", [P, B, 2])
        self.inv_std, self.shift = keep(name + "_inv_std", [P, B]), keep(name + "_shift", [P, B])
        self.stat_d, self.mv_d, self.var_d, self.std_d, self.shift_d, self.done = (
            sem(name + "_" + n) for n in ("stats", "mean_var", "var", "inv_std", "shift", "applied"))

    def statistics(self, dve, tiles, c):
        wait_apart(dve, self.std_d, done(c - 1))
        for b in range(B):
            last = dve.bn_stats(self.stat[:, b, :], tiles[:, b, :])
        last.then_inc(self.stat_d, 1)
        wait_apart(dve, self.stat_d, done(c))
        for b in range(B):
            last = dve.bn_aggr(self.mv[:, b, :], self.stat[:, b, :])
        last.then_inc(self.mv_d, 1)

    def scale_and_shift(self, pool, c):
        pool.wait_ge(self.mv_d, done(c))
        pool.wait_ge(self.done, done(c - 1))
        inv_std, shift = self.inv_std[:, :], self.shift[:, :]
        pool.tensor_tensor(shift, self.mv[:, :, 0], self.fixed.minus_one[:, :], ALU.mult)
        pool.tensor_tensor(inv_std, self.mv[:, :, 1], self.fixed.eps[:, :], ALU.add).then_inc(self.var_d, 1)
        pool.wait_ge(self.var_d, done(c))
        pool.tensor_tensor(inv_std, inv_std, self.fixed.minus_half[:, :], ALU.pow).then_inc(self.std_d, 1)
        pool.wait_ge(self.std_d, done(c))
        pool.tensor_tensor(shift, shift, inv_std, ALU.mult).then_inc(self.shift_d, 1)

    def apply(self, act, tiles, dst, c):
        act.wait_ge(self.shift_d, done(c))
        for b in range(B):
            last = act.activation(dst[:, b, :], tiles[:, b, :], ACT.Identity, bias=self.shift[:, b:b + 1],
                                  scale=self.inv_std[:, b:b + 1])
        last.then_inc(self.done, 1)


def chunk_tiles(tok, c):
    return tok[:, :, :].rearrange("p (b c) d -> p b c d", b=B)[:, :, bass.ds(c, 1), :].rearrange("p b a d -> p b (a d)")


def build(nc, x_ch, x_tok, wqk3, bqk3, wv_t, bv, alpha, proxy_t, gate_t, w1, b1_t, w2, b2, out):
    wsplit = nc.dram_tensor("wsplit", [E, P, WROW], F32, kind="Internal").ap()
    normed = nc.dram_tensor("normed", [TOK + P, C], F32, kind="Internal").ap()
    places = nc.dram_tensor("places", [SLOTS, 2], I32, kind="Internal").ap()
    with ExitStack() as outer:
        def sem(name):
            return outer.enter_context(nc.semaphore(name))

        def keep(name, shape, dt=F32):
            return outer.enter_context(nc.sbuf_tensor(name, shape, dt))

        tok = keep("tok", [P, NT, C])
        wbuf = keep("wbuf", [P, 2, WROW], F32R)
        ident = keep("ident", [P, P])
        fixed = Fixed(keep)
        xraw = keep("xraw", [P, KT, N])
        xn = xraw[:, :, :].rearrange("p q (b d) -> p q b d", b=B)
        norm1 = Norm(keep, sem, "norm1", fixed)
        record_out = [sem(f"record_out{par}") for par in range(2)]
        stage_a(nc, sem, tok, wbuf, ident, fixed, xraw, xn, norm1, record_out, wsplit, normed, places, proxy_t, gate_t,
                x_ch, x_tok, wqk3, bqk3, wv_t, bv, alpha, w1, w2)
        tabs = keep("tabs", [P, 6, TILES], I32)
        bias1, bias2 = keep("bias1", [P, E, FT]), keep("bias2", [P, E, C])
        stage_b(nc, sem, tok, ident, fixed, xn, norm1, record_out, tabs, bias1, bias2, normed, places, b1_t, b2, out)
        stage_c(nc, sem, wbuf, ident, tabs, bias1, bias2, wsplit, normed, places, out)


def stage_a(nc, sem, tok, wbuf, ident, fixed, xraw, xn, norm1, record_out, wsplit, normed, places, proxy_t, gate_t,
            x_ch, x_tok, wqk3, bqk3, wv_t, bv, alpha, w1, w2):
    with ExitStack() as ctx:
        def sb(name, shape, dt=F32):
            return ctx.enter_context(nc.sbuf_tensor(name, shape, dt))

        xh, xl = sb("xh", [P, KT, N], F32R), sb("xl", [P, KT, N], F32R)
        wq_raw = sb("wq_raw", [P, 2, KT, 3 * MID])
        wqh, wql = sb("wqh", [P, 2, KT, 3 * MID], F32R), sb("wql", [P, 2, KT, 3 * MID], F32R)
        bqk = sb("bqk", [3 * MID, 2])
        wv_raw = sb("wv_raw", [P, KT, C])
        wvh, wvl = sb("wvh", [P, KT, C], F32R), sb("wvl", [P, KT, C], F32R)
        bvb = sb("bvb", [P, 1, C])
        alb = sb("alb", [P, 1])
        qk3 = sb("qk3", [3 * MID, 2, N], F32R)
        vf = sb("vf", [P, 2, HALF])
        vh, vl = sb("vh", [P, IT, C], F32R), sb("vl", [P, IT, C], F32R)
        prob = sb("prob", [P, 2, N])
        qkf = prob[0:3 * MID]
        pth, ptl = sb("pth", [P, 2, IT, P], F32R), sb("ptl", [P, 2, IT, P], F32R)
        negmax, rowsum, scale = sb("negmax", [P, 4]), sb("rowsum", [P, 4]), sb("scale", [P, 4])
        wraw = sb("wraw", [P, 2, WROW // 4])
        no_token, zero_row = sb("no_token", [P, SLOTS // P, 2], I32), sb("zero_row", [P, C])

        ps_sc = ctx.enter_context(nc.psum_tensor("ps_sc", [P, N], F32))
        ps_pt = [ctx.enter_context(nc.psum_tensor(f"ps_pt{i}", [P, N], F32)) for i in range(2)]
        ps_o = [ctx.enter_context(nc.psum_tensor(f"ps_o{i}", [P, HALF], F32)) for i in range(2)]

        wqk_in, consts, x_in, tok_in = sem("a_wqk_in"), sem("a_consts"), sem("a_x_in"), sem("a_tok_in")
        ident0, ident_ok, wsm_hi, wsm_ok = sem("a_ident0"), sem("a_ident"), sem("a_wsm_hi"), sem("a_wsm")
        x_hi, x_split = sem("a_x_hi"), sem("a_x_split")
        qk_mm, qk_full, qk_hi, qk_ok = sem("a_qk_mm"), sem("a_qk_full"), sem("a_qk_hi"), sem("a_qk_ok")
        v_mm, v_full, v_hi, v_ok = sem("a_v_mm"), sem("a_v_full"), sem("a_v_hi"), sem("a_v_ok")
        scored, maxed, exped = sem("a_scored"), sem("a_maxed"), sem("a_exped")
        turned, pt_hi, pt_ok = sem("a_turned"), sem("a_pt_hi"), sem("a_pt_ok")
        recip, scaled = sem("a_recip"), sem("a_scaled")
        summed, added = sem("a_summed"), sem("a_added")
        set0, norm_set, padding_ok = sem("a_set0"), sem("a_norm_set"), sem("a_padding")
        routing_in = sem("a_routing_in")
        w_in, w_hi, w_lo = [sem("a_w1_in"), sem("a_w2_in")], sem("a_w_hi"), sem("a_w_lo")
        w_out = [[sem(f"a_w{part + 1}_out{par}") for part in range(2)] for par in range(2)]

        def images(eng, image):
            with eng.Fori(0, B - 1) as b:
                image(b, True)
            image(B - 1, False)

        block = ctx.enter_context(nc.Block())

        @block.sync
        def _(sp):
            for kind in range(2):
                sp.dma_start(wq_raw[:, kind], wqk3[kind].rearrange("(k p) m -> p k m", p=P)).then_inc(wqk_in, 16)
            sp.dma_start(bqk[:, :], bqk3).then_inc(consts, 16)
            sp.dma_start(wv_raw[:, :, :], wv_t.rearrange("(k p) m -> p k m", p=P)).then_inc(consts, 16)
            sp.dma_start(bvb[:, 0, :], bv.partition_broadcast(P)).then_inc(consts, 16)
            sp.dma_start(alb[:, :], alpha.partition_broadcast(P)).then_inc(consts, 16)
            sp.wait_ge(x_in, 16)
            sp.wait_ge(consts, 64)
            sp.dma_start(tok[:, :, :], x_tok.rearrange("(g p) c -> p g c", p=P)).then_inc(tok_in, 16)

            sp.dma_start(fixed.proxy[:, :, :], proxy_t.rearrange("(k p) n -> p k n", p=P)).then_inc(routing_in, 16)
            sp.dma_start(fixed.gate[:, :, :], gate_t.rearrange("(k p) n -> p k n", p=P)).then_inc(routing_in, 16)

            def load(e, part):
                src = (w1, w2)[part][bass.ds(e, 1)].rearrange("a (k p) f -> p (a k) f", p=P)
                dst = wraw[:, part].rearrange("p (k f) -> p k f", k=(KT, FT)[part])
                sp.dma_start(dst, src).then_inc(w_in[part], 16)

            def store(i, par, part):
                at = slice(part * W2AT, (part + 1) * W2AT)
                sp.dma_start(wsplit[bass.ds(i + 2, 1)].rearrange("a p w -> (a p) w")[:, at],
                             wbuf[:, par, at].bitcast(F32)).then_inc(w_out[par][part], 16)

            load(2, 0)
            load(2, 1)
            with sp.Fori(0, E // 2 - 1) as h:
                for par in range(2):
                    for part in range(2):
                        wait_apart(sp, w_lo, done((h * 2 + par) * 2 + part))
                        load((h * 2 + (par + 3)) % E, part)
                        store(h * 2 + par, par, part)
            for part in range(2):
                wait_apart(sp, w_lo, done((E - 2) * 2 + part))
                load(1, part)
            for s in w_out[0] + w_out[1]:
                sp.wait_ge(s, 16 * (E // 2))
            sp.wait_ge(routing_in, 32)

        @block.gpsimd
        def _(pool):
            pool.sem_inc(w_lo, CREDIT)
            for s in (v_ok, norm1.var_d, norm1.std_d, norm1.shift_d):
                pool.sem_inc(s, CREDIT)
            for s in w_out[0] + w_out[1]:
                pool.sem_inc(s, 16)
            pool.memset(ident[:, :], 0.0).then_inc(ident0, 1)
            pool.wait_ge(ident0, 1)
            pool.affine_select(out=ident[:, :], in_=ident[:, :], compare_op=ALU.not_equal, fill=1.0,
                               base=0, pattern=[[-1, P]], channel_multiplier=1).then_inc(ident_ok, 1)

            pool.memset(fixed.causal[:, :], 1.0).then_inc(set0, 1)
            pool.memset(fixed.before[:, :], 1.0).then_inc(set0, 1)
            pool.memset(fixed.ones[:, :], 1.0)
            pool.memset(fixed.minus_half[:, :], -0.5).then_inc(norm_set, 1)
            pool.memset(fixed.minus_one[:, :], -1.0).then_inc(norm_set, 1)
            pool.memset(fixed.eps[:, :], LN_EPS).then_inc(norm_set, 1)
            pool.iota(fixed.expert_id[:, :], pattern=[[1, E]], base=0, channel_multiplier=0,
                      allow_small_or_imprecise_dtypes=True)
            pool.iota(fixed.tile_id[:, :], pattern=[[1, TILES]], base=0, channel_multiplier=0,
                      allow_small_or_imprecise_dtypes=True)
            pool.iota(fixed.place0[:, :], pattern=[[CAP, E]], base=0, channel_multiplier=0,
                      allow_small_or_imprecise_dtypes=True)
            pool.iota(fixed.token_id[:, :], pattern=[[N, B]], base=0, channel_multiplier=1,
                      allow_small_or_imprecise_dtypes=True)
            pool.iota(no_token[:, :, 0], pattern=[[0, SLOTS // P // P], [1, P]], base=TOK,
                      channel_multiplier=0).then_inc(padding_ok, 1)
            pool.memset(no_token[:, :, 1], 0).then_inc(padding_ok, 1)
            pool.memset(zero_row[:, :], 0.0).then_inc(padding_ok, 1)
            pool.wait_ge(set0, 2)
            pool.affine_select(out=fixed.causal[:, :], in_=fixed.causal[:, :], compare_op=ALU.is_ge, fill=0.0, base=0,
                               pattern=[[1, P]], channel_multiplier=-1)
            pool.affine_select(out=fixed.before[:, :], in_=fixed.before[:, :], compare_op=ALU.is_gt, fill=0.0, base=0,
                               pattern=[[1, P]], channel_multiplier=-1)

            pool.wait_ge(padding_ok, 3)
            pool.dma_start(places.rearrange("(p g) r -> p (g r)", p=P),
                           no_token[:, :, :].rearrange("p g r -> p (g r)")).then_inc(record_out[0], 16)
            pool.dma_start(normed[TOK:TOK + P, :], zero_row[:, :]).then_inc(record_out[1], 16)

            def image(b, more):
                for ch in range(4):
                    pool.wait_ge(v_hi, done(b * 4 + ch))
                    pool.tensor_tensor(vl[:, 2 * ch:2 * ch + 2, :], vf[:, ch % 2].rearrange("p (j c) -> p j c", j=2),
                                       vh[:, 2 * ch:2 * ch + 2, :].bitcast(F32), ALU.subtract).then_inc(v_ok, 1)
                for par in range(2):
                    for part in range(2):
                        if more and (par, part) == (0, 1):
                            pool.wait_ge(x_hi, b + 3)
                            pool.tensor_tensor(xl[:, :, :], xraw[:, :, :], xh[:, :, :].bitcast(F32),
                                               ALU.subtract).then_inc(x_split, 1)
                        pool.wait_ge(w_hi, (b * 4 + (par * 2 + part + 1)) * 2)
                        at, n = part * W2AT, W2AT // 2
                        pool.tensor_tensor(wbuf[:, par, at + n:at + 2 * n], wraw[:, part],
                                           wbuf[:, par, at:at + n].bitcast(F32), ALU.subtract).then_inc(w_lo, 1)
                        if not more and (par, part) == (1, 0):
                            pool.wait_ge(norm_set, 3)
                            norm1.scale_and_shift(pool, 0)

            images(pool, image)
            for s in record_out:
                pool.wait_ge(s, 16)

        @block.scalar
        def _(act):
            for s in (exped, pt_hi, qk_full, v_hi, norm1.done):
                act.sem_inc(s, CREDIT)

            def load_x(b):
                act.dma_start(xraw[:, :, :], x_ch[bass.ds(b, 1)].rearrange("a (k p) n -> p (a k) n", p=P)
                              ).then_inc(x_in, 16)

            def whole_qk(b, kind):
                act.wait_ge(qk_mm, done(b * 2 + kind))
                act.wait_ge(turned, done(b * IT - 2 + kind))
                act.activation(qkf[:, kind], (ps_sc, ps_pt[0])[kind][0:3 * MID, :], ACT.Identity,
                               bias=bqk[:, kind:kind + 1]).then_inc(qk_full, 1)

            def image(b, more):
                def high_v(ch):
                    act.wait_ge(v_full, done(b * 4 + ch))
                    if ch == 0:
                        act.wait_ge(summed, done(b * IT - 1))
                    act.activation(vh[:, 2 * ch:2 * ch + 2, :], vf[:, ch % 2], ACT.Copy).then_inc(v_hi, 1)

                def exp_tile(it):
                    act.wait_ge(maxed, done(b * IT + it))
                    act.wait_ge(turned, done(b * IT + it - 2))
                    col = slice(it % 4, it % 4 + 1)
                    act.activation(prob[:, it % 2], ps_sc[:, :], ACT.Exp, bias=negmax[:, col],
                                   accum_out=rowsum[:, col]).then_inc(exped, 1)

                def hi_tile(it):
                    act.wait_ge(turned, done(b * IT + it))
                    act.wait_ge(summed, done(b * IT + it - 2))
                    act.activation(pth[:, it % 2], ps_pt[it % 2].rearrange("p (j i) -> p j i", j=IT),
                                   ACT.Copy).then_inc(pt_hi, 1)

                def weights_high(it):
                    par, part, half = it // 4, it // 2 % 2, it % 2
                    if half == 0:
                        act.wait_ge(w_in[part], (b * 2 + (par + 1)) * 16)
                        act.wait_ge(w_out[par][part], (b + 1) * 16)
                    at, n = part * W2AT, W2AT // 4
                    act.activation(wbuf[:, par, at + half * n:at + (half + 1) * n], wraw[:, part, half * n:(half + 1) * n],
                                   ACT.Copy).then_inc(w_hi, 1)

                high_v(0)
                exp_tile(0)
                high_v(1)
                high_v(2)
                exp_tile(1)
                high_v(3)
                hi_tile(0)
                for it in range(IT):
                    if it == 7 and more:
                        whole_qk(b + 1, 0)
                    for n in [it] if more or it < IT - 3 else [[IT - 3, IT - 2], [IT - 1], []][it - (IT - 3)]:
                        weights_high(n)
                    if it + 1 < IT:
                        hi_tile(it + 1)
                    if it + 2 < IT:
                        exp_tile(it + 2)
                    if it == IT - 2 and not more:
                        act.wait_ge(x_in, 16 * (B + 1))
                        norm1.apply(act, chunk_tiles(tok, 0), xn[:, 0], 0)
                    if it == 2 and more:
                        act.wait_ge(x_in, (b + 2) * 16)
                        act.wait_ge(v_mm, done(b * 4 + 3))
                        act.activation(xh[:, :, :], xraw[:, :, :], ACT.Copy).then_inc(x_hi, 1)
                    if it == 6 and more:
                        wait_apart(act, x_split, b + 3)
                        load_x((b + 2) % B)
                if more:
                    whole_qk(b + 1, 1)

            load_x(0)
            act.wait_ge(x_in, 16)
            for k in range(KT):
                act.activation(xh[:, k], xraw[:, k], ACT.Copy).then_inc(x_hi, 1)
            act.wait_ge(x_split, 2)
            load_x(1)
            act.wait_ge(consts, 64)
            whole_qk(0, 0)
            whole_qk(0, 1)
            images(act, image)

        @block.vector
        def _(dve):
            for s in (norm1.stat_d, norm1.mv_d, qk_ok, v_full, maxed, pt_ok, scaled, recip, added, qk_hi):
                dve.sem_inc(s, CREDIT)
            dve.wait_ge(wqk_in, 32)
            dve.tensor_copy(wqh[:, :, :, :], wq_raw[:, :, :, :]).then_inc(wsm_hi, 1)
            dve.wait_ge(wsm_hi, 1)
            dve.tensor_tensor(wql[:, :, :, :], wq_raw[:, :, :, :], wqh[:, :, :, :].bitcast(F32), ALU.subtract).then_inc(wsm_ok, 1)
            for k in range(KT):
                dve.wait_ge(x_hi, k + 1)
                dve.tensor_tensor(xl[:, k], xraw[:, k], xh[:, k].bitcast(F32), ALU.subtract).then_inc(x_split, 1)
            dve.wait_ge(consts, 64)
            dve.tensor_copy(wvh[:, :, :], wv_raw[:, :, :]).then_inc(wsm_hi, 1)
            dve.wait_ge(wsm_hi, 2)
            dve.tensor_tensor(wvl[:, :, :], wv_raw[:, :, :], wvh[:, :, :].bitcast(F32), ALU.subtract).then_inc(wsm_ok, 1)

            def stack(b, kind):
                dve.wait_ge(qk_full, done(b * 2 + kind))
                dve.wait_ge(scored, done(b * IT - 1))
                dve.tensor_copy(qk3[:, kind], qkf[:, kind]).then_inc(qk_hi, 1)
                dve.wait_ge(qk_hi, done(b * 2 + kind))
                at = slice(MID, 2 * MID) if kind == 0 else slice(2 * MID, 3 * MID)
                dve.tensor_tensor(qk3[at, kind], qkf[at, kind], qk3[at, kind].bitcast(F32), ALU.subtract).then_inc(qk_ok, 1)

            def image(b, more):
                def full_v(ch):
                    dve.wait_ge(v_mm, done(b * 4 + ch))
                    dve.wait_ge(v_ok, done(b * 4 + ch - 2))
                    src = ps_pt[1][:, ch * HALF:(ch + 1) * HALF] if ch < 2 else ps_o[ch - 2][:, :]
                    dve.tensor_tensor(vf[:, ch % 2].rearrange("p (j c) -> p j c", j=2), src.rearrange("p (j c) -> p j c", j=2),
                                      bvb[:, :, :].to_broadcast([P, 2, C]), ALU.add).then_inc(v_full, 1)

                def max_tile(it):
                    dve.wait_ge(scored, done(b * IT + it))
                    dve.tensor_reduce(negmax[:, it % 4:it % 4 + 1], ps_sc[:, :], AX.X, ALU.max, negate=True).then_inc(maxed, 1)

                def low_tile(it):
                    h = it % 2
                    dve.wait_ge(pt_hi, done(b * IT + it))
                    dve.tensor_tensor(ptl[:, h], ps_pt[h].rearrange("p (j i) -> p j i", j=IT), pth[:, h].bitcast(F32),
                                      ALU.subtract).then_inc(pt_ok, 1)

                full_v(0)
                max_tile(0)
                full_v(1)
                full_v(2)
                max_tile(1)
                full_v(3)
                low_tile(0)
                for it in range(IT):
                    g, h = b * IT + it, it % 2
                    col = slice(it % 4, it % 4 + 1)
                    if it + 2 < IT:
                        max_tile(it + 2)
                    dve.wait_ge(exped, done(g))
                    dve.reciprocal(scale[:, col], rowsum[:, col]).then_inc(recip, 1)
                    if it + 1 < IT:
                        low_tile(it + 1)
                    dve.wait_ge(recip, done(g))
                    dve.tensor_tensor(scale[:, col], scale[:, col], alb[:, :], ALU.mult).then_inc(scaled, 1)
                    dve.wait_ge(scaled, done(g))
                    if it == 0:
                        wait_apart(dve, tok_in, 16)
                    if more and it == IT - 1:
                        stack(b + 1, 1)
                    dve.wait_ge(summed, done(g))
                    mine = tok[:, bass.ds(g, 1), :].rearrange("p a c -> p (a c)")
                    dve.scalar_tensor_tensor(out=mine, in0=ps_o[h][:, 0:C], scalar=scale[:, col], in1=mine,
                                             op0=ALU.mult, op1=ALU.add).then_inc(added, 1)
                    if more and it == IT - 2:
                        stack(b + 1, 0)
                    if not more and it == 3:
                        dve.wait_ge(added, done(b * IT))
                        norm1.statistics(dve, chunk_tiles(tok, 0), 0)

            stack(0, 0)
            stack(0, 1)
            images(dve, image)

        @block.tensor
        def _(pe):
            for s in (qk_mm, v_mm, scored, turned, summed):
                pe.sem_inc(s, CREDIT)
            pe.wait_ge(wsm_ok, 1)
            pe.wait_ge(ident_ok, 1)

            def project_qk(b, kind):
                if kind == 0:
                    pe.wait_ge(x_split, b + 2)
                    pe.wait_ge(exped, done(b * IT - 1))
                else:
                    pe.wait_ge(pt_ok, done(b * IT - 2))
                dst = (ps_sc, ps_pt[0])[kind]
                for n in range(N // HALF):
                    cols = slice(n * HALF, (n + 1) * HALF)
                    for k in range(KT):
                        last = mm3(pe, dst[0:3 * MID, cols], (wqh[:, kind, k], wql[:, kind, k]),
                                   (xh[:, k, cols], xl[:, k, cols]), k == 0, k == KT - 1)
                last.then_inc(qk_mm, 1)

            def image(b, more):
                pe.wait_ge(pt_ok, done(b * IT - 1))

                def project_v(ch):
                    if ch == 2:
                        pe.wait_ge(added, done(b * IT - 1))
                    dst = ps_pt[1][:, ch * HALF:(ch + 1) * HALF] if ch < 2 else ps_o[ch - 2][:, :]
                    for j in range(2):
                        rows = slice((2 * ch + j) * P, (2 * ch + j + 1) * P)
                        for k in range(KT):
                            last = mm3(pe, dst[:, j * C:(j + 1) * C], (xh[:, k, rows], xl[:, k, rows]),
                                       (wvh[:, k], wvl[:, k]), k == 0, k == KT - 1)
                    last.then_inc(v_mm, 1)

                def score(it):
                    if it == 0:
                        pe.wait_ge(qk_full, done(b * 2))
                        pe.wait_ge(qk_ok, done(b * 2 + 1))
                    pe.wait_ge(exped, done(b * IT + it - 1))
                    for n in range(N // HALF):
                        cols = slice(n * HALF, (n + 1) * HALF)
                        last = pe.matmul(ps_sc[:, cols], qk3[:, 0, it * P:(it + 1) * P], qk3[:, 1, cols],
                                         start=True, stop=True)
                    last.then_inc(scored, 1)

                def turn(it):
                    pe.wait_ge(exped, done(b * IT + it))
                    pe.wait_ge(pt_ok, done(b * IT + it - 2))
                    if it == 1:
                        pe.wait_ge(v_full, done(b * 4 + 1))
                    for j in range(IT):
                        last = pe.transpose(ps_pt[it % 2][:, j * P:(j + 1) * P], prob[:, it % 2, j * P:(j + 1) * P], ident[:, :])
                    last.then_inc(turned, 1)

                def weigh(it):
                    pe.wait_ge(pt_ok, done(b * IT + it))
                    pe.wait_ge(added, done(b * IT + it - 2))
                    if it == 0:
                        pe.wait_ge(v_ok, done(b * 4 + 3))
                    for j in range(IT):
                        last = mm3(pe, ps_o[it % 2][:, 0:C], (pth[:, it % 2, j], ptl[:, it % 2, j]),
                                   (vh[:, j], vl[:, j]), j == 0, j == IT - 1)
                    last.then_inc(summed, 1)

                project_v(0)
                score(0)
                project_v(1)
                project_v(2)
                score(1)
                project_v(3)
                turn(0)
                for it in range(IT):
                    if it + 2 < IT:
                        score(it + 2)
                    if it + 1 < IT:
                        turn(it + 1)
                    if more and it >= IT - 2:
                        project_qk(b + 1, it - (IT - 2))
                    weigh(it)

            project_qk(0, 0)
            project_qk(0, 1)
            pe.wait_ge(wsm_ok, 2)
            images(pe, image)


def stage_b(nc, sem, tok, ident, fixed, xn, norm1, record_out, tabs, bias1, bias2, normed, places, b1_t, b2, out):
    with ExitStack() as ctx:
        def sb(name, shape, dt=F32):
            return ctx.enter_context(nc.sbuf_tensor(name, shape, dt))

        def ps(name, shape):
            return ctx.enter_context(nc.psum_tensor(name, shape, F32))

        xt1 = sb("xt1", [P, B, KT, P])
        prod = sb("prod", [P, 2, B, NP])
        prod_rel, prod_w = sb("prod_rel", [P, B, NP]), sb("prod_w", [P, B, NP])
        prod_max, prod_sum = sb("prod_max", [P, B]), sb("prod_sum", [P, B])
        turned_pw = sb("turned_pw", [NP, 2, 2 * B, P])
        attn = sb("attn", [P, B, P])
        state = sb("state", [NP, 2, B, C])
        norm2 = Norm(sb, sem, "norm2", fixed)
        x2 = sb("x2", [P, B, C])
        xt2 = sb("xt2", [P, B, KT, P])
        logit = sb("logit", [P, B, E])
        top, top_id = sb("top", [P, B, 8]), sb("top_id", [P, B, 8], U32)
        top_f = sb("top_f", [P, B, 2])
        hot = sb("hot", [P, 2, B, E])
        chose = sb("chose", [P, B, E], BF16)
        counts_m = sb("counts_m", [P, E], BF16)
        newly = sb("newly", [P, E])
        rank = sb("rank", [P, B, E])
        hot_rank = sb("hot_rank", [P, 2, B, E])
        place_f = sb("place_f", [P, 2, B])
        place = sb("place", [P, 2, 2, B], I32)
        gap, gap_exp, gap_den = sb("gap", [P, B]), sb("gap_exp", [P, B]), sb("gap_den", [P, B])
        record = sb("record", [P, 2, 2, B, 2], I32)

        count_i, tiles_i = sb("count_i", [P, E], I32), sb("tiles_i", [P, E], I32)
        n_tiles, ends = sb("n_tiles", [P, E]), sb("ends", [P, E])
        past, picked = sb("past", [P, TILES, E]), sb("picked", [P, TILES, E])
        passed, starts, first = sb("passed", [P, TILES]), sb("starts", [P, TILES]), sb("first", [P, TILES])
        expert, expert_i = sb("expert", [P, TILES]), sb("expert_i", [P, TILES], I32)

        ps_xt = ps("ps_xt", [P, B * KT * P])
        ps_small = ps("ps_small", [P, HALF])
        ps_pw = ps("ps_pw", [P, 2 * B * P])
        ps_a = ps("ps_a", [P, B * P])
        ps_out = ps("ps_out", [P, B * C])
        ps_prod = ps_small[:, 0:B * NP].rearrange("p (b n) -> p b n", b=B)
        ps_logit = ps_small[:, 64:64 + B * E].rearrange("p (b n) -> p b n", b=B)
        ps_rank = ps_a[:, 0:B * E]
        ps_count = ps_small[:, 0:E]

        def sems(names):
            return [sem("b_" + n) for n in names.split()]

        zeroed = sem("b_zeroed")
        biases_in, counted, table_step = sems("biases_in counted table_step")
        prod_d, pmax_d, prel_d, psum_d, prec_d, pw_d = sems(
            "prod prod_max prod_rel prod_sum prod_recip prod_w")
        attn_d, tok_d, state_d, logit_d, top_d, topid_d = sems(
            "attn tok state logit top top_id")
        topf_d, hot_d, chose_d, newly_d, count_d, rank_d, hotrank_d, placef_d, place_d = sems(
            "top_f hot chose newly count rank hot_rank place_f place")
        gap_d, den_d, share_d, record_d, tokid_d = sems("gap gap_den share record token_id")
        xt1_d, pexp_d, pw_turned_d, xt2_d, gexp_d = sems("xt1 prod_exp turned_pw xt2 gap_exp")
        t1_mm, prod_mm, pw_mm, a_mm, state_mm, out_mm, t2_mm, logit_mm, rank_mm = sems(
            "t1_mm prod_mm pw_mm a_mm state_mm out_mm t2_mm logit_mm rank_mm")
        tok_out, x2_out = sems("tok_out x2_out")
        CH = IT

        def exists(c):
            return not isinstance(c, int) or 0 <= c < CH

        def steps(eng, body):
            for i in range(-2, 1):
                body(i, i % 2)
            with eng.Fori(0, CH // 2 - 2) as k:
                for j in range(2):
                    body(k * 2 + (1 + j), 1 - j)
            for i in range(CH - 3, CH + 1):
                body(i, i % 2)

        block = ctx.enter_context(nc.Block())
        out_v = out[0:TOK, :].rearrange("(b c p) d -> c p b d", b=B, p=P)
        normed_v = normed[0:TOK, :].rearrange("(b c p) d -> c p b d", b=B, p=P)

        @block.sync
        def _(sp):
            sp.dma_start(bias1[:, :, :], b1_t).then_inc(biases_in, 16)
            sp.dma_start(bias2[:, :, :].rearrange("p e c -> p (e c)"),
                         b2.rearrange("e c -> (e c)").partition_broadcast(P)).then_inc(biases_in, 16)

            def body(i, par):
                if exists(i):
                    wait_apart(sp, norm2.done, done(i))
                    sp.dma_start(normed_v[bass.ds(i, 1)].rearrange("a p b d -> p (a b) d"), x2[:, :, :]).then_inc(x2_out, 16)
                near = i + 1
                if exists(near):
                    wait_apart(sp, tok_d, done(near))
                    sp.dma_start(out_v[bass.ds(near, 1)].rearrange("a p b d -> p (a b) d"),
                                 chunk_tiles(tok, near)).then_inc(tok_out, 16)

            steps(sp, body)
            sp.wait_ge(tok_out, 16 * CH)
            sp.wait_ge(x2_out, 16 * CH)
            sp.wait_ge(biases_in, 32)

        @block.gpsimd
        def _(pool):
            for s in (norm2.var_d, norm2.std_d, norm2.shift_d):
                pool.sem_inc(s, CREDIT)

            def scatter(c, par):
                wait_apart(pool, record_d, done(c))
                for k, b in [(k, b) for k in range(2) for b in range(B)]:
                    pool.indirect_dma_start(
                        out=places, out_offset=bass.IndirectOffsetOnAxis(ap=place[:, par, k, b:b + 1], axis=0),
                        in_=record[:, par, k, b, :], in_offset=None).then_inc(record_out[par], 16)

            def body(i, par):
                near, new = i + 1, i + 3
                if exists(new):
                    norm1.scale_and_shift(pool, new)
                if exists(i - 1):
                    scatter(i - 1, 1 - par)
                if exists(near):
                    norm2.scale_and_shift(pool, near)

            pool.memset(state[:, 0], 0.0).then_inc(zeroed, 1)
            pool.memset(counts_m[:, :], 0.0).then_inc(zeroed, 1)
            steps(pool, body)
            for par in range(2):
                pool.wait_ge(record_out[par], 16 * B * CH + 16)

        @block.scalar
        def _(act):
            for s in (norm2.done, xt1_d, pexp_d, pw_turned_d, xt2_d, gexp_d):
                act.sem_inc(s, CREDIT)

            def evacuate_turned(c, dst, ready, turned, read):
                act.wait_ge(turned, done(c))
                act.wait_ge(read, done(c - 1))
                act.activation(dst[:, :, :, :], ps_xt[:, :].rearrange("p (b k t) -> p b k t", b=B, k=KT),
                               ACT.Copy).then_inc(ready, 1)

            def normalise_new(new, par):
                act.wait_ge(out_mm, done(new - 2))
                norm1.apply(act, chunk_tiles(tok, new), xn[:, 1 - par], new)

            def body(i, par):
                near, far, new = i + 1, i + 2, i + 3
                if exists(far):
                    evacuate_turned(far, xt1, xt1_d, t1_mm, prod_mm)
                if exists(i):
                    if exists(i - 1):
                        act.wait_ge(x2_out, i * 16)
                    act.wait_ge(t2_mm, done(i - 1))
                    norm2.apply(act, chunk_tiles(tok, i), x2, i)
                if exists(i - 1):
                    act.wait_ge(gap_d, done(i - 1))
                    act.activation(gap_exp[:, :], gap[:, :], ACT.Exp).then_inc(gexp_d, 1)
                if exists(new) and not exists(near):
                    normalise_new(new, par)
                if exists(far):
                    act.wait_ge(prel_d, done(far))
                    act.activation(prod_rel[:, :, :], prod_rel[:, :, :], ACT.Exp, scale=float(NP) ** -0.5).then_inc(pexp_d, 1)
                if exists(i):
                    evacuate_turned(i, xt2, xt2_d, t2_mm, logit_mm)
                if exists(new) and exists(near):
                    normalise_new(new, par)
                if exists(far):
                    act.wait_ge(pw_mm, done(far))
                    act.wait_ge(out_mm, done(far - 2))
                    act.activation(turned_pw[:, par], ps_pw[0:NP, :].rearrange("p (b t) -> p b t", b=2 * B),
                                   ACT.Copy).then_inc(pw_turned_d, 1)

            steps(act, body)

        @block.vector
        def _(dve):
            for s in (norm2.stat_d, norm2.mv_d, prod_d, pmax_d, prel_d, psum_d, prec_d, pw_d, attn_d, tok_d, state_d,
                      logit_d, top_d, topid_d, topf_d, hot_d, chose_d, newly_d, count_d, rank_d,
                      hotrank_d, placef_d, place_d, gap_d, den_d, share_d, record_d, tokid_d):
                dve.sem_inc(s, CREDIT)
            def wide(small):
                return small.unsqueeze(2).to_broadcast([P, B, NP])

            def proxy_softmax_in(c, par):
                dve.wait_ge(prod_mm, done(c))
                dve.wait_ge(state_mm, done(c - 2))
                dve.tensor_copy(prod[:, par], ps_prod).then_inc(prod_d, 1)
                dve.tensor_reduce(prod_max[:, :], ps_prod, AX.X, ALU.max).then_inc(pmax_d, 1)
                dve.wait_ge(prod_d, done(c))
                dve.wait_ge(pmax_d, done(c))
                dve.tensor_tensor(prod_rel[:, :, :], prod[:, par], wide(prod_max[:, :]), ALU.subtract).then_inc(prel_d, 1)

            def proxy_softmax_out(c):
                dve.wait_ge(pexp_d, done(c))
                dve.tensor_reduce(prod_sum[:, :], prod_rel[:, :, :], AX.X, ALU.add).then_inc(psum_d, 1)
                dve.wait_ge(psum_d, done(c))
                dve.reciprocal(prod_sum[:, :], prod_sum[:, :]).then_inc(prec_d, 1)
                dve.wait_ge(prec_d, done(c))
                dve.wait_ge(pw_mm, done(c - 1))
                dve.tensor_tensor(prod_w[:, :, :], prod_rel[:, :, :], wide(prod_sum[:, :]), ALU.mult).then_inc(pw_d, 1)

            def mask(c):
                dve.wait_ge(a_mm, done(c))
                dve.tensor_tensor(attn[:, :, :], ps_a[:, :].rearrange("p (b t) -> p b t", b=B),
                                  fixed.causal[:, :].unsqueeze(1).to_broadcast([P, B, P]), ALU.mult).then_inc(attn_d, 1)

            def grow_state(c, par):
                dve.wait_ge(state_mm, done(c))
                dve.wait_ge(out_mm, done(c - 1))
                dve.tensor_tensor(state[:, 1 - par], ps_pw[0:NP, :].rearrange("p (b d) -> p b d", b=B), state[:, par],
                                  ALU.add).then_inc(state_d, 1)

            def add_out(c):
                dve.wait_ge(out_mm, done(c))
                dve.tensor_tensor(chunk_tiles(tok, c), ps_out[:, :].rearrange("p (b d) -> p b d", b=B), chunk_tiles(tok, c),
                                  ALU.add).then_inc(tok_d, 1)

            def choose(c):
                dve.wait_ge(logit_mm, done(c))
                dve.tensor_copy(logit[:, :, :], ps_logit).then_inc(logit_d, 1)
                wait_apart(dve, logit_d, done(c))
                for b in range(B):
                    last = dve.max(top[:, b, :], logit[:, b, :])
                last.then_inc(top_d, 1)
                dve.wait_ge(top_d, done(c))
                dve.tensor_tensor(gap[:, :], top[:, :, 1], top[:, :, 0], ALU.subtract).then_inc(gap_d, 1)
                for b in range(B):
                    last = dve.max_index(top_id[:, b, :], top[:, b, :], logit[:, b, :])
                last.then_inc(topid_d, 1)

            def mark(c):
                dve.wait_ge(topid_d, done(c))
                dve.tensor_copy(top_f[:, :, :], top_id[:, :, 0:2]).then_inc(topf_d, 1)
                dve.wait_ge(topf_d, done(c))
                for k in range(2):
                    last = dve.tensor_tensor(hot[:, k], fixed.expert_id[:, :].unsqueeze(1).to_broadcast([P, B, E]),
                                             top_f[:, :, k:k + 1].to_broadcast([P, B, E]), ALU.is_equal)
                last.then_inc(hot_d, 1)
                dve.wait_ge(hot_d, done(c))
                dve.wait_ge(rank_mm, done(c - 1))
                dve.wait_ge(newly_d, done(c - 1))
                dve.tensor_tensor(chose[:, :, :], hot[:, 0], hot[:, 1], ALU.add).then_inc(chose_d, 1)

            def find_places(c, par):
                dve.wait_ge(rank_mm, done(c))
                dve.tensor_tensor(rank[:, :, :], ps_rank.rearrange("p (b e) -> p b e", b=B),
                                  fixed.place0[:, :].unsqueeze(1).to_broadcast([P, B, E]), ALU.add).then_inc(rank_d, 1)
                dve.wait_ge(rank_d, done(c))
                for k in range(2):
                    last = dve.tensor_tensor(hot_rank[:, k], hot[:, k], rank[:, :, :], ALU.mult)
                last.then_inc(hotrank_d, 1)
                dve.tensor_reduce(newly[:, :], chose[:, :, :].rearrange("p b e -> p e b"), AX.X, ALU.add).then_inc(newly_d, 1)
                dve.wait_ge(newly_d, done(c))
                dve.tensor_tensor(counts_m[:, :], counts_m[:, :], newly[:, :], ALU.add).then_inc(count_d, 1)
                dve.wait_ge(gexp_d, done(c))
                dve.tensor_scalar(gap_den[:, :], gap_exp[:, :], 1.0, None, ALU.add).then_inc(den_d, 1)
                dve.wait_ge(hotrank_d, done(c))
                dve.tensor_reduce(place_f[:, :, :], hot_rank[:, :, :, :], AX.X, ALU.add).then_inc(placef_d, 1)
                dve.wait_ge(record_out[par], (c - par) * (B * 16) + 16)
                dve.wait_ge(den_d, done(c))
                dve.reciprocal(record[:, par, 0, :, 1].bitcast(F32), gap_den[:, :]).then_inc(share_d, 1)
                dve.wait_ge(placef_d, done(c))
                dve.tensor_copy(place[:, par], place_f[:, :, :]).then_inc(place_d, 1)
                for k in range(2):
                    last = dve.tensor_copy(record[:, par, k, :, 0], fixed.token_id[:, :])
                last.then_inc(place_d, 1)
                dve.wait_ge(share_d, done(c))
                dve.wait_ge(place_d, c * 2 + (CREDIT + 2))
                dve.tensor_scalar(fixed.token_id[:, :], fixed.token_id[:, :], float(P), None, ALU.add).then_inc(tokid_d, 1)
                dve.tensor_tensor(record[:, par, 1, :, 1].bitcast(F32), gap_exp[:, :], record[:, par, 0, :, 1].bitcast(F32),
                                  ALU.mult).then_inc(record_d, 1)
                dve.wait_ge(tokid_d, done(c))

            def body(i, par):
                near, far, new = i + 1, i + 2, i + 3
                if exists(near):
                    mask(near)
                if exists(new):
                    norm1.statistics(dve, chunk_tiles(tok, new), new)
                if exists(i - 1):
                    find_places(i - 1, 1 - par)
                if exists(near):
                    grow_state(near, 1 - par)
                if exists(far):
                    proxy_softmax_in(far, par)
                    proxy_softmax_out(far)
                if exists(near):
                    add_out(near)
                    dve.wait_ge(tok_d, done(near))
                    norm2.statistics(dve, chunk_tiles(tok, near), near)
                if exists(i):
                    choose(i)
                    mark(i)

            def make_table():
                n = 0

                def then(instruction):
                    nonlocal n
                    n += 1
                    instruction.then_inc(table_step, 1)
                    dve.wait_ge(table_step, n)

                def per_tile(x):
                    return x.unsqueeze(1).to_broadcast([P, TILES, E])

                dve.wait_ge(counted, 1)
                then(dve.tensor_scalar(count_i[:, :], ps_count, float(P - 1), None, ALU.add))
                then(dve.tensor_scalar(tiles_i[:, :], count_i[:, :], P.bit_length() - 1, None, ALU.arith_shift_right))
                then(dve.tensor_scalar(n_tiles[:, :], tiles_i[:, :], 1.0, None, ALU.max))
                then(dve.tensor_tensor_scan(ends[:, :], fixed.ones[:, 0:E], n_tiles[:, :], 0.0, ALU.mult, ALU.add))
                dve.tensor_copy(tabs[:, T_TOTAL, 0:1], ends[:, E - 1:E])
                then(dve.tensor_tensor(past[:, :, :], fixed.tile_id[:, :].unsqueeze(2).to_broadcast([P, TILES, E]),
                                       per_tile(ends[:, :]), ALU.is_ge))
                then(dve.tensor_reduce(passed[:, :], past[:, :, :], AX.X, ALU.add))
                then(dve.tensor_tensor(picked[:, :, :], past[:, :, :], per_tile(n_tiles[:, :]), ALU.mult))
                then(dve.tensor_reduce(starts[:, :], picked[:, :, :], AX.X, ALU.add))
                then(dve.tensor_tensor(starts[:, :], fixed.tile_id[:, :], starts[:, :], ALU.subtract))
                then(dve.scalar_tensor_tensor(out=tabs[:, T_PLACE, :], in0=passed[:, :], scalar=float(CAP // P),
                                              in1=starts[:, :], op0=ALU.mult, op1=ALU.add))
                then(dve.tensor_scalar(expert[:, :], passed[:, :], float(E - 1), None, ALU.min))
                dve.tensor_copy(tabs[:, T_EXPERT, :], expert[:, :])
                dve.tensor_scalar(tabs[:, T_NEXT, :], expert[:, :], 1.0, float(E - 1), ALU.add, ALU.min)
                dve.memset(tabs[:, T_FIRST, 0:1], 0)
                dve.tensor_tensor(first[:, 1:TILES], expert[:, 1:TILES], expert[:, 0:TILES - 1], ALU.is_gt)
                then(dve.tensor_copy(expert_i[:, :], expert[:, :]))
                dve.tensor_scalar(tabs[:, T_BUFFER, :], expert_i[:, :], 1, None, ALU.bitwise_and)
                then(dve.scalar_tensor_tensor(out=tabs[:, T_FIRST, 1:TILES], in0=expert[:, 1:TILES], scalar=float(E - 1),
                                              in1=first[:, 1:TILES], op0=ALU.is_lt, op1=ALU.mult))

            dve.wait_ge(zeroed, 2)
            steps(dve, body)
            make_table()

        @block.tensor
        def _(pe):
            for s in (t1_mm, prod_mm, pw_mm, a_mm, state_mm, out_mm, t2_mm, logit_mm, rank_mm):
                pe.sem_inc(s, CREDIT)

            def turn(src, ready):
                for b in range(B):
                    for k in range(KT):
                        last = pe.transpose(ps_xt[:, (b * KT + k) * P:(b * KT + k + 1) * P], src[:, b, k * P:(k + 1) * P],
                                            ident[:, :])
                last.then_inc(ready, 1)

            def project(dst, x, w, n, ready):
                for b in range(B):
                    for k in range(KT):
                        last = pe.matmul(dst[:, b, :], x[:, b, k, :], w[:, k, :], start=k == 0, stop=k == KT - 1)
                last.then_inc(ready, 1)

            def attend(c, par):
                pe.wait_ge(pw_turned_d, done(c))
                if exists(c - 3):
                    pe.wait_ge(rank_d, done(c - 3))
                for b in range(B):
                    last = pe.matmul(ps_a[:, b * P:(b + 1) * P], turned_pw[:, par, b, :], turned_pw[:, par, B + b, :],
                                     start=True, stop=True)
                last.then_inc(a_mm, 1)
                for b in range(B):
                    last = pe.matmul(ps_pw[0:NP, b * C:(b + 1) * C], prod[:, par, b, :], xn[:, par, b, :],
                                     start=True, stop=True)
                last.then_inc(state_mm, 1)

            def output(c, par):
                pe.wait_ge(attn_d, done(c))
                pe.wait_ge(tok_d, done(c - 1))
                pe.wait_ge(state_d, done(c - 1))
                for b in range(B):
                    dst = ps_out[:, b * C:(b + 1) * C]
                    pe.matmul(dst, attn[:, b, :], xn[:, par, b, :], start=True, stop=False)
                    last = pe.matmul(dst, turned_pw[:, par, B + b, :], state[:, par, b, :], start=False, stop=True)
                last.then_inc(out_mm, 1)

            def turn_products(c, par):
                pe.wait_ge(pw_d, done(c))
                pe.wait_ge(state_d, done(c - 1))
                for j, src in enumerate((prod[:, par], prod_w)):
                    for b in range(B):
                        at = (j * B + b) * P
                        last = pe.transpose(ps_pw[0:NP, at:at + P], src[:, b, :], ident[:, :])
                last.then_inc(pw_mm, 1)

            def rank_choices(c):
                pe.wait_ge(chose_d, done(c))
                pe.wait_ge(count_d, done(c - 1))
                if exists(c + 2):
                    pe.wait_ge(attn_d, done(c + 2))
                pe.matmul(ps_rank, fixed.before[:, :], chose[:, :, :].rearrange("p b e -> p (b e)"), start=True, stop=False)
                for d in range(1, B):
                    pe.matmul(ps_rank[:, d * E:B * E], fixed.ones[:, :], chose[:, 0:B - d, :].rearrange("p b e -> p (b e)"),
                              start=False, stop=False)
                for b in range(B):
                    last = pe.matmul(ps_rank[:, b * E:(b + 1) * E], fixed.ones[:, :], counts_m[:, :], start=False, stop=b == B - 1)
                last.then_inc(rank_mm, 1)

            def body(i, par):
                near, far = i + 1, i + 2
                if exists(far):
                    pe.wait_ge(norm1.done, done(far))
                    if exists(i - 1):
                        pe.wait_ge(xt2_d, done(i - 1))
                    turn(xn[:, par], t1_mm)
                if exists(near):
                    attend(near, 1 - par)
                if exists(i - 1):
                    rank_choices(i - 1)
                if exists(far):
                    pe.wait_ge(xt1_d, done(far))
                    if exists(i - 1):
                        pe.wait_ge(logit_d, done(i - 1))
                    project(ps_prod, xt1, fixed.proxy, NP, prod_mm)
                if exists(i):
                    pe.wait_ge(norm2.done, done(i))
                    if exists(far):
                        pe.wait_ge(xt1_d, done(far))
                    turn(x2, t2_mm)
                if exists(near):
                    output(near, 1 - par)
                if exists(i):
                    pe.wait_ge(xt2_d, done(i))
                    if exists(far):
                        pe.wait_ge(prel_d, done(far))
                    project(ps_logit, xt2, fixed.gate, E, logit_mm)
                if exists(far):
                    turn_products(far, par)

            steps(pe, body)
            pe.wait_ge(count_d, done(CH - 1))
            pe.wait_ge(logit_d, done(CH - 1))
            pe.matmul(ps_count, fixed.ones[:, :], counts_m[:, :], start=True, stop=True).then_inc(counted, 1)


T_EXPERT, T_PLACE, T_FIRST, T_NEXT, T_BUFFER, T_TOTAL = range(6)


def stage_c(nc, sem, wbuf, ident, tabs, bias1, bias2, wsplit, normed, places, out):
    with ExitStack() as ctx:
        def sb(name, shape, dt=F32):
            return ctx.enter_context(nc.sbuf_tensor(name, shape, dt))

        def ps(name, shape):
            return ctx.enter_context(nc.psum_tensor(name, shape, F32))

        SLOT = 4
        records = sb("records", [P, TILES, 2], I32)
        from_row, to_row = sb("from_row", [P, SLOT], I32), sb("to_row", [P, 2], I32)
        x = sb("x_rows", [P, SLOT, C])
        xth, xtl = sb("xth", [P, 2, KT, P], F32R), sb("xtl", [P, 2, KT, P], F32R)
        h = sb("h", [P, F])
        hb = sb("hb", [P, FT, P])
        g = sb("g", [P, FT, P])
        gh, gl = sb("gh", [P, 2, FT, P], F32R), sb("gl", [P, 2, FT, P], F32R)
        yb, y = sb("yb", [P, C]), sb("y", [P, 2, C])
        ps_x = ps("ps_x", [P, KT * P])
        ps_h = ps("ps_h", [P, F])
        ps_ht = ps("ps_ht", [P, F])
        ps_y = [ps(f"ps_y{i}", [P, HALF]) for i in range(2)]

        opening_records, first_records, record_in = sem("c_opening_records"), sem("c_first_records"), sem("c_record_in")
        w_in = [sem("c_w1_in"), sem("c_w2_in")]
        x_in = [sem(f"c_x_in{i}") for i in range(SLOT)]
        y_out, from_d, to_d = sem("c_y_out"), sem("c_from_row"), sem("c_to_row")
        xt_mm, h_mm, ht_mm, y_mm = sem("c_xt_mm"), sem("c_h_mm"), sem("c_ht_mm"), sem("c_y_mm")
        xh_d, h_d, g_d = sem("c_x_high"), sem("c_h"), sem("c_g")
        xl_d, hb_d, gh_d, gl_d, yb_d, y_d = (sem("c_" + n) for n in ("x_low", "hb", "g_high", "g_low", "yb", "y"))
        AHEAD, LEAD = 8, 5

        def steps(eng, body, lo, hi, end):
            u = lo
            if hi == USUAL:
                start = lo + SLOT
                loops = (hi - 1 - AHEAD - start) // SLOT
                for u in range(lo, start):
                    body(u, u % SLOT)
                with eng.Fori(0, loops) as k:
                    for i in range(SLOT):
                        body(k * SLOT + (start + i), (start + i) % SLOT)
                u = start + loops * SLOT
            for u in range(u, end + 1):
                body(u, u % SLOT)

        def within(u, lo, hi):
            return not isinstance(u, int) or lo <= u < hi

        def all_tiles(eng, run):
            run(0, USUAL)
            with eng.If(entry(eng, T_TOTAL, 0, TILES) > USUAL):
                run(USUAL, TILES)

        def later(u, step):
            return not isinstance(u, int) or u >= step

        def entry(eng, row, u, top):
            return eng.value_load(tabs[0:1, row, bass.ds(u, 1)], min_val=0, max_val=top)

        def before(u, slot):
            return u // SLOT if isinstance(u, int) else (u - slot) // SLOT

        block = ctx.enter_context(nc.Block())

        @block.sync
        def _(sp):
            def load_record(u, loaded):
                at = entry(sp, T_PLACE, u, SLOTS // P - 1)
                sp.dma_start(records[:, bass.ds(u, 1), :].rearrange("p a r -> p (a r)"),
                             places.rearrange("(t p) r -> t p r", p=P)[bass.ds(at, 1)].rearrange("a p r -> (a p) r")
                             ).then_inc(loaded, 16)

            def load_weights(part, expert, buffer, cond=None):
                at = slice(part * W2AT, (part + 1) * W2AT)
                sp.dma_start(wbuf[:, bass.ds(buffer, 1), at].rearrange("p a w -> p (a w)").bitcast(F32),
                             wsplit[bass.ds(expert, 1)].rearrange("a p w -> (a p) w")[:, at],
                             **({} if cond is None else {"cond": cond})).then_inc(w_in[part], 16)

            for u in range(AHEAD):
                load_record(u, opening_records if u < 2 else first_records)

            def run(lo, hi):
                def body(u, slot):
                    if lo == 0 and within(u + AHEAD, AHEAD, TILES):
                        if later(u, 1):
                            wait_apart(sp, record_in, u * 16)
                        load_record(u + AHEAD, record_in)
                    for part, used in enumerate((h_mm, y_mm)):
                        t = u - 2 * part
                        if within(t, max(lo - 1, 0), hi - 1):
                            first = entry(sp, T_FIRST, t, 1)
                            nxt = entry(sp, T_NEXT, t, E - 1)
                            buffer = entry(sp, T_BUFFER, t, 1)
                            wait_apart(sp, used, done(t - 1))
                            if later(t, 1):
                                wait_apart(sp, w_in[part], t * 16)
                            load_weights(part, nxt, 1 - buffer, cond=first)

                steps(sp, body, max(lo - 1, 0), hi, hi)
                for part in range(2):
                    sp.wait_ge(w_in[part], (hi - 1) * 16)
                if lo == 0:
                    sp.wait_ge(record_in, (TILES - AHEAD) * 16)

            all_tiles(sp, run)

        @block.gpsimd
        def _(pool):
            for s in (from_d, to_d):
                pool.sem_inc(s, CREDIT)

            def gather(u, slot):
                if later(u, SLOT):
                    wait_apart(pool, x_in[slot], before(u, slot) * 16)
                if later(u, AHEAD):
                    wait_apart(pool, record_in, (u - (AHEAD - 1)) * 16)
                pool.tensor_copy(from_row[:, slot:slot + 1], records[:, bass.ds(u, 1), 0]).then_inc(from_d, 1)
                if later(u, SLOT):
                    wait_apart(pool, xt_mm, done(u - SLOT))
                wait_apart(pool, from_d, done(u))
                pool.indirect_dma_start(out=x[:, slot, :], out_offset=None, in_=normed,
                                        in_offset=bass.IndirectOffsetOnAxis(ap=from_row[:, slot:slot + 1], axis=0)
                                        ).then_inc(x_in[slot], 16)

            def scatter(u, par):
                if later(u, 1):
                    wait_apart(pool, y_out, u * 16)
                pool.tensor_copy(to_row[:, par:par + 1], records[:, bass.ds(u, 1), 0]).then_inc(to_d, 1)
                wait_apart(pool, y_d, done(u))
                wait_apart(pool, to_d, done(u))
                pool.indirect_dma_start(out=out, out_offset=bass.IndirectOffsetOnAxis(ap=to_row[:, par:par + 1], axis=0),
                                        in_=y[:, par, :], in_offset=None, compute_op=ALU.add).then_inc(y_out, 16)

            def run(lo, hi):
                def body(u, slot):
                    if within(u + LEAD, lo, hi):
                        gather(u + LEAD, (slot + LEAD) % SLOT)
                    if within(u - 2, lo, hi):
                        scatter(u - 2, slot % 2)

                for u in range(lo, min(lo + LEAD, hi)):
                    if u == 2:
                        wait_apart(pool, first_records, (AHEAD - 2) * 16)
                    gather(u, u % SLOT)
                steps(pool, body, lo, hi, hi + 1)
                pool.wait_ge(y_out, hi * 16)

            pool.wait_ge(opening_records, 32)
            all_tiles(pool, run)

        @block.scalar
        def _(act):
            for s in (xh_d, h_d, g_d):
                act.sem_inc(s, CREDIT)

            def x_high(u, par):
                act.wait_ge(xt_mm, done(u))
                act.wait_ge(h_mm, done(u - 2))
                act.activation(xth[:, par], ps_x[:, :].rearrange("p (k t) -> p k t", k=KT), ACT.Copy).then_inc(xh_d, 1)

            def run(lo, hi):
                def body(u, slot):
                    par = slot % 2
                    if within(u, lo, hi):
                        act.wait_ge(h_mm, done(u))
                        act.wait_ge(ht_mm, done(u - 1))
                        act.activation(h[:, :], ps_h[:, :], ACT.Copy).then_inc(h_d, 1)
                    if within(u + 2, lo, hi):
                        x_high(u + 2, par)
                    if within(u, lo, hi):
                        act.wait_ge(hb_d, done(u))
                        act.wait_ge(gl_d, done(u - 1))
                        act.activation(g[:, :, :], hb[:, :, :], ACT.Gelu_apprx_tanh).then_inc(g_d, 1)

                x_high(lo, lo % 2)
                x_high(lo + 1, (lo + 1) % 2)
                steps(act, body, lo, hi, hi - 1)

            all_tiles(act, run)

        @block.vector
        def _(dve):
            for s in (xl_d, hb_d, gh_d, gl_d, yb_d, y_d):
                dve.sem_inc(s, CREDIT)

            def x_low(u, par):
                dve.wait_ge(xh_d, done(u))
                dve.tensor_tensor(xtl[:, par], ps_x[:, :].rearrange("p (k t) -> p k t", k=KT), xth[:, par].bitcast(F32),
                                  ALU.subtract).then_inc(xl_d, 1)

            def result(u, par):
                e = entry(dve, T_EXPERT, u, E - 1)
                dve.wait_ge(y_mm, done(u))
                dve.wait_ge(y_d, done(u - 1))
                dve.tensor_tensor(yb[:, :], ps_y[par][:, 0:C], bias2[:, bass.ds(e, 1), :].rearrange("p a c -> p (a c)"),
                                  ALU.add).then_inc(yb_d, 1)
                if later(u, 2):
                    dve.wait_ge(y_out, (u - 1) * 16)
                dve.wait_ge(yb_d, done(u))
                share = records[:, bass.ds(u, 1), 1].bitcast(F32)
                dve.tensor_scalar(y[:, par, :], yb[:, :], share, None, ALU.mult).then_inc(y_d, 1)

            def run(lo, hi):
                def body(u, slot):
                    par = slot % 2
                    if within(u - 2, lo, hi):
                        result(u - 2, par)
                    if within(u, lo, hi):
                        e = entry(dve, T_EXPERT, u, E - 1)
                        dve.wait_ge(ht_mm, done(u))
                        dve.wait_ge(g_d, done(u - 1))
                        bias = bias1[:, bass.ds(e, 1), :].rearrange("p a f -> p (a f)").unsqueeze(2).to_broadcast([P, FT, P])
                        dve.tensor_tensor(hb[:, :, :], ps_ht[:, :].rearrange("p (f t) -> p f t", f=FT), bias,
                                          ALU.add).then_inc(hb_d, 1)
                    if within(u + 2, lo, hi):
                        x_low(u + 2, par)
                    if within(u, lo, hi):
                        dve.wait_ge(g_d, done(u))
                        dve.wait_ge(y_mm, done(u - 2))
                        dve.tensor_copy(gh[:, par], g[:, :, :]).then_inc(gh_d, 1)
                        dve.wait_ge(gh_d, done(u))
                        dve.tensor_tensor(gl[:, par], g[:, :, :], gh[:, par].bitcast(F32), ALU.subtract).then_inc(gl_d, 1)

                x_low(lo, lo % 2)
                x_low(lo + 1, (lo + 1) % 2)
                if lo == 0:
                    dve.wait_ge(opening_records, 32)
                    dve.wait_ge(first_records, (AHEAD - 2) * 16)
                steps(dve, body, lo, hi, hi + 1)

            all_tiles(dve, run)

        @block.tensor
        def _(pe):
            for s in (xt_mm, h_mm, ht_mm, y_mm):
                pe.sem_inc(s, CREDIT)

            def turn_x(u, slot):
                pe.wait_ge(x_in[slot], (before(u, slot) + 1) * 16)
                pe.wait_ge(xl_d, done(u - 1))
                for k in range(KT):
                    last = pe.transpose(ps_x[:, k * P:(k + 1) * P], x[:, slot, k * P:(k + 1) * P], ident[:, :])
                last.then_inc(xt_mm, 1)

            def weights(u, part):
                buffer = entry(pe, T_BUFFER, u, 1)
                both = wbuf[:, bass.ds(buffer, 1), part * W2AT:(part + 1) * W2AT].rearrange("p a w -> p (a w)")
                rows = (KT, FT)[part]
                return [both[:, i * W2AT // 2:(i + 1) * W2AT // 2].rearrange("p (k n) -> p k n", k=rows) for i in range(2)]

            def layer1(u, par):
                wh, wl = weights(u, 0)
                if later(u, 1):
                    pe.wait_ge(w_in[0], u * 16)
                pe.wait_ge(xl_d, done(u))
                pe.wait_ge(h_d, done(u - 1))
                for n in range(F // HALF):
                    cols = slice(n * HALF, (n + 1) * HALF)
                    for k in range(KT):
                        last = mm3(pe, ps_h[:, cols], (xth[:, par, k], xtl[:, par, k]), (wh[:, k, cols], wl[:, k, cols]),
                                   k == 0, k == KT - 1)
                last.then_inc(h_mm, 1)

            def turn_h(u):
                pe.wait_ge(h_d, done(u))
                pe.wait_ge(hb_d, done(u - 1))
                for f in range(FT):
                    last = pe.transpose(ps_ht[:, f * P:(f + 1) * P], h[:, f * P:(f + 1) * P], ident[:, :])
                last.then_inc(ht_mm, 1)

            def layer2(u, par):
                wh, wl = weights(u, 1)
                if later(u, 1):
                    pe.wait_ge(w_in[1], u * 16)
                pe.wait_ge(gl_d, done(u))
                pe.wait_ge(yb_d, done(u - 2))
                for f in range(FT):
                    last = mm3(pe, ps_y[par][:, 0:C], (gh[:, par, f], gl[:, par, f]), (wh[:, f], wl[:, f]),
                               f == 0, f == FT - 1)
                last.then_inc(y_mm, 1)

            def run(lo, hi):
                def body(u, slot):
                    par = slot % 2
                    if within(u, lo, hi):
                        layer1(u, par)
                    if within(u - 2, lo, hi):
                        layer2(u - 2, par)
                    if within(u, lo, hi):
                        turn_h(u)
                    if within(u + 2, lo, hi):
                        turn_x(u + 2, (slot + 2) % SLOT)

                turn_x(lo, lo % SLOT)
                turn_x(lo + 1, (lo + 1) % SLOT)
                steps(pe, body, lo, hi, hi + 1)

            all_tiles(pe, run)


INPUTS = ["x_ch", "x_tok", "wqk3", "bqk3", "wv_t", "bv", "alpha", "proxy_t", "gate_t", "w1", "b1_t", "w2", "b2"]


def kernel(x, L0_conv_Wq, L0_conv_bq, L0_conv_Wk, L0_conv_bk, L0_conv_Wv, L0_conv_bv, L0_conv_alpha,
           L1_attn_proxy, L1_ffn_gate_w, L1_ffn_w1, L1_ffn_b1, L1_ffn_w2, L1_ffn_b2):
    import numpy as np
    import concourse.bacc as bacc
    from concourse.bass_utils import run_bass_kernel_spmd

    flat = np.asarray(x).reshape(B, C, N)
    wq, wk, wv = (np.asarray(w) for w in (L0_conv_Wq, L0_conv_Wk, L0_conv_Wv))
    laid = {
        "x_ch": flat,
        "x_tok": flat.transpose(0, 2, 1).reshape(TOK, C),
        "wqk3": np.stack([np.tile(wq.T, (1, 3)), np.tile(wk.T, (1, 3))]),
        "bqk3": np.stack([np.tile(np.asarray(L0_conv_bq), 3), np.tile(np.asarray(L0_conv_bk), 3)], axis=1),
        "wv_t": wv.T,
        "bv": L0_conv_bv,
        "alpha": L0_conv_alpha,
        "proxy_t": np.asarray(L1_attn_proxy).T,
        "gate_t": np.asarray(L1_ffn_gate_w).T,
        "w1": L1_ffn_w1,
        "b1_t": np.asarray(L1_ffn_b1).reshape(E, FT, P).transpose(2, 0, 1),
        "w2": L1_ffn_w2,
        "b2": L1_ffn_b2,
    }
    nc = bacc.Bacc("TRN2", target_bir_lowering=False, num_devices=1)
    arrays, args = {}, []
    for name in INPUTS:
        a = np.ascontiguousarray(laid[name])
        arrays[f"in_{name}"] = a
        args.append(nc.dram_tensor(f"in_{name}", a.shape, mybir.dt.from_np(a.dtype), kind="ExternalInput").ap())
    out = nc.dram_tensor("out_tok", (TOK + P, C), F32, kind="ExternalOutput").ap()
    build(nc, *args, out)
    got = run_bass_kernel_spmd(nc, [arrays], core_ids=[0]).results[0]["out_tok"]
    return np.ascontiguousarray(np.asarray(got)[:TOK].reshape(B, N, C).transpose(0, 2, 1)).reshape(x.shape)
```
